# Optimizing a Trainium2 kernel written in Bass

```python
import numpy as np
import jax
import jax.numpy as jnp

def _softmax(x, axis=-1):
    return jax.nn.softmax(x, axis=axis)

def _gelu(x):
    return jax.nn.gelu(x, approximate=True)

def _silu(x):
    return jax.nn.silu(x)

def _sigmoid(x):
    return jax.nn.sigmoid(x)

def _layernorm(x, axis=-1, eps=1e-05):
    m = jnp.mean(x, axis=axis, keepdims=True)
    v = jnp.var(x, axis=axis, keepdims=True)
    return (x - m) / jnp.sqrt(v + eps)

def _scatter_add(tgt, idx, src, axis=0):
    return tgt.at[idx].add(src)

def _segment_sum(src, seg, n):
    return jax.ops.segment_sum(src, seg, n)
kernel_name = 'mk_decoder_postln_d2_seqx_r8_db1f20'

def setup_inputs(seed: int=0):
    np.random.seed(seed)
    _w = jnp.asarray

    def _rec_inputs():
        import jax
        import jax.numpy as jnp
        _rk = jax.random.key(seed)
        x = 2.818e-05 + 1 * jax.random.normal(jax.random.fold_in(_rk, 1), (64, 64, 128), jnp.float32)
        _lenS = 64 - jax.random.randint(jax.random.fold_in(_rk, 7), (64,), 0, max(1, 64 // 4) + 1, jnp.int32)
        _lenS2 = 64 - jax.random.randint(jax.random.fold_in(_rk, 8), (64,), 0, max(1, 64 // 4) + 1, jnp.int32)
        _ctx_2048P = jax.random.normal(jax.random.fold_in(_rk, 11), (64, 16, 256), jnp.float32)
        _ctx_2048c = jax.random.dirichlet(jax.random.fold_in(_rk, 511), 0.3 * jnp.ones((16,), jnp.float32), (64, 64))
        _ctx_2048t = jnp.einsum('bsk,bkd->bsd', _ctx_2048c, _ctx_2048P)
        _ctx_2048t = _ctx_2048t * jax.lax.rsqrt(jnp.mean(jnp.square(_ctx_2048t)) + 1e-12) * 0.953939
        ctx_2048 = -0.000125008 + 0.999885 * (_ctx_2048t + 0.3 * jax.random.normal(jax.random.fold_in(_rk, 611), (64, 64, 256), jnp.float32))
        _validS = jnp.arange(64)[None, :] < _lenS[:, None]
        _validS2 = jnp.arange(64)[None, :] < _lenS2[:, None]
        _causal = jnp.tril(jnp.ones((64, 64), dtype=bool))
        mask_BxS2_fk1 = jnp.where(jnp.broadcast_to(_validS2[:, :], (64, 64)), 1.0, 0.0).astype(jnp.float32)
        return (x, ctx_2048, mask_BxS2_fk1)
    x, ctx_2048, mask_BxS2_fk1 = _rec_inputs()

    def _L0_attn_setup():
        import math
        import jax, jax.numpy as jnp
        import numpy as np
        B, L, DIM, HEADS = (4, 256, 128, 8)
        HEAD = DIM // HEADS
        SCALE_BASE = 512.0
        EPS = 1e-05

        def _xpos(x, downscale=False):
            l, dh = (x.shape[-2], x.shape[-1])
            half = dh // 2
            pos = jnp.arange(l, dtype=x.dtype)
            base = (jnp.arange(0, dh, 2, dtype=x.dtype) + 0.4 * dh) / (1.4 * dh)
            scale = base[None, :] ** (pos[:, None] / SCALE_BASE)
            inv_freq = 1.0 / 10000.0 ** (jnp.arange(half, dtype=x.dtype) / half)
            sinusoid = pos[:, None] * inv_freq[None, :]
            sin, cos = (jnp.sin(sinusoid), jnp.cos(sinusoid))
            if downscale:
                scale = 1.0 / scale
            s = jnp.repeat(sin * scale, 2, axis=-1)
            c = jnp.repeat(cos * scale, 2, axis=-1)
            x1, x2 = (x[..., ::2], x[..., 1::2])
            rot = jnp.stack([-x2, x1], axis=-1).reshape(x.shape)
            return x * c + rot * s

        def _decay_mask(l, gammas):
            n = jnp.arange(l)[:, None]
            m = jnp.arange(l)[None, :]
            lg = jnp.log(gammas)
            expo = (n - m).astype(jnp.float32)[None, :, :] * lg[:, None, None]
            return jnp.where((n >= m)[None], jnp.exp(expo), 0.0)
        key = jax.random.key(seed)
        ks = jax.random.split(key, 6)
        d = DIM
        return {'X': jax.random.normal(ks[0], (B, L, DIM), dtype=jnp.float32), 'W_Q': jax.random.normal(ks[1], (HEADS, DIM, HEAD), dtype=jnp.float32) / d, 'W_K': jax.random.normal(ks[2], (HEADS, DIM, HEAD), dtype=jnp.float32) / d, 'W_V': jax.random.normal(ks[3], (HEADS, DIM, HEAD), dtype=jnp.float32) / d, 'W_G': jax.random.normal(ks[4], (DIM, DIM), dtype=jnp.float32) / d, 'W_O': jax.random.normal(ks[5], (DIM, DIM), dtype=jnp.float32) / d, 'gn_weight': jnp.ones((DIM,), dtype=jnp.float32), 'gn_bias': jnp.zeros((DIM,), dtype=jnp.float32)}
    _L0_attn_all = _L0_attn_setup()
    _L0_attn_in = {k: v for k, v in _L0_attn_all.items() if k in ('W_Q', 'W_K', 'W_V', 'W_G', 'W_O', 'gn_weight', 'gn_bias')}
    del _L0_attn_all

    def _L0_xattn_setup():
        import jax, jax.numpy as jnp
        import numpy as np
        B, S, T = (32, 64, 64)
        SRC_SIZE, TGT_SIZE, OUT_SIZE, NUM_HEAD = (256, 128, 128, 8)
        HEAD_DIM = OUT_SIZE // NUM_HEAD
        key = jax.random.key(seed)
        ks = jax.random.split(key, 12)
        src = jax.random.normal(ks[0], (B, S, SRC_SIZE), dtype=jnp.float32)
        tgt = jax.random.normal(ks[1], (B, T, TGT_SIZE), dtype=jnp.float32)
        src_mask = (jax.random.uniform(ks[2], (B, S)) > 0.3).astype(jnp.float32)
        src_mask = src_mask.at[:, 0].set(1.0)
        tgt_mask = (jax.random.uniform(ks[3], (B, T)) > 0.3).astype(jnp.float32)
        tgt_mask = tgt_mask.at[:, 0].set(1.0)

        def lin(k, out_f, in_f):
            return jax.random.normal(k, (out_f, in_f), dtype=jnp.float32) / np.sqrt(in_f)
        W_src = lin(ks[4], 2 * OUT_SIZE, SRC_SIZE)
        b_src = jnp.zeros((2 * OUT_SIZE,), jnp.float32)
        W_tgt = lin(ks[5], OUT_SIZE, TGT_SIZE)
        b_tgt = jnp.zeros((OUT_SIZE,), jnp.float32)
        W_out = lin(ks[6], OUT_SIZE, OUT_SIZE + TGT_SIZE)
        b_out = jnp.zeros((OUT_SIZE,), jnp.float32)
        return {'src': src, 'tgt': tgt, 'src_mask': src_mask, 'tgt_mask': tgt_mask, 'W_src': W_src, 'b_src': b_src, 'W_tgt': W_tgt, 'b_tgt': b_tgt, 'W_out': W_out, 'b_out': b_out}
    _L0_xattn_all = _L0_xattn_setup()
    _L0_xattn_in = {k: v for k, v in _L0_xattn_all.items() if k in ('W_src', 'b_src', 'W_tgt', 'b_tgt', 'W_out', 'b_out')}
    del _L0_xattn_all

    def _L0_ffn_setup():
        import jax, jax.numpy as jnp
        import numpy as np
        E = 8
        K = 2
        S = 1
        THRESHOLD = 0.7
        NORM_TOPK = True
        H = 128
        F = 128
        B, SEQ = (2, 128)
        key = jax.random.key(seed)
        k1, k2, k3, k4, k5 = jax.random.split(key, 5)
        hidden_states = jax.random.normal(k1, (B, SEQ, H), jnp.float32)
        gate_weight = jax.random.normal(k2, (E, H), jnp.float32) * 0.02
        gate_up_proj = jax.random.normal(k3, (E, 2 * F, H), jnp.float32) * 0.02
        down_proj = jax.random.normal(k4, (E, H, F), jnp.float32) * 0.02
        sim = jax.random.uniform(k5, (E, E), jnp.float32)
        sim = (sim + sim.T) / 2.0
        sim = sim.at[jnp.arange(E), jnp.arange(E)].set(1.0)
        return {'hidden_states': hidden_states, 'gate_weight': gate_weight, 'gate_up_proj': gate_up_proj, 'down_proj': down_proj, 'similarity_matrix': sim}
    _L0_ffn_all = _L0_ffn_setup()
    _L0_ffn_in = {k: v for k, v in _L0_ffn_all.items() if k in ('gate_weight', 'gate_up_proj', 'down_proj', 'similarity_matrix')}
    del _L0_ffn_all

    def _L1_attn_setup():
        import jax, jax.numpy as jnp
        import numpy as np
        N_HEAD = 16
        Q_DIM = 64
        V_DIM = 64
        WINDOW = 129
        DIL = 1
        key = jax.random.key(seed)
        ks = jax.random.split(key, 9)
        B, N, E = (1, 256, 128)
        s = 0.02
        return {'x': jax.random.normal(ks[0], (B, N, E), jnp.float32), 'Wq': jax.random.normal(ks[1], (E, N_HEAD * Q_DIM), jnp.float32) * s, 'bq': jax.random.normal(ks[2], (N_HEAD * Q_DIM,), jnp.float32) * s, 'Wk': jax.random.normal(ks[3], (E, N_HEAD * Q_DIM), jnp.float32) * s, 'bk': jax.random.normal(ks[4], (N_HEAD * Q_DIM,), jnp.float32) * s, 'Wv': jax.random.normal(ks[5], (E, N_HEAD * V_DIM), jnp.float32) * s, 'bv': jax.random.normal(ks[6], (N_HEAD * V_DIM,), jnp.float32) * s, 'Wo': jax.random.normal(ks[7], (N_HEAD * V_DIM, E), jnp.float32) * s, 'bo': jax.random.normal(ks[8], (E,), jnp.float32) * s}
    _L1_attn_all = _L1_attn_setup()
    _L1_attn_in = {k: v for k, v in _L1_attn_all.items() if k in ('Wq', 'bq', 'Wk', 'bk', 'Wv', 'bv', 'Wo', 'bo')}
    del _L1_attn_all

    def _L1_xattn_setup():
        import jax, jax.numpy as jnp
        import numpy as np
        NUM_HEADS = 16
        key = jax.random.key(seed)
        ks = jax.random.split(key, 5)
        dim = 128
        B, N, N_c = (4, 128, 32)
        x = jax.random.normal(ks[0], (B, N, dim), dtype=jnp.float32)
        context = jax.random.normal(ks[1], (B, N_c, 2 * dim), dtype=jnp.float32)
        w_qkv = jax.random.normal(ks[2], (3 * dim, dim), dtype=jnp.float32) * 0.02
        w_proj = jax.random.normal(ks[3], (dim, dim), dtype=jnp.float32) * 0.02
        b_proj = jax.random.normal(ks[4], (dim,), dtype=jnp.float32) * 0.02
        return {'x': x, 'context': context, 'w_qkv': w_qkv, 'w_proj': w_proj, 'b_proj': b_proj}
    _L1_xattn_all = _L1_xattn_setup()
    _L1_xattn_in = {k: v for k, v in _L1_xattn_all.items() if k in ('w_qkv', 'w_proj', 'b_proj')}
    del _L1_xattn_all

    def _L1_ffn_setup():
        import jax, jax.numpy as jnp
        import numpy as np
        from math import sqrt
        B, S, D, H, E, K, FF = (2, 128, 128, 16, 8, 2, 512)
        HD = D // H
        EPS = 1e-05

        def _rope_cache(seq_len, hd):
            inv_freq = 1.0 / 10000.0 ** (jnp.arange(0, hd, 2, dtype=jnp.float32) / hd)
            t = jnp.arange(seq_len, dtype=jnp.float32)
            freqs = t[:, None] * inv_freq[None, :]
            emb = jnp.concatenate([freqs, freqs], axis=-1)
            return (jnp.cos(emb), jnp.sin(emb))

        def _rotate_half(x):
            x1, x2 = jnp.split(x, 2, axis=-1)
            return jnp.concatenate([-x2, x1], axis=-1)

        def _layernorm(x, g, b):
            m = jnp.mean(x, axis=-1, keepdims=True)
            v = jnp.var(x, axis=-1, keepdims=True)
            return (x - m) * jax.lax.rsqrt(v + EPS) * g + b

        def _forward(x, Wq, bq, Wk, bk, Wv, bv, Wo, bo, Wg, bg, W1, b1, W2, b2, g1, be1, g2, be2):
            bsz, seq, d = x.shape
            q = (x @ Wq + bq).reshape(bsz, seq, H, HD).transpose(0, 2, 1, 3)
            k = (x @ Wk + bk).reshape(bsz, seq, H, HD).transpose(0, 2, 1, 3)
            v = (x @ Wv + bv).reshape(bsz, seq, H, HD).transpose(0, 2, 1, 3)
            cos, sin = _rope_cache(seq, HD)
            cos = cos[None, None]
            sin = sin[None, None]
            q = q * cos + _rotate_half(q) * sin
            k = k * cos + _rotate_half(k) * sin
            scores = jnp.einsum('bhqd,bhkd->bhqk', q, k) / sqrt(HD)
            attn = jax.nn.softmax(scores, axis=-1)
            ao = jnp.einsum('bhqk,bhkd->bhqd', attn, v)
            ao = ao.transpose(0, 2, 1, 3).reshape(bsz, seq, d)
            attn_out = ao @ Wo + bo
            x1 = _layernorm(x + attn_out, g1, be1)
            gate_logits = x1 @ Wg + bg
            gate_probs = jax.nn.softmax(gate_logits, axis=-1)
            topk_p, topk_i = jax.lax.top_k(gate_probs, K)
            topk_p = topk_p / jnp.sum(topk_p, axis=-1, keepdims=True)
            comb = jnp.sum(jax.nn.one_hot(topk_i, E, dtype=x.dtype) * topk_p[..., None], axis=-2)
            h = jax.nn.gelu(jnp.einsum('bsd,edf->bsef', x1, W1) + b1, approximate=False)
            y = jnp.einsum('bsef,efd->bsed', h, W2) + b2
            moe_out = jnp.einsum('bse,bsed->bsd', comb, y)
            return _layernorm(x1 + moe_out, g2, be2)
        key = jax.random.key(seed)
        ks = jax.random.split(key, 20)
        std = 0.02
        p = lambda k, sh: jax.random.normal(k, sh, dtype=jnp.float32) * std
        return {'x': jax.random.normal(ks[0], (B, S, D), dtype=jnp.float32), 'Wq': p(ks[1], (D, D)), 'bq': jnp.zeros((D,), jnp.float32), 'Wk': p(ks[2], (D, D)), 'bk': jnp.zeros((D,), jnp.float32), 'Wv': p(ks[3], (D, D)), 'bv': jnp.zeros((D,), jnp.float32), 'Wo': p(ks[4], (D, D)), 'bo': jnp.zeros((D,), jnp.float32), 'Wg': p(ks[5], (D, E)), 'bg': jnp.zeros((E,), jnp.float32), 'W1': p(ks[6], (E, D, FF)), 'b1': jnp.zeros((E, FF), jnp.float32), 'W2': p(ks[7], (E, FF, D)), 'b2': jnp.zeros((E, D), jnp.float32), 'g1': jnp.ones((D,), jnp.float32), 'be1': jnp.zeros((D,), jnp.float32), 'g2': jnp.ones((D,), jnp.float32), 'be2': jnp.zeros((D,), jnp.float32)}
    _L1_ffn_all = _L1_ffn_setup()
    _L1_ffn_in = {k: v for k, v in _L1_ffn_all.items() if k in ('Wq', 'bq', 'Wk', 'bk', 'Wv', 'bv', 'Wo', 'bo', 'Wg', 'bg', 'W1', 'b1', 'W2', 'b2', 'g1', 'be1', 'g2', 'be2')}
    del _L1_ffn_all
    return {'x': x, 'ctx_2048': ctx_2048, 'mask_BxS2_fk1': mask_BxS2_fk1, 'L0_attn_W_Q': _L0_attn_in['W_Q'], 'L0_attn_W_K': _L0_attn_in['W_K'], 'L0_attn_W_V': _L0_attn_in['W_V'], 'L0_attn_W_G': _L0_attn_in['W_G'], 'L0_attn_W_O': _L0_attn_in['W_O'], 'L0_attn_gn_weight': _L0_attn_in['gn_weight'], 'L0_attn_gn_bias': _L0_attn_in['gn_bias'], 'L0_xattn_W_src': _L0_xattn_in['W_src'], 'L0_xattn_b_src': _L0_xattn_in['b_src'], 'L0_xattn_W_tgt': _L0_xattn_in['W_tgt'], 'L0_xattn_b_tgt': _L0_xattn_in['b_tgt'], 'L0_xattn_W_out': _L0_xattn_in['W_out'], 'L0_xattn_b_out': _L0_xattn_in['b_out'], 'L0_ffn_gate_weight': _L0_ffn_in['gate_weight'], 'L0_ffn_gate_up_proj': _L0_ffn_in['gate_up_proj'], 'L0_ffn_down_proj': _L0_ffn_in['down_proj'], 'L0_ffn_similarity_matrix': _L0_ffn_in['similarity_matrix'], 'L1_attn_Wq': _L1_attn_in['Wq'], 'L1_attn_bq': _L1_attn_in['bq'], 'L1_attn_Wk': _L1_attn_in['Wk'], 'L1_attn_bk': _L1_attn_in['bk'], 'L1_attn_Wv': _L1_attn_in['Wv'], 'L1_attn_bv': _L1_attn_in['bv'], 'L1_attn_Wo': _L1_attn_in['Wo'], 'L1_attn_bo': _L1_attn_in['bo'], 'L1_xattn_w_qkv': _L1_xattn_in['w_qkv'], 'L1_xattn_w_proj': _L1_xattn_in['w_proj'], 'L1_xattn_b_proj': _L1_xattn_in['b_proj'], 'L1_ffn_Wq': _L1_ffn_in['Wq'], 'L1_ffn_bq': _L1_ffn_in['bq'], 'L1_ffn_Wk': _L1_ffn_in['Wk'], 'L1_ffn_bk': _L1_ffn_in['bk'], 'L1_ffn_Wv': _L1_ffn_in['Wv'], 'L1_ffn_bv': _L1_ffn_in['bv'], 'L1_ffn_Wo': _L1_ffn_in['Wo'], 'L1_ffn_bo': _L1_ffn_in['bo'], 'L1_ffn_Wg': _L1_ffn_in['Wg'], 'L1_ffn_bg': _L1_ffn_in['bg'], 'L1_ffn_W1': _L1_ffn_in['W1'], 'L1_ffn_b1': _L1_ffn_in['b1'], 'L1_ffn_W2': _L1_ffn_in['W2'], 'L1_ffn_b2': _L1_ffn_in['b2'], 'L1_ffn_g1': _L1_ffn_in['g1'], 'L1_ffn_be1': _L1_ffn_in['be1'], 'L1_ffn_g2': _L1_ffn_in['g2'], 'L1_ffn_be2': _L1_ffn_in['be2']}

def reference(x, ctx_2048, mask_BxS2_fk1, L0_attn_W_Q, L0_attn_W_K, L0_attn_W_V, L0_attn_W_G, L0_attn_W_O, L0_attn_gn_weight, L0_attn_gn_bias, L0_xattn_W_src, L0_xattn_b_src, L0_xattn_W_tgt, L0_xattn_b_tgt, L0_xattn_W_out, L0_xattn_b_out, L0_ffn_gate_weight, L0_ffn_gate_up_proj, L0_ffn_down_proj, L0_ffn_similarity_matrix, L1_attn_Wq, L1_attn_bq, L1_attn_Wk, L1_attn_bk, L1_attn_Wv, L1_attn_bv, L1_attn_Wo, L1_attn_bo, L1_xattn_w_qkv, L1_xattn_w_proj, L1_xattn_b_proj, L1_ffn_Wq, L1_ffn_bq, L1_ffn_Wk, L1_ffn_bk, L1_ffn_Wv, L1_ffn_bv, L1_ffn_Wo, L1_ffn_bo, L1_ffn_Wg, L1_ffn_bg, L1_ffn_W1, L1_ffn_b1, L1_ffn_W2, L1_ffn_b2, L1_ffn_g1, L1_ffn_be1, L1_ffn_g2, L1_ffn_be2):
    import jax
    import jax.numpy as jnp

    def _L0_attn_ref(X, W_Q, W_K, W_V, W_G, W_O, gn_weight, gn_bias):
        import math
        import jax, jax.numpy as jnp
        import numpy as np
        B, L, DIM, HEADS = (4, 256, 128, 8)
        HEAD = DIM // HEADS
        SCALE_BASE = 512.0
        EPS = 1e-05

        def _xpos(x, downscale=False):
            l, dh = (x.shape[-2], x.shape[-1])
            half = dh // 2
            pos = jnp.arange(l, dtype=x.dtype)
            base = (jnp.arange(0, dh, 2, dtype=x.dtype) + 0.4 * dh) / (1.4 * dh)
            scale = base[None, :] ** (pos[:, None] / SCALE_BASE)
            inv_freq = 1.0 / 10000.0 ** (jnp.arange(half, dtype=x.dtype) / half)
            sinusoid = pos[:, None] * inv_freq[None, :]
            sin, cos = (jnp.sin(sinusoid), jnp.cos(sinusoid))
            if downscale:
                scale = 1.0 / scale
            s = jnp.repeat(sin * scale, 2, axis=-1)
            c = jnp.repeat(cos * scale, 2, axis=-1)
            x1, x2 = (x[..., ::2], x[..., 1::2])
            rot = jnp.stack([-x2, x1], axis=-1).reshape(x.shape)
            return x * c + rot * s

        def _decay_mask(l, gammas):
            n = jnp.arange(l)[:, None]
            m = jnp.arange(l)[None, :]
            lg = jnp.log(gammas)
            expo = (n - m).astype(jnp.float32)[None, :, :] * lg[:, None, None]
            return jnp.where((n >= m)[None], jnp.exp(expo), 0.0)
        b, l, d = X.shape
        h = W_Q.shape[0]
        gammas = 1.0 - jnp.exp(jnp.linspace(math.log(1.0 / 32.0), math.log(1.0 / 512.0), h)).astype(jnp.float32)
        Q = jnp.einsum('bld,hde->bhle', X, W_Q)
        K = jnp.einsum('bld,hde->bhle', X, W_K)
        V = jnp.einsum('bld,hdv->bhlv', X, W_V)
        Q = _xpos(Q)
        K = _xpos(K, downscale=True)
        D = _decay_mask(l, gammas).astype(X.dtype)
        scores = jnp.einsum('bhle,bhme->bhlm', Q, K) * D[None]
        Y = jnp.einsum('bhlm,bhmv->bhlv', scores, V)
        mean = Y.mean(axis=-1, keepdims=True)
        var = Y.var(axis=-1, keepdims=True)
        Yn = (Y - mean) * jax.lax.rsqrt(var + EPS)
        Yn = jnp.transpose(Yn, (0, 2, 1, 3)).reshape(b, l, -1)
        Yn = Yn * gn_weight + gn_bias
        G = X @ W_G
        out = G * jax.nn.sigmoid(G) * Yn @ W_O
        return out

    def _L0_xattn_ref(src, tgt, src_mask, tgt_mask, W_src, b_src, W_tgt, b_tgt, W_out, b_out):
        import jax, jax.numpy as jnp
        import numpy as np
        B, S, T = (32, 64, 64)
        SRC_SIZE, TGT_SIZE, OUT_SIZE, NUM_HEAD = (256, 128, 128, 8)
        HEAD_DIM = OUT_SIZE // NUM_HEAD
        b, s, _ = src.shape
        t = tgt.shape[1]
        src_trans = jnp.einsum('bsf,of->bso', src, W_src) + b_src
        tgt_trans = jnp.einsum('btf,of->bto', tgt, W_tgt) + b_tgt
        src_trans = src_trans * src_mask[:, :, None]
        tgt_trans = tgt_trans * tgt_mask[:, :, None]
        src_key, src_val = jnp.split(src_trans, 2, axis=2)
        k = src_key.reshape(b, s, NUM_HEAD, HEAD_DIM)
        v = src_val.reshape(b, s, NUM_HEAD, HEAD_DIM)
        q = tgt_trans.reshape(b, t, NUM_HEAD, HEAD_DIM)
        scores = jnp.einsum('bthd,bshd->bhts', q, k) / np.sqrt(HEAD_DIM)
        scores = jnp.where(src_mask[:, None, None, :] == 0, -jnp.inf, scores)
        attn = jax.nn.softmax(scores, axis=-1)
        tgt_update = jnp.einsum('bhts,bshd->bthd', attn, v).reshape(b, t, OUT_SIZE)
        cat_tgt = jnp.concatenate([tgt, tgt_update], axis=2)
        return jnp.einsum('btf,of->bto', cat_tgt, W_out) + b_out

    def _L0_ffn_ref(hidden_states, gate_weight, gate_up_proj, down_proj, similarity_matrix):
        import jax, jax.numpy as jnp
        import numpy as np
        E = 8
        K = 2
        S = 1
        THRESHOLD = 0.7
        NORM_TOPK = True
        H = 128
        F = 128
        B, SEQ = (2, 128)
        b, s, h = hidden_states.shape
        x = hidden_states.reshape(-1, h)
        N = x.shape[0]
        logits = x @ gate_weight.T
        probs = jax.nn.softmax(logits.astype(jnp.float32), axis=-1)
        top_w, top_i = jax.lax.top_k(probs, K)
        if NORM_TOPK:
            top_w = top_w / jnp.clip(jnp.sum(top_w, -1, keepdims=True), 1e-12)
        primary_mask = jnp.zeros((E,), bool).at[top_i[:, :S].reshape(-1)].set(True)
        sim = jnp.where(primary_mask[None, :], similarity_matrix.astype(jnp.float32), -jnp.inf)
        best_j = jnp.argmax(sim, axis=-1)
        best_sim = jnp.max(sim, axis=-1)
        ids = jnp.arange(E)
        expert_map = jnp.where(~primary_mask & (best_sim >= THRESHOLD), best_j, ids)
        rerouted = expert_map[top_i]
        rows = jnp.arange(N)[:, None]
        dense = jnp.zeros((N, E), top_w.dtype).at[rows, rerouted].add(top_w)
        fw, fi = jax.lax.top_k(dense, K)
        combine = jnp.zeros((N, E), fw.dtype).at[rows, fi].add(jnp.where(fw > 0, fw, 0.0))
        gu = jnp.einsum('nh,efh->enf', x, gate_up_proj)
        g, u = jnp.split(gu, 2, axis=-1)
        hmid = jax.nn.silu(g) * u
        y = jnp.einsum('enf,ehf->enh', hmid, down_proj)
        out = jnp.einsum('ne,enh->nh', combine, y)
        return out.reshape(b, s, h)

    def _L1_attn_ref(x, Wq, bq, Wk, bk, Wv, bv, Wo, bo):
        import jax, jax.numpy as jnp
        import numpy as np
        N_HEAD = 16
        Q_DIM = 64
        V_DIM = 64
        WINDOW = 129
        DIL = 1
        B, N, E = x.shape
        Q = (x @ Wq + bq).reshape(B, N, N_HEAD, Q_DIM).transpose(0, 2, 1, 3)
        K = (x @ Wk + bk).reshape(B, N, N_HEAD, Q_DIM).transpose(0, 2, 1, 3)
        V = (x @ Wv + bv).reshape(B, N, N_HEAD, V_DIM).transpose(0, 2, 1, 3)
        scores = jnp.einsum('bhid,bhjd->bhij', Q, K)
        idx = jnp.arange(N)
        diff = idx[None, :] - idx[:, None]
        half = WINDOW // 2
        band = (jnp.abs(diff) <= half * DIL) & (diff % DIL == 0)
        columns = jnp.where(band[None, None], scores, jnp.float32(0.0))
        attn = jax.nn.softmax(columns, axis=-1)
        out = attn @ V
        out = out.transpose(0, 2, 1, 3).reshape(B, N, N_HEAD * V_DIM)
        return out @ Wo + bo

    def _L1_xattn_ref(x, context, w_qkv, w_proj, b_proj):
        import jax, jax.numpy as jnp
        import numpy as np
        NUM_HEADS = 16
        B, N, C = x.shape
        H = NUM_HEADS
        D = C // H
        scale = D ** (-0.5)
        qkv = (x @ w_qkv.T).reshape(B, N, 3, H, D).transpose(2, 0, 3, 1, 4)
        q, k, v = (qkv[0], qkv[1], qkv[2])
        N_c = context.shape[1]
        kv = context.reshape(B, N_c, 2, H, D).transpose(2, 0, 3, 1, 4)
        extra_k, extra_v = (kv[0], kv[1])
        k = jnp.concatenate([extra_k, k], axis=2)
        v = jnp.concatenate([extra_v, v], axis=2)
        dtype = q.dtype
        attn = jnp.einsum('bhnd,bhmd->bhnm', q * scale, k).astype(jnp.float32)
        attn = jax.nn.softmax(attn, axis=-1).astype(dtype)
        out = jnp.einsum('bhnm,bhmd->bhnd', attn, v)
        out = out.transpose(0, 2, 1, 3).reshape(B, N, C)
        return out @ w_proj.T + b_proj

    def _L1_ffn_ref(x, Wq, bq, Wk, bk, Wv, bv, Wo, bo, Wg, bg, W1, b1, W2, b2, g1, be1, g2, be2):
        import jax, jax.numpy as jnp
        import numpy as np
        from math import sqrt
        B, S, D, H, E, K, FF = (2, 128, 128, 16, 8, 2, 512)
        HD = D // H
        EPS = 1e-05

        def _rope_cache(seq_len, hd):
            inv_freq = 1.0 / 10000.0 ** (jnp.arange(0, hd, 2, dtype=jnp.float32) / hd)
            t = jnp.arange(seq_len, dtype=jnp.float32)
            freqs = t[:, None] * inv_freq[None, :]
            emb = jnp.concatenate([freqs, freqs], axis=-1)
            return (jnp.cos(emb), jnp.sin(emb))

        def _rotate_half(x):
            x1, x2 = jnp.split(x, 2, axis=-1)
            return jnp.concatenate([-x2, x1], axis=-1)

        def _layernorm(x, g, b):
            m = jnp.mean(x, axis=-1, keepdims=True)
            v = jnp.var(x, axis=-1, keepdims=True)
            return (x - m) * jax.lax.rsqrt(v + EPS) * g + b

        def _forward(x, Wq, bq, Wk, bk, Wv, bv, Wo, bo, Wg, bg, W1, b1, W2, b2, g1, be1, g2, be2):
            bsz, seq, d = x.shape
            q = (x @ Wq + bq).reshape(bsz, seq, H, HD).transpose(0, 2, 1, 3)
            k = (x @ Wk + bk).reshape(bsz, seq, H, HD).transpose(0, 2, 1, 3)
            v = (x @ Wv + bv).reshape(bsz, seq, H, HD).transpose(0, 2, 1, 3)
            cos, sin = _rope_cache(seq, HD)
            cos = cos[None, None]
            sin = sin[None, None]
            q = q * cos + _rotate_half(q) * sin
            k = k * cos + _rotate_half(k) * sin
            scores = jnp.einsum('bhqd,bhkd->bhqk', q, k) / sqrt(HD)
            attn = jax.nn.softmax(scores, axis=-1)
            ao = jnp.einsum('bhqk,bhkd->bhqd', attn, v)
            ao = ao.transpose(0, 2, 1, 3).reshape(bsz, seq, d)
            attn_out = ao @ Wo + bo
            x1 = _layernorm(x + attn_out, g1, be1)
            gate_logits = x1 @ Wg + bg
            gate_probs = jax.nn.softmax(gate_logits, axis=-1)
            topk_p, topk_i = jax.lax.top_k(gate_probs, K)
            topk_p = topk_p / jnp.sum(topk_p, axis=-1, keepdims=True)
            comb = jnp.sum(jax.nn.one_hot(topk_i, E, dtype=x.dtype) * topk_p[..., None], axis=-2)
            h = jax.nn.gelu(jnp.einsum('bsd,edf->bsef', x1, W1) + b1, approximate=False)
            y = jnp.einsum('bsef,efd->bsed', h, W2) + b2
            moe_out = jnp.einsum('bse,bsed->bsd', comb, y)
            return _layernorm(x1 + moe_out, g2, be2)
        return _forward(x, Wq, bq, Wk, bk, Wv, bv, Wo, bo, Wg, bg, W1, b1, W2, b2, g1, be1, g2, be2)
    x = _layernorm(x + _L0_attn_ref(x, L0_attn_W_Q, L0_attn_W_K, L0_attn_W_V, L0_attn_W_G, L0_attn_W_O, L0_attn_gn_weight, L0_attn_gn_bias), axis=-1)
    x = _layernorm(x + _L0_xattn_ref(ctx_2048, x, mask_BxS2_fk1, mask_BxS2_fk1, L0_xattn_W_src, L0_xattn_b_src, L0_xattn_W_tgt, L0_xattn_b_tgt, L0_xattn_W_out, L0_xattn_b_out), axis=-1)
    x = _layernorm(x + _L0_ffn_ref(x, L0_ffn_gate_weight, L0_ffn_gate_up_proj, L0_ffn_down_proj, L0_ffn_similarity_matrix), axis=-1)
    x = _layernorm(x + _L1_attn_ref(x, L1_attn_Wq, L1_attn_bq, L1_attn_Wk, L1_attn_bk, L1_attn_Wv, L1_attn_bv, L1_attn_Wo, L1_attn_bo), axis=-1)
    x = _layernorm(x + _L1_xattn_ref(x, ctx_2048, L1_xattn_w_qkv, L1_xattn_w_proj, L1_xattn_b_proj), axis=-1)
    x = _layernorm(x + _L1_ffn_ref(x, L1_ffn_Wq, L1_ffn_bq, L1_ffn_Wk, L1_ffn_bk, L1_ffn_Wv, L1_ffn_bv, L1_ffn_Wo, L1_ffn_bo, L1_ffn_Wg, L1_ffn_bg, L1_ffn_W1, L1_ffn_b1, L1_ffn_W2, L1_ffn_b2, L1_ffn_g1, L1_ffn_be1, L1_ffn_g2, L1_ffn_be2), axis=-1)
    return x

_drawn_inputs = setup_inputs


def setup_inputs(seed=0):
    import zlib

    import numpy as np

    out = dict(_drawn_inputs(seed))
    spreads = {'L0_attn_gn_weight': (1.0, 0.6),
     'L0_attn_gn_bias': (0.0, 0.8),
     'L0_xattn_b_src': (0.0, 0.1),
     'L0_xattn_b_tgt': (0.0, 0.61),
     'L0_xattn_b_out': (0.0, 0.1),
     'L1_ffn_bq': (0.0, 0.8),
     'L1_ffn_bk': (0.0, 0.8),
     'L1_ffn_bv': (0.0, 0.626),
     'L1_ffn_bo': (0.0, 0.1),
     'L1_ffn_bg': (0.0, 0.3),
     'L1_ffn_b1': (0.0, 0.8),
     'L1_ffn_b2': (0.0, 0.1),
     'L1_ffn_g1': (1.0, 0.2),
     'L1_ffn_be1': (0.0, 0.1),
     'L1_ffn_g2': (1.0, 0.2),
     'L1_ffn_be2': (0.0, 0.1)}
    factors = {'L0_attn_W_Q': 8.0,
     'L0_attn_W_K': 8.0,
     'L0_attn_W_V': 8.0,
     'L0_attn_W_G': 8.0,
     'L0_attn_W_O': 8.0,
     'L0_ffn_gate_weight': 8.0,
     'L0_ffn_gate_up_proj': 8.0,
     'L0_ffn_down_proj': 8.0,
     'L1_attn_Wq': 5.975,
     'L1_attn_bq': 8.0,
     'L1_attn_Wk': 5.883,
     'L1_attn_bk': 8.0,
     'L1_attn_bv': 4.151,
     'L1_attn_bo': 2.668,
     'L1_xattn_w_qkv': 5.198,
     'L1_ffn_Wq': 8.0,
     'L1_ffn_Wk': 8.0,
     'L1_ffn_Wv': 5.889,
     'L1_ffn_Wo': 3.896,
     'L1_ffn_W1': 2.965}
    for name, (base, spread) in spreads.items():
        noise = np.random.default_rng([zlib.crc32(name.encode()), seed]).standard_normal(out[name].shape)
        drawn = base * np.exp(spread * noise) if base else spread * noise
        out[name] = jnp.asarray(drawn.astype(out[name].dtype))
    for name, factor in factors.items():
        out[name] = (out[name] * factor).astype(out[name].dtype)
    return out
```

```python
from contextlib import ExitStack

import numpy as np

import concourse.bass as bass
from concourse import mybir

F32 = mybir.dt.float32
U32 = mybir.dt.uint32
ACT = mybir.ActivationFunctionType
ALU = mybir.AluOpType
AX = mybir.AxisListType

SEQ = 64
DIM = 128
CTX = 256
SLOTS = 2
TB = 8
T = 4
NT = TB * SEQ
NE = 8
FF = 512
NC = FF // 128
EPS = 1e-5
NEG = -1e30



def spans(*sizes):
    at, out = 0, {}
    for name, n in sizes:
        out[name] = (at, n)
        at += n
    return out, at


CONST, NCONST = spans(("ident", 128), ("cq", 64), ("sq", 64), ("ck", 64), ("sk", 64), ("decay", 256),
                      ("cos", 64), ("sin", 64), ("par", 2), ("quad", 4), ("iota", 8),
                      ("ones", 8))
WA, NWA = spans(("wq", 128), ("wqs", 128), ("wk", 128), ("wks", 128), ("wv", 128), ("wg", 128), ("wo", 128),
                ("xk", 256), ("xv", 256), ("xq", 128), ("xo", 128), ("gate", 8))
W64, NW64 = spans(("xo", 256), ("x1", 256), ("fo", 256))
ROWS, NROWS = spans(("gnw", 128), ("gnb", 128), ("xbv", 128), ("xbo", 128),
                    ("abo", 128), ("pb", 128), ("fbv", 128), ("fbo", 128), ("g1", 128), ("be1", 128),
                    ("g2", 128), ("be2", 128), ("bg", 8), ("abv", 1024))
COLS, NCOLS = spans(("xbt", 1), ("xbk", 1), ("abq", 8), ("abk", 8), ("fbq", 1), ("fbqs", 1), ("fbk", 1),
                    ("fbks", 1), ("b1", 32))
WB, NWB = spans(("gu", NE * 256), ("down", NE * 128), ("aq", 1024), ("ak", 1024), ("av", 1024), ("ao", 1024),
                ("cq", 128), ("ck", 128), ("cv", 128), ("fq", 128), ("fqs", 128), ("fk", 128), ("fks", 128),
                ("fv", 128), ("fg", 8))
W8, NW8 = spans(("sim", 8), ("eye", 8), ("b2", 128))


class Signal:

    def __init__(self, sem, each=1, uses=1):
        self.sem, self.each, self.per_pass = sem, each, SLOTS * each * uses

    def at(self, n, s, k=None, use=0):
        return n * self.per_pass + (SLOTS * use + s) * self.each + (self.each if k is None else k)


def apart(eng):
    eng.nop(nofuse=True)


class Steps:

    def __init__(self, sem, per_pass, base=0):
        self.sem, self.per_pass, self.k, self.base = sem, per_pass, 0, base

    def __call__(self, eng, n, ins):
        self.k += 1
        ins.then_inc(self.sem, 1)
        eng.wait_ge(self.sem, n * self.per_pass + self.k + self.base)


def build(nc, d, out, groups):
    passes = groups // SLOTS
    ctx = ExitStack()
    with ctx:
        def sb(name, shape, dt=F32):
            return ctx.enter_context(nc.sbuf_tensor(name, shape, dt))

        def sem(name):
            return ctx.enter_context(nc.semaphore(name))

        def signal(name, each=1, uses=1):
            return Signal(sem(name), each, uses)

        const = sb("const", [128, NCONST])
        wa = sb("wa", [128, NWA])
        w64 = sb("w64", [64, NW64])
        rows = sb("rows", [128, NROWS])
        cols = sb("cols", [128, NCOLS])
        wb = sb("wb", [128, NWB])
        w8 = sb("w8", [8, NW8])

        def part(tensor, table, name, p=128):
            at, n = table[name]
            return tensor[0:p, at:at + n]

        def C(name): return part(const, CONST, name)
        def A(name): return part(wa, WA, name)
        def Wp(name, par): return part(w64, W64, name, 64)[:, par * 128:par * 128 + 128]
        def Row(name): return part(rows, ROWS, name)
        def Col(name, k=0): return part(cols, COLS, name)[:, k:k + 1]
        def B(name): return part(wb, WB, name)
        def W8p(name): return part(w8, W8, name, 8)
        ident = C("ident")
        x_mid = d["x_mid"]
        wt_all = sb("wt_all", [128, groups * T, NE])
        prim = sb("prim", [128, NE])

        def per_slot(name, shape, dt=F32):
            return [sb(f"{name}{s}", shape, dt) for s in range(SLOTS)]

        X = per_slot("X", [128, T, DIM])
        XT = per_slot("XT", [128, NT])
        R = per_slot("R", [128, T, DIM])
        X1 = per_slot("X1", [128, T, DIM])
        P = per_slot("P", [128, 4, 512])
        PT = per_slot("PT", [128, 4, 512])
        Q2 = per_slot("Q2", [128, 4, 1024])
        K8 = per_slot("K8", [128, 2048])
        V8 = per_slot("V8", [128, 2048])
        O = per_slot("O", [128, TB, 64])
        stats = per_slot("stats", [128, T, 6])
        mv = per_slot("mv", [128, T, 2])
        rstd = per_slot("rstd", [128, T])
        small = per_slot("small", [128, 5, 32])
        gs = per_slot("gs", [128, 8, 32])
        gidx = per_slot("gidx", [128, T, 8], U32)
        maskc = per_slot("maskc", [128, T])
        power = sb("power", [128, 32])
        w1r = [sb(f"w1r{k}", [128, FF]) for k in range(2)]
        w2r = [sb(f"w2r{k}", [128, NC, DIM]) for k in range(2)]
        emap = sb("emap", [8, 12, 8])
        eidx = sb("eidx", [8, 8], U32)

        banks = [[ctx.enter_context(nc.psum_tensor(f"bank{s}_{k}", [128, 512], F32)) for k in range(4)]
                 for s in range(SLOTS)]

        def tok(ap):
            return ap.rearrange("p (t d) -> p t d", t=T)

        def seqs(ap):
            return ap.rearrange("p (b l) -> p b l", l=SEQ)

        def over(ap, n):
            return ap.unsqueeze(1).to_broadcast([ap.shape[0], n, ap.shape[1]])

        def each(ap, n):
            return ap.unsqueeze(2).to_broadcast([ap.shape[0], ap.shape[1], n])

        ctxT = [V8[s][:, 0:1024].rearrange("p (c n) -> p c n", c=2) for s in range(SLOTS)]
        maskr = [V8[s][:, 1024:1536] for s in range(SLOTS)]
        maskb = [V8[s][:, 1536:2048] for s in range(SLOTS)]
        KT = [K8[s][:, 0:512] for s in range(SLOTS)]
        QT = [K8[s][:, 512:1024] for s in range(SLOTS)]
        tmpa = [K8[s][:, 1024:1536] for s in range(SLOTS)]
        tmpb = [K8[s][:, 1536:2048] for s in range(SLOTS)]
        pair = [PT[s][:, 0:2, :].rearrange("p a (b r l) -> p (a b) r l", r=2, l=SEQ) for s in range(SLOTS)]
        vdiag = [Q2[s][:, 0, :].rearrange("p (b i c) -> p b i c", b=TB, c=32) for s in range(SLOTS)]
        xv = [Q2[s][:, 1:3, :].rearrange("p a c -> p (a c)")[:, 0:T * 4 * 66]
              .rearrange("p (t i b c) -> p t i b c", t=T, i=4, b=2) for s in range(SLOTS)]
        sg = [Q2[s][:, 3, 0:512] for s in range(SLOTS)]
        yc = [Q2[s][:, 3, 512:1024] for s in range(SLOTS)]
        ysq = [PT[s][:, 2, :] for s in range(SLOTS)]
        hT = [PT[s][:, 3, :] for s in range(SLOTS)]
        OT2 = [P[s][0:64, 0:2, :] for s in range(SLOTS)]

        s_const, s_init = sem("s_const"), sem("s_init")
        s_init_v = sem("s_init_v")
        loaded = [sem(f"loaded{s}") for s in range(SLOTS)]
        stored = [sem(f"stored{s}") for s in range(SLOTS)]
        a_qk_ps = signal("a_qk_ps", 4)
        a_qk_mul = signal("a_qk_mul", 4)
        a_k_sum = signal("a_k_sum", 2)
        a_k_pair = signal("a_k_pair")
        a_vg_ps = signal("a_vg_ps", 2)
        a_v_diag = signal("a_v_diag")
        a_tanh = signal("a_tanh")
        a_gated = signal("a_gated")
        a_st_ps = signal("a_st_ps", 4)
        a_st = signal("a_st", 4)
        a_y_ps = signal("a_y_ps")
        a_y_cent = signal("a_y_cent")
        a_y_sq = signal("a_y_sq")
        a_y_var = signal("a_y_var")
        a_y_rstd = signal("a_y_rstd")
        a_y_norm = signal("a_y_norm")
        a_y_aff = signal("a_y_aff")
        a_h = signal("a_h")
        a_h_ps = signal("a_h_ps")
        a_hT = signal("a_hT")
        a_o_ps = signal("a_o_ps")
        a_ln_mv = signal("a_ln_mv", 1, 2)
        a_ln_rstd = signal("a_ln_rstd", 1, 2)
        a_x = signal("a_x", 1, 2)
        a_x_ps = signal("a_x_ps", 1, 2)
        a_xT = signal("a_xT", 1, 2)
        a_kv_ps = signal("a_kv_ps", 3)
        a_bias = signal("a_bias")
        a_q = signal("a_q")
        a_kT = signal("a_kT")
        a_v = signal("a_v")
        a_q_pair = signal("a_q_pair")
        a_s_ps = signal("a_s_ps", 4)
        a_s_sub = signal("a_s_sub", 4)
        a_p = signal("a_p", 4)
        a_p_ps = signal("a_p_ps", 4)
        a_pT = signal("a_pT", 4)
        a_r_ps = signal("a_r_ps", 4)
        a_r = signal("a_r")
        a_rt_ps = signal("a_rt_ps", 2)
        a_rT = signal("a_rT", 2)
        a_o2_ps = signal("a_o2_ps")
        a_g_ps = signal("a_g_ps")
        a_g_diff = signal("a_g_diff")
        a_g_exp = signal("a_g_exp")
        a_g_done = signal("a_g_done")
        dve1, act1, pool1 = Steps(sem("dve1"), STEPS["dve1"]), Steps(sem("act1"), STEPS["act1"]), Steps(sem("pool1"), STEPS["pool1"])

        kcat = [K8[s][:, 0:1024].rearrange("p (b m) -> p b m", m=128) for s in range(SLOTS)]
        vcat = [V8[s][:, 0:TB * 8 * 17].rearrange("p (b g c) -> p b g c", b=TB, g=8) for s in range(SLOTS)]
        vf = [V8[s][:, 0:T * 8 * 34].rearrange("p (t g b c) -> p t g b c", t=T, g=8, b=2) for s in range(SLOTS)]
        qdiag = [Q2[s][:, :, :].rearrange("p c (b r l) -> p c b r l", r=2, l=SEQ) for s in range(SLOTS)]
        kc = [K8[s][:, :].rearrange("p (c n) -> p c n", c=4) for s in range(SLOTS)]
        va = [V8[s][:, :].rearrange("p (t n) -> p t n", t=T) for s in range(SLOTS)]
        q4 = [[Q2[s][:, 2 * k:2 * k + 2, :].rearrange("p a (b j l) -> p (a b) j l", j=4, l=SEQ)
               for s in range(SLOTS)] for k in range(2)]
        kf = [K8[s][:, 0:512] for s in range(SLOTS)]
        qf = [K8[s][:, 512:1024] for s in range(SLOTS)]
        wts = [gs[s][:, 2, :].rearrange("p (t e) -> p t e", t=T) for s in range(SLOTS)]
        share = [gs[s][:, 3, :].rearrange("p (t e) -> p t e", t=T) for s in range(SLOTS)]
        wtT = [O[s][0:8, :, :].rearrange("p b c -> p (b c)") for s in range(SLOTS)]
        s_prim, s_cnt, s_map, s_q2 = sem("s_prim"), sem("s_cnt"), sem("s_map"), sem("s_q2")
        s_mid = Steps(sem("s_mid"), 0)
        reloaded = [sem(f"reloaded{s}") for s in range(SLOTS)]
        context = [sem(f"context{s}") for s in range(SLOTS)]
        w_loaded = [sem(f"w_loaded{k}") for k in range(2)]
        written = [sem(f"written{s}") for s in range(SLOTS)]
        b_x_ps = signal("b_x_ps", 1, 5)
        b_xT = signal("b_xT", 1, 5)
        b_x = signal("b_x", 1, 4)
        b_x1 = signal("b_x1")
        b_ln_x1 = signal("b_ln_x1", 1, 2)
        b_ln_mv = signal("b_ln_mv", 1, 6)
        b_ln_rstd = signal("b_ln_rstd", 1, 6)
        b_wts = signal("b_wts")
        b_wt_ps = signal("b_wt_ps", 1, 2)
        b_wtT = signal("b_wtT", 1, 2)
        b_share_ps = signal("b_share_ps")
        b_share = signal("b_share")
        b_up_ps = signal("b_up_ps", 2, 8)
        b_tanh = signal("b_tanh", 1, 8)
        b_fh = signal("b_fh", 1, 8)
        b_down_ps = signal("b_down_ps", 1, 8)
        b_comb = signal("b_comb", 1, 8)
        b_aq_ps = signal("b_aq_ps", 4, 2)
        b_aq_a = signal("b_aq_a", 2, 2)
        b_aq_v = signal("b_aq_v", 2, 2)
        b_ak_ps = signal("b_ak_ps", 4, 2)
        b_ak = signal("b_ak", 4, 2)
        b_av_ps = signal("b_av_ps", 4, 2)
        b_av = signal("b_av", 4, 2)
        b_as_ps = signal("b_as_ps", 4, 2)
        b_as_sub = signal("b_as_sub", 4, 2)
        b_ap = signal("b_ap", 4, 2)
        b_arc = signal("b_arc", 4, 2)
        b_an = signal("b_an", 4, 2)
        b_ap_ps = signal("b_ap_ps", 4, 2)
        b_apT = signal("b_apT", 4, 2)
        b_ao_ps = signal("b_ao_ps", 4, 2)
        b_aoT = signal("b_aoT", 4, 2)
        b_out_ps = signal("b_out_ps", 1, 2)
        b_out = signal("b_out", 1, 2)
        b_cqk_ps = signal("b_cqk_ps", 2)
        b_cv_ps = signal("b_cv_ps", 2)
        b_cq = signal("b_cq")
        b_ck = signal("b_ck")
        b_cv = signal("b_cv")
        b_cones = signal("b_cones")
        b_s_ps = signal("b_s_ps", 4, 6)
        b_s_sub = signal("b_s_sub", 4, 6)
        b_p = signal("b_p", 4, 6)
        b_p_ps = signal("b_p_ps", 4, 6)
        b_pT = signal("b_pT", 4, 6)
        b_r_ps = signal("b_r_ps", 1, 6)
        b_r = signal("b_r", 1, 6)
        b_rt_ps = signal("b_rt_ps", 2, 2)
        b_rT = signal("b_rT", 2, 2)
        b_o_ps = signal("b_o_ps", 1, 2)
        b_fqk_ps = signal("b_fqk_ps", 4)
        b_frot = signal("b_frot", 4)
        b_fsum = signal("b_fsum", 2)
        b_fq = signal("b_fq")
        b_fzero = signal("b_fzero")
        b_fv_ps = signal("b_fv_ps")
        b_fv = signal("b_fv")
        b_g_ps = signal("b_g_ps")
        b_g_diff = signal("b_g_diff")
        b_g_exp = signal("b_g_exp")
        b_g_done = signal("b_g_done")
        b_b2_ps = signal("b_b2_ps")
        b_b2 = signal("b_b2")
        b_mup_ps = signal("b_mup_ps", 4, 8)
        b_gelu = signal("b_gelu", 4, 8)
        b_mdown_ps = signal("b_mdown_ps", 1, 8)
        b_mcomb = signal("b_mcomb", 1, 8)
        b_r2 = signal("b_r2")
        dve2, pool2 = Steps(sem("dve2"), STEPS["dve2"]), Steps(sem("pool2"), STEPS["pool2"])

        block = ctx.enter_context(nc.Block())

        @block.sync
        def _(sp):
            for dst, src in ((const, d["const"]), (wa, d["wa"]), (w64, d["w64"]), (cols, d["cols"]),
                             (w8, d["w8"]), (wb, d["wb"])):
                sp.dma_start(dst[:, :], src).then_inc(s_const, 16)
            sp.dma_start(rows[:, :], d["rows"].partition_broadcast(128)).then_inc(s_const, 16)

            def loads(n, s):
                g0 = (n * SLOTS + s) * TB
                t0 = (n * SLOTS + s) * NT
                sp.dma_start(XT[s][:, :], d["xT"][:, bass.ds(t0, NT)]).then_inc(loaded[s], 16)
                for c in range(2):
                    sp.dma_start(ctxT[s][:, c, :], d["ctxT"][c * 128:c * 128 + 128, bass.ds(t0, NT)])\
                      .then_inc(loaded[s], 16)
                sp.dma_start(X[s][:, :, :], d["x"][bass.ds(t0, NT), :].rearrange("(t p) d -> p t d", p=128))\
                  .then_inc(loaded[s], 16)
                sp.dma_start(maskr[s], d["mask"][bass.ds(t0, NT)].partition_broadcast(128))\
                  .then_inc(loaded[s], 16)
                sp.dma_start(maskc[s][:, :], d["mask"][bass.ds(t0, NT)].rearrange("(t p) -> p t", p=128),
                             allow_slow_non_contiguous=True).then_inc(loaded[s], 16)

            def store_mid(n, s):
                sp.wait_ge(a_x.sem, a_x.at(n, s, use=1))
                sp.dma_start(x_mid[bass.ds((n * SLOTS + s) * NT, NT), :].rearrange("(t p) d -> p t d", p=128),
                             X[s][:, :, :]).then_inc(stored[s], 16)

            for s in range(SLOTS):
                loads(0, s)
            with sp.Fori(0, passes - 1) as n:
                for s in range(SLOTS):
                    store_mid(n, s)
                    sp.wait_ge(a_g_done.sem, a_g_done.at(n, s))
                    sp.wait_ge(stored[s], 16 * n + 16)
                    loads(n + 1, s)
            for s in range(SLOTS):
                store_mid(passes - 1, s)
            for s in range(SLOTS):
                sp.wait_ge(stored[s], 16 * passes)
                sp.wait_ge(a_g_done.sem, a_g_done.at(passes - 1, s))

            def load_state(n, s):
                sp.dma_start(X[s][:, :, :], x_mid[bass.ds((n * SLOTS + s) * NT, NT), :]
                             .rearrange("(t p) d -> p t d", p=128)).then_inc(reloaded[s], 16)

            def load_context(n, s):
                g0, t0 = (n * SLOTS + s) * TB, (n * SLOTS + s) * NT
                sp.wait_ge(b_ao_ps.sem, b_ao_ps.at(n, s, use=1))
                sp.dma_start(kcat[s][:, :, 0:SEQ], d["ctxT"][0:128, bass.ds(t0, NT)]
                             .rearrange("p (b m) -> p b m", m=SEQ)).then_inc(context[s], 16)
                for b in range(TB):
                    sp.dma_start(vcat[s][0:SEQ, b, :, 0:16], d["ctx"][bass.ds(t0 + SEQ * b, SEQ), 128:256]
                                 .rearrange("m (g v) -> m g v", v=16)).then_inc(context[s], 16)

            def load_expert(e):
                sp.dma_start(w1r[e % 2][:, :], d["w1"][e]).then_inc(w_loaded[e % 2], 16)
                sp.dma_start(w2r[e % 2][:, :, :], d["w2"][e].rearrange("(c p) d -> p c d", p=128))\
                  .then_inc(w_loaded[e % 2], 16)

            def store(n, s):
                sp.wait_ge(b_x.sem, b_x.at(n, s, use=3))
                sp.dma_start(out[bass.ds((n * SLOTS + s) * NT, NT), :].rearrange("(t p) d -> p t d", p=128),
                             X[s][:, :, :]).then_inc(written[s], 16)

            def one_pass(n, last):
                for s in range(SLOTS):
                    load_context(n, s)
                for e in range(NE):
                    sp.wait_ge(b_mdown_ps.sem, b_mdown_ps.at(n, 1, use=e))
                    if e < NE - 2 or not last:
                        load_expert((e + 2) % NE)
                for s in range(SLOTS):
                    store(n, s)
                    if not last:
                        sp.wait_ge(written[s], 16 * n + 16)
                        load_state(n + 1, s)

            for s in range(SLOTS):
                load_state(0, s)
            for e in range(2):
                load_expert(e)
            with sp.Fori(0, passes - 1) as n:
                one_pass(n, False)
            one_pass(passes - 1, True)
            for s in range(SLOTS):
                sp.wait_ge(written[s], 16 * passes)

        @block.gpsimd
        def _(pool):
            pool.memset(power[:, :], -0.5)
            pool.memset(prim[:, :], 0.0)
            for s in range(SLOTS):
                last = pool.memset(Q2[s][:, :, :], 0.0)
            last.then_inc(s_init, 1)
            pool.wait_ge(s_init, 1)
            for s in range(SLOTS):
                for b in range(2):
                    last = pool.memset(xv[s][64 * b:64 * b + 64, :, :, b, 32:33], 1.0)
            last.then_inc(s_init, 1)
            pool.wait_ge(s_const, 16 * 7)

            def norm_rstd(n, s, use):
                pool.wait_ge(a_ln_mv.sem, a_ln_mv.at(n, s, use=use))
                apart(pool)
                pool1(pool, n, pool.tensor_scalar(rstd[s][:, :], mv[s][:, :, 1], EPS, None, ALU.add))
                pool.tensor_tensor(rstd[s][:, :], rstd[s][:, :], power[:, 0:T], ALU.pow).then_inc(a_ln_rstd.sem, 1)

            with pool.Fori(0, passes) as n:
                for s in range(SLOTS):
                    pool.wait_ge(a_qk_mul.sem, a_qk_mul.at(n, s, 2))
                    pool.tensor_tensor(KT[s], P[s][:, 0, :], P[s][:, 1, :], ALU.add).then_inc(a_k_sum.sem, 1)
                    pool.wait_ge(a_qk_mul.sem, a_qk_mul.at(n, s, 4))
                    pool.tensor_tensor(QT[s], P[s][:, 2, :], P[s][:, 3, :], ALU.add).then_inc(a_k_sum.sem, 1)
                    pool.tensor_scalar(maskb[s], maskr[s], 0.0, NEG, ALU.is_equal, ALU.mult).then_inc(a_bias.sem, 1)
                for s in range(SLOTS):
                    pool.wait_ge(a_y_var.sem, a_y_var.at(n, s))
                    apart(pool)
                    pool1(pool, n, pool.tensor_scalar(gs[s][:, 2, :], gs[s][:, 1, :], 1.0 / 16, EPS, ALU.mult, ALU.add))
                    pool.tensor_tensor(gs[s][:, 3, :], gs[s][:, 2, :], power[:, :], ALU.pow).then_inc(a_y_rstd.sem, 1)
                for s in range(SLOTS):
                    pool.wait_ge(a_y_norm.sem, a_y_norm.at(n, s))
                    pool1(pool, n, pool.tensor_tensor(tok(yc[s]), tok(yc[s]), over(Row("gnw"), T), ALU.mult))
                    pool.tensor_tensor(tok(yc[s]), tok(yc[s]), over(Row("gnb"), T), ALU.add).then_inc(a_y_aff.sem, 1)
                for s in range(SLOTS):
                    norm_rstd(n, s, 0)
                for s in range(SLOTS):
                    norm_rstd(n, s, 1)

            for s in range(SLOTS):
                pool.wait_ge(a_g_done.sem, a_g_done.at(passes - 1, s))
            for s in range(SLOTS):
                pool.memset(Q2[s][:, :, :], 0.0).then_inc(s_q2, 1)

            def rstd2(n, s, use):
                pool.wait_ge(b_ln_mv.sem, b_ln_mv.at(n, s, use=use))
                apart(pool)
                pool2(pool, n, pool.tensor_scalar(rstd[s][:, :], mv[s][:, :, 1], EPS, None, ALU.add))
                pool.tensor_tensor(rstd[s][:, :], rstd[s][:, :], power[:, 0:T], ALU.pow).then_inc(b_ln_rstd.sem, 1)

            def scale_shift(n, s, g, b):
                pool2(pool, n, pool.tensor_tensor(X1[s][:, :, :], X1[s][:, :, :], over(Row(g), T), ALU.mult))
                return pool.tensor_tensor(X1[s][:, :, :], X1[s][:, :, :], over(Row(b), T), ALU.add)

            with pool.Fori(0, passes) as n:
                for s in range(SLOTS):
                    apart(pool)
                    pool.tensor_copy(wts[s], wt_all[:, bass.ds((n * SLOTS + s) * T, T), :]).then_inc(b_wts.sem, 1)
                for s in range(SLOTS):
                    rstd2(n, s, 0)
                for r in range(2):
                    for s in range(SLOTS):
                        for c in range(4):
                            pool.wait_ge(b_arc.sem, b_arc.at(n, s, c + 1, use=r))
                            pool.tensor_tensor(seqs(P[s][:, c, :]), seqs(P[s][:, c, :]),
                                                           each(gs[s][:, 2, 8 * c:8 * c + 8], SEQ), ALU.mult).then_inc(b_an.sem, 1)
                for s in range(SLOTS):
                    pool.wait_ge(b_ao_ps.sem, b_ao_ps.at(n, s, use=1))
                    apart(pool)
                    pool.memset(vcat[s][:, :, :, 16:17], 1.0).then_inc(b_cones.sem, 1)
                for s in range(SLOTS):
                    rstd2(n, s, 1)
                for s in range(SLOTS):
                    pool.wait_ge(b_r_ps.sem, b_r_ps.at(n, s, use=3))
                    apart(pool)
                    pool2(pool, n, pool.memset(V8[s][:, 0:T * 8 * 34], 0.0))
                    apart(pool)
                    for b in range(2):
                        last = pool.memset(vf[s][64 * b:64 * b + 64, :, :, b, 16:17], 1.0)
                    last.then_inc(b_fzero.sem, 1)
                    pool.wait_ge(b_fzero.sem, b_fzero.at(n, s))
                    apart(pool)
                for s in range(SLOTS):
                    rstd2(n, s, 2)
                for s in range(SLOTS):
                    pool.wait_ge(b_frot.sem, b_frot.at(n, s, 2))
                    pool.tensor_tensor(qf[s], P[s][:, 0, :], P[s][:, 1, :], ALU.add).then_inc(b_fsum.sem, 1)
                    pool.wait_ge(b_frot.sem, b_frot.at(n, s, 4))
                    pool.tensor_tensor(kf[s], P[s][:, 2, :], P[s][:, 3, :], ALU.add).then_inc(b_fsum.sem, 1)
                for s in range(SLOTS):
                    pool.wait_ge(b_s_ps.sem, b_s_ps.at(n, s, use=5))
                    apart(pool)
                    pool.memset(Q2[s][:, :, :], 0.0).then_inc(s_q2, 1)
                for s in range(SLOTS):
                    rstd2(n, s, 3)
                for s in range(SLOTS):
                    pool.wait_ge(b_ln_x1.sem, b_ln_x1.at(n, s, use=0))
                    scale_shift(n, s, "g1", "be1").then_inc(b_x1.sem, 1)
                for s in range(SLOTS):
                    rstd2(n, s, 4)
                for s in range(SLOTS):
                    pool.wait_ge(b_ln_x1.sem, b_ln_x1.at(n, s, use=1))
                    pool2(pool, n, scale_shift(n, s, "g2", "be2"))
                    pool.tensor_tensor(R[s][:, :, :], X1[s][:, :, :], X[s][:, :, :], ALU.add).then_inc(b_r2.sem, 1)
                for s in range(SLOTS):
                    rstd2(n, s, 5)

        @block.scalar
        def _(act):
            act.wait_ge(s_init, 2)
            act.wait_ge(s_const, 16 * 7)
            with act.Fori(0, passes) as n:
                for s in range(SLOTS):
                    act.wait_ge(a_k_sum.sem, a_k_sum.at(n, s, 1))
                    for r in range(2):
                        last = act.activation(pair[s][:, :, r, :], seqs(KT[s]), ACT.Copy, scale=C("par")[:, r:r + 1])
                    last.then_inc(a_k_pair.sem, 1)
                for s in range(SLOTS):
                    act.wait_ge(a_vg_ps.sem, a_vg_ps.at(n, s, 1))
                    for r in range(2):
                        h = slice(64 * r, 64 * r + 64)
                        last = act.activation(vdiag[s][h, :, :, 16 * r:16 * r + 16],
                                              banks[s][0][h, :].rearrange("p (b i v) -> p b i v", b=TB, v=16), ACT.Copy)
                    last.then_inc(a_v_diag.sem, 1)
                    act.wait_ge(a_vg_ps.sem, a_vg_ps.at(n, s, 2))
                    act.activation(sg[s], banks[s][1][:, :], ACT.Tanh, scale=0.5).then_inc(a_tanh.sem, 1)
                for s in range(SLOTS):
                    act.wait_ge(a_y_cent.sem, a_y_cent.at(n, s))
                    act.activation(ysq[s], yc[s], ACT.Square).then_inc(a_y_sq.sem, 1)
                for s in range(SLOTS):
                    act.wait_ge(a_h_ps.sem, a_h_ps.at(n, s))
                    act.activation(hT[s], banks[s][1][:, :], ACT.Copy).then_inc(a_hT.sem, 1)
                for s in range(SLOTS):
                    act.wait_ge(a_x_ps.sem, a_x_ps.at(n, s, use=0))
                    act.activation(XT[s][:, :], banks[s][0][:, :], ACT.Copy).then_inc(a_xT.sem, 1)
                for s in range(SLOTS):
                    act.wait_ge(a_q.sem, a_q.at(n, s))
                    for r in range(2):
                        last = act.activation(pair[s][:, :, r, :], seqs(QT[s]), ACT.Copy, scale=C("par")[:, r:r + 1])
                    last.then_inc(a_q_pair.sem, 1)
                for s in range(SLOTS):
                    for i in range(4):
                        act.wait_ge(a_s_sub.sem, a_s_sub.at(n, s, i + 1))
                        act.activation(P[s][:, i, :], P[s][:, i, :], ACT.Exp).then_inc(a_p.sem, 1)
                for s in range(SLOTS):
                    for i in range(4):
                        act.wait_ge(a_p_ps.sem, a_p_ps.at(n, s, i + 1))
                        act.activation(PT[s][:, i, :], banks[s][i][:, :], ACT.Copy).then_inc(a_pT.sem, 1)
                for s in range(SLOTS):
                    for k in range(2):
                        act.wait_ge(a_rt_ps.sem, a_rt_ps.at(n, s, k + 1))
                        act.activation(
                            OT2[s][:, :, 256 * k:256 * k + 256].rearrange("p r (b l) -> p b r l", l=SEQ),
                            banks[s][k][0:64, :].rearrange("p (b r l) -> p b r l", r=2, l=SEQ), ACT.Copy).then_inc(a_rT.sem, 1)
                for s in range(SLOTS):
                    act.wait_ge(a_x_ps.sem, a_x_ps.at(n, s, use=1))
                    act.activation(XT[s][:, :], banks[s][3][:, :], ACT.Copy).then_inc(a_xT.sem, 1)
                for s in range(SLOTS):
                    act.wait_ge(a_g_diff.sem, a_g_diff.at(n, s))
                    act.activation(small[s][:, 1, 0:4], small[s][:, 0, 0:4], ACT.Exp).then_inc(a_g_exp.sem, 1)

            def turned(n, use, bank, src=None):
                for s in range(SLOTS):
                    act.wait_ge(b_x_ps.sem, b_x_ps.at(n, s, use=use))
                    act.activation(XT[s][:, :], banks[s][bank][:, :], ACT.Copy).then_inc(b_xT.sem, 1)

            def weights_turned(n, use):
                for s in range(SLOTS):
                    act.wait_ge(b_wt_ps.sem, b_wt_ps.at(n, s, use=use))
                    act.activation(wtT[s], banks[s][1][0:8, :], ACT.Copy).then_inc(b_wtT.sem, 1)

            def exps(n, use, scale):
                for s in range(SLOTS):
                    for i in range(4):
                        act.wait_ge(b_s_sub.sem, b_s_sub.at(n, s, i + 1, use=use))
                        act.activation(P[s][:, i, :], P[s][:, i, :], ACT.Exp, scale=scale).then_inc(b_p.sem, 1)
                for s in range(SLOTS):
                    for i in range(4):
                        act.wait_ge(b_p_ps.sem, b_p_ps.at(n, s, i + 1, use=use))
                        act.activation(PT[s][:, i, :], banks[s][i][:, :], ACT.Copy).then_inc(b_pT.sem, 1)

            def results_turned(n, use, base):
                for s in range(SLOTS):
                    for k in range(2):
                        act.wait_ge(b_rt_ps.sem, b_rt_ps.at(n, s, k + 1, use=use))
                        act.activation(
                            OT2[s][:, :, 256 * k:256 * k + 256].rearrange("p r (b l) -> p b r l", l=SEQ),
                            banks[s][base + k][0:64, :].rearrange("p (b r l) -> p b r l", r=2, l=SEQ), ACT.Copy).then_inc(b_rT.sem, 1)

            with act.Fori(0, passes) as n:
                turned(n, 0, 0)
                weights_turned(n, 0)
                for e in range(NE):
                    for s in range(SLOTS):
                        act.wait_ge(b_up_ps.sem, b_up_ps.at(n, s, 1, use=e))
                        act.activation(P[s][:, 0, :], banks[s][0][:, :], ACT.Tanh, scale=0.5).then_inc(b_tanh.sem, 1)
                turned(n, 1, 0)
                for r in range(2):
                    for s in range(SLOTS):
                        act.wait_ge(s_q2, SLOTS * n + SLOTS)
                        for c in (0, 2):
                            act.wait_ge(b_aq_ps.sem, b_aq_ps.at(n, s, c + 1, use=r))
                            for q in range(2):
                                h = slice(64 * q, 64 * q + 64)
                                last = act.activation(qdiag[s][h, c, :, q, :], seqs(banks[s][c][h, :]),
                                                      ACT.Identity, bias=Col("abq", 4 * r + c)[h, :])
                            last.then_inc(b_aq_a.sem, 1)
                    for s in range(SLOTS):
                        for c in range(4):
                            act.wait_ge(b_ak_ps.sem, b_ak_ps.at(n, s, c + 1, use=r))
                            act.activation(kc[s][:, c, :], banks[s][c][:, :], ACT.Identity,
                                                       bias=Col("abk", 4 * r + c)).then_inc(b_ak.sem, 1)
                    for s in range(SLOTS):
                        for c in range(4):
                            act.wait_ge(b_as_sub.sem, b_as_sub.at(n, s, c + 1, use=r))
                            act.activation(P[s][:, c, :], P[s][:, c, :], ACT.Exp).then_inc(b_ap.sem, 1)
                    for s in range(SLOTS):
                        for c in range(4):
                            act.wait_ge(b_ap_ps.sem, b_ap_ps.at(n, s, c + 1, use=r))
                            act.activation(PT[s][:, c, :], banks[s][c][:, :], ACT.Copy).then_inc(b_apT.sem, 1)
                    for s in range(SLOTS):
                        for c in range(4):
                            act.wait_ge(b_ao_ps.sem, b_ao_ps.at(n, s, c + 1, use=r))
                            act.activation(
                                P[s][:, 2 * (c % 2):2 * (c % 2) + 2, :].rearrange("p c (t b l) -> p c t b l", t=T, b=2)[:, :, :, c // 2, :],
                                banks[s][c][:, :].rearrange("p (c t l) -> p c t l", c=2, t=T), ACT.Copy).then_inc(b_aoT.sem, 1)
                turned(n, 2, 0)
                for s in range(SLOTS):
                    act.wait_ge(b_cqk_ps.sem, b_cqk_ps.at(n, s, 1))
                    for j in range(4):
                        last = act.activation(q4[0][s][:, :, j, :], seqs(banks[s][0][:, :]), ACT.Copy,
                                              scale=C("quad")[:, j:j + 1])
                    last.then_inc(b_cq.sem, 1)
                for t in range(T):
                    exps(n, t, 8 ** -0.5)
                results_turned(n, 0, 1)
                turned(n, 3, 0)
                for s in range(SLOTS):
                    act.wait_ge(b_fsum.sem, b_fsum.at(n, s, 1))
                    for j in range(4):
                        last = act.activation(q4[1][s][:, :, j, :], seqs(qf[s]), ACT.Copy, scale=C("quad")[:, j:j + 1])
                    last.then_inc(b_fq.sem, 1)
                for jh in range(2):
                    exps(n, 4 + jh, 8 ** -0.5)
                results_turned(n, 1, 2)
                turned(n, 4, 3)
                for s in range(SLOTS):
                    act.wait_ge(b_g_diff.sem, b_g_diff.at(n, s))
                    act.activation(small[s][:, 1, 0:4], small[s][:, 0, 0:4], ACT.Exp).then_inc(b_g_exp.sem, 1)
                weights_turned(n, 1)
                for e in range(NE):
                    for s in range(SLOTS):
                        for c in range(NC):
                            act.wait_ge(b_mup_ps.sem, b_mup_ps.at(n, s, c + 1, use=e))
                            act.activation(PT[s][:, c, :], banks[s][c % 3][:, :], ACT.Gelu,
                                                         bias=Col("b1", NC * e + c)).then_inc(b_gelu.sem, 1)

        @block.vector
        def _(dve):
            dve.wait_ge(s_init, 2)
            dve.wait_ge(s_const, 16 * 7)

            def norm(n, s, use, ln_mv, ln_rstd, steps, done, dst=None):
                dst = dst or X[s]
                for t in range(T):
                    last = dve.bn_stats(stats[s][:, t, :], R[s][:, t, :])
                steps(dve, n, last)
                apart(dve)
                for t in range(T):
                    last = dve.bn_aggr(mv[s][:, t, :], stats[s][:, t, :])
                last.then_inc(ln_mv.sem, 1)
                dve.wait_ge(ln_rstd.sem, ln_rstd.at(n, s, use=use))
                for t in range(T):
                    last = dve.tensor_scalar(dst[:, t, :], R[s][:, t, :], mv[s][:, t, 0:1], rstd[s][:, t:t + 1],
                                             ALU.subtract, ALU.mult)
                last.then_inc(done.sem, 1)

            def choose(n, s, g_diff, g_exp, g_done, steps, logits, weights, primary):
                st = lambda ins: steps(dve, n, ins)
                mx = gs[s][:, 4, :].rearrange("p (t e) -> p t e", t=T)
                idf = gs[s][:, 5, 0:8].rearrange("p (t k) -> p t k", t=T)
                one1 = gs[s][:, 6, :].rearrange("p (t e) -> p t e", t=T)
                one2 = gs[s][:, 7, :].rearrange("p (t e) -> p t e", t=T)
                apart(dve)
                for t in range(T):
                    last = dve.max(mx[:, t, :], logits[:, t, :])
                st(last)
                apart(dve)
                for t in range(T):
                    last = dve.max_index(gidx[s][:, t, :], mx[:, t, :], logits[:, t, :])
                st(last)
                dve.tensor_copy(idf, gidx[s][:, :, 0:2])
                dve.tensor_tensor(small[s][:, 0, 0:4], mx[:, :, 1], mx[:, :, 0], ALU.subtract).then_inc(g_diff.sem, 1)
                dve.wait_ge(g_exp.sem, g_exp.at(n, s))
                st(dve.tensor_scalar(small[s][:, 2, 0:4], small[s][:, 1, 0:4], 1.0, None, ALU.add))
                st(dve.reciprocal(small[s][:, 3, 0:4], small[s][:, 2, 0:4]))
                dve.tensor_tensor(small[s][:, 4, 0:4], small[s][:, 1, 0:4], small[s][:, 3, 0:4], ALU.mult)
                iota = over(C("iota"), T)
                dve.tensor_tensor(one1, iota, each(idf[:, :, 0], NE), ALU.is_equal)
                st(dve.tensor_tensor(one2, iota, each(idf[:, :, 1], NE), ALU.is_equal))
                if primary:
                    st(dve.tensor_reduce(small[s][:, 2, 0:8], one1.rearrange("p t e -> p e t"), AX.X, ALU.max))
                    dve.tensor_tensor(prim[:, :], prim[:, :], small[s][:, 2, 0:8], ALU.max)
                dve.tensor_tensor(one1, one1, each(small[s][:, 3, 0:4], NE), ALU.mult)
                st(dve.tensor_tensor(one2, one2, each(small[s][:, 4, 0:4], NE), ALU.mult))
                dve.tensor_tensor(weights, one1, one2, ALU.add).then_inc(g_done.sem, 1)

            with dve.Fori(0, passes) as n:
                st1 = lambda ins: dve1(dve, n, ins)
                for s in range(SLOTS):
                    for k, (bank, table) in enumerate(((0, "ck"), (1, "sk"), (2, "cq"), (3, "sq"))):
                        dve.wait_ge(a_qk_ps.sem, a_qk_ps.at(n, s, k + 1))
                        dve.tensor_tensor(seqs(P[s][:, k, :]), seqs(banks[s][bank][:, :]),
                                                          over(C(table), TB), ALU.mult).then_inc(a_qk_mul.sem, 1)
                for s in range(SLOTS):
                    dve.wait_ge(a_tanh.sem, a_tanh.at(n, s))
                    dve.scalar_tensor_tensor(sg[s], sg[s], 1.0, banks[s][1][:, :], ALU.add, ALU.mult).then_inc(a_gated.sem, 1)
                for s in range(SLOTS):
                    for i in range(4):
                        dve.wait_ge(a_st_ps.sem, a_st_ps.at(n, s, i + 1))
                        dve.tensor_tensor(seqs(P[s][:, i, :]), seqs(banks[s][i][:, :]),
                                                      over(C("decay")[:, 64 * i:64 * i + 64], TB), ALU.mult).then_inc(a_st.sem, 1)
                for s in range(SLOTS):
                    dve.wait_ge(a_y_ps.sem, a_y_ps.at(n, s))
                    y = banks[s][0][:, :].rearrange("p (g v) -> p g v", v=16)
                    ycv = yc[s].rearrange("p (g v) -> p g v", v=16)
                    st1(dve.tensor_reduce(gs[s][:, 0, :], y, AX.X, ALU.add))
                    st1(dve.tensor_scalar(gs[s][:, 1, :], gs[s][:, 0, :], 1.0 / 16, None, ALU.mult))
                    dve.tensor_tensor(ycv, y, each(gs[s][:, 1, :], 16), ALU.subtract).then_inc(a_y_cent.sem, 1)
                for s in range(SLOTS):
                    dve.wait_ge(a_y_sq.sem, a_y_sq.at(n, s))
                    dve.tensor_reduce(gs[s][:, 1, :], ysq[s].rearrange("p (g v) -> p g v", v=16),
                                                     AX.X, ALU.add).then_inc(a_y_var.sem, 1)
                for s in range(SLOTS):
                    dve.wait_ge(a_y_rstd.sem, a_y_rstd.at(n, s))
                    ycv = yc[s].rearrange("p (g v) -> p g v", v=16)
                    dve.tensor_tensor(ycv, ycv, each(gs[s][:, 3, :], 16), ALU.mult).then_inc(a_y_norm.sem, 1)
                for s in range(SLOTS):
                    dve.wait_ge(a_y_aff.sem, a_y_aff.at(n, s))
                    dve.scalar_tensor_tensor(yc[s], sg[s], 0.5, yc[s], ALU.mult, ALU.mult).then_inc(a_h.sem, 1)
                for s in range(SLOTS):
                    dve.wait_ge(a_o_ps.sem, a_o_ps.at(n, s))
                    st1(dve.tensor_tensor(R[s][:, :, :], tok(banks[s][2][:, :]), X[s][:, :, :], ALU.add))
                    norm(n, s, 0, a_ln_mv, a_ln_rstd, dve1, a_x)
                for s in range(SLOTS):
                    dve.wait_ge(a_kv_ps.sem, a_kv_ps.at(n, s, 1))
                    dve.scalar_tensor_tensor(KT[s], banks[s][2][:, :], Col("xbk"), maskr[s],
                                                         ALU.add, ALU.mult).then_inc(a_kT.sem, 1)
                    dve.wait_ge(a_kv_ps.sem, a_kv_ps.at(n, s, 2))
                    st1(dve.tensor_tensor(tok(tmpa[s]), tok(banks[s][3][:, :]), over(Row("xbv"), T), ALU.add))
                    for b in range(2):
                        h = slice(64 * b, 64 * b + 64)
                        for t in range(T):
                            last = dve.tensor_scalar(
                                xv[s][h, t, :, b, 0:32], tmpa[s][h, 128 * t:128 * t + 128].rearrange("p (i c) -> p i c", c=32),
                                maskc[s][h, t:t + 1], None, ALU.mult)
                    last.then_inc(a_v.sem, 1)
                for s in range(SLOTS):
                    dve.wait_ge(a_kv_ps.sem, a_kv_ps.at(n, s, 3))
                    dve.scalar_tensor_tensor(QT[s], banks[s][1][:, :], Col("xbt"), maskr[s],
                                                        ALU.add, ALU.mult).then_inc(a_q.sem, 1)
                for s in range(SLOTS):
                    dve.wait_ge(a_bias.sem, a_bias.at(n, s))
                    for i in range(4):
                        dve.wait_ge(a_s_ps.sem, a_s_ps.at(n, s, i + 1))
                        st1(dve.scalar_tensor_tensor(P[s][:, i, :], banks[s][i][:, :], 0.25, maskb[s], ALU.mult, ALU.add))
                        st1(dve.tensor_reduce(gs[s][:, 0, 8 * i:8 * i + 8], seqs(P[s][:, i, :]), AX.X, ALU.max))
                        dve.tensor_tensor(seqs(P[s][:, i, :]), seqs(P[s][:, i, :]),
                                                         each(gs[s][:, 0, 8 * i:8 * i + 8], SEQ), ALU.subtract).then_inc(a_s_sub.sem, 1)
                for s in range(SLOTS):
                    for t in range(T):
                        dve.wait_ge(a_r_ps.sem, a_r_ps.at(n, s, t + 1))
                        rv = banks[s][t][:, 0:264].rearrange("p (b i c) -> p b i c", b=2, i=4)
                        rc = gs[s][:, 1, 8 * t:8 * t + 8]
                        st1(dve.reciprocal(rc.rearrange("p (b i) -> p b i", b=2), rv[:, :, :, 32]))
                        for r in range(2):
                            h = slice(64 * r, 64 * r + 64)
                            last = dve.tensor_tensor(
                                O[s][h, 2 * t:2 * t + 2, :].rearrange("p b (i v) -> p (b i) v", v=16),
                                banks[s][t][h, 0:264].rearrange("p (g c) -> p g c", c=33)[:, :, 16 * r:16 * r + 16],
                                each(rc[h, :], 16), ALU.mult)
                    last.then_inc(a_r.sem, 1)
                for s in range(SLOTS):
                    dve.wait_ge(a_o2_ps.sem, a_o2_ps.at(n, s))
                    st1(dve.tensor_tensor(R[s][:, :, :], tok(banks[s][2][:, :]), X[s][:, :, :], ALU.add))
                    st1(dve.tensor_tensor(R[s][:, :, :], R[s][:, :, :], over(Row("xbo"), T), ALU.add))
                    norm(n, s, 1, a_ln_mv, a_ln_rstd, dve1, a_x)
                for s in range(SLOTS):
                    dve.wait_ge(a_g_ps.sem, a_g_ps.at(n, s))
                    lg = small[s][:, 3, :].rearrange("p (t e) -> p t e", t=T)
                    st1(dve.tensor_copy(lg, banks[s][0][:, 0:T * NE].rearrange("p (t e) -> p t e", t=T)))
                    choose(n, s, a_g_diff, a_g_exp, a_g_done, dve1, lg, wt_all[:, bass.ds((n * SLOTS + s) * T, T), :], True)

            for s in range(SLOTS):
                dve.wait_ge(a_g_done.sem, a_g_done.at(passes - 1, s))
            dve.tensor_copy(prim[:, :], prim[:, :]).then_inc(s_prim, 1)
            dve.wait_ge(s_cnt, 1)
            mid = lambda ins: s_mid(dve, 0, ins)
            E = lambda k: emap[:, k, :]
            dve.tensor_scalar(E(0), banks[0][0][0:8, 0:8], 0.0, None, ALU.is_gt)
            mid(dve.tensor_scalar(E(1), banks[0][0][0:8, 8:16], 0.0, None, ALU.is_gt))
            mid(dve.tensor_tensor(E(2), W8p("sim"), E(0), ALU.mult))
            mid(dve.tensor_scalar(E(3), E(0), -NEG, NEG, ALU.mult, ALU.add))
            mid(dve.tensor_tensor(E(2), E(2), E(3), ALU.add))
            mid(dve.max(E(4), E(2)))
            mid(dve.max_index(eidx[:, :], E(4), E(2)))
            mid(dve.tensor_copy(E(5), eidx[:, :]))
            mid(dve.tensor_tensor(E(6), C("iota")[0:8, :], E(5)[:, 0:1].to_broadcast([8, 8]), ALU.is_equal))
            mid(dve.tensor_tensor(E(6), E(6), W8p("eye"), ALU.subtract))
            mid(dve.tensor_scalar(E(7), E(4), float(np.float32(0.7)), None, ALU.is_ge))
            mid(dve.tensor_scalar(E(8), E(1), -1.0, 1.0, ALU.mult, ALU.add))
            mid(dve.tensor_tensor(E(9), E(7)[:, 0:1].to_broadcast([8, 8]), E(8), ALU.mult))
            mid(dve.tensor_tensor(E(10), E(6), E(9), ALU.mult))
            dve.tensor_tensor(E(11), E(10), W8p("eye"), ALU.add).then_inc(s_map, 1)

            def combine(n, s, use, bank, done, src):
                for t in range(T):
                    last = dve.scalar_tensor_tensor(R[s][:, t, :], bank[:, 128 * t:128 * t + 128],
                                                    share[s][:, t, use:use + 1], src[:, t, :], ALU.mult, ALU.add)
                last.then_inc(done.sem, 1)

            def swiglu(n, s, e):
                dve.wait_ge(b_tanh.sem, b_tanh.at(n, s, use=e))
                st2(dve.scalar_tensor_tensor(P[s][:, 0, :], P[s][:, 0, :], 1.0, banks[s][0][:, :], ALU.add, ALU.mult))
                dve.wait_ge(b_up_ps.sem, b_up_ps.at(n, s, 2, use=e))
                dve.scalar_tensor_tensor(P[s][:, 1, :], P[s][:, 0, :], 0.5, banks[s][1][:, :],
                                                     ALU.mult, ALU.mult).then_inc(b_fh.sem, 1)

            def down(n, s, e):
                dve.wait_ge(b_down_ps.sem, b_down_ps.at(n, s, use=e))
                if e:
                    dve.wait_ge(b_comb.sem, b_comb.at(n, s, use=e - 1))
                combine(n, s, e, banks[s][2 + e % 2], b_comb, R[s] if e else X[s])

            def subtract_max(n, s, use, width):
                g = 512 // width
                for i in range(4):
                    dve.wait_ge(b_s_ps.sem, b_s_ps.at(n, s, i + 1, use=use))
                    v = banks[s][i][:, :].rearrange("p (g m) -> p g m", m=width)
                    mx = gs[s][:, 0, g * i:g * i + g]
                    st2(dve.tensor_reduce(mx, v, AX.X, ALU.max))
                    dve.tensor_tensor(P[s][:, i, :].rearrange("p (g m) -> p g m", m=width), v,
                                                     each(mx, width), ALU.subtract).then_inc(b_s_sub.sem, 1)

            def project_add(n, s, use, bank, row, norm_use):
                dve.wait_ge(b_o_ps.sem, b_o_ps.at(n, s, use=use))
                st2(dve.tensor_tensor(R[s][:, :, :], tok(bank[:, :]), X[s][:, :, :], ALU.add))
                st2(dve.tensor_tensor(R[s][:, :, :], R[s][:, :, :], over(Row(row), T), ALU.add))

            with dve.Fori(0, passes) as n:
                st2 = lambda ins: dve2(dve, n, ins)
                for s in range(SLOTS):
                    dve.wait_ge(b_share_ps.sem, b_share_ps.at(n, s))
                    dve.tensor_copy(share[s], banks[s][2][:, 0:T * NE].rearrange("p (t e) -> p t e", t=T)).then_inc(b_share.sem, 1)
                    dve.wait_ge(b_share.sem, b_share.at(n, s))
                swiglu(n, 0, 0)
                for e in range(NE):
                    if e:
                        down(n, 1, e - 1)
                    swiglu(n, 1, e)
                    down(n, 0, e)
                    if e < NE - 1:
                        swiglu(n, 0, e + 1)
                down(n, 1, NE - 1)
                for s in range(SLOTS):
                    dve.wait_ge(b_comb.sem, b_comb.at(n, s, use=NE - 1))
                    norm(n, s, 0, b_ln_mv, b_ln_rstd, dve2, b_x)
                for r in range(2):
                    for s in range(SLOTS):
                        dve.wait_ge(s_q2, SLOTS * n + SLOTS)
                        for c in (1, 3):
                            dve.wait_ge(b_aq_ps.sem, b_aq_ps.at(n, s, c + 1, use=r))
                            for q in range(2):
                                h = slice(64 * q, 64 * q + 64)
                                last = dve.tensor_scalar(qdiag[s][h, c, :, q, :], seqs(banks[s][c][h, :]),
                                                         Col("abq", 4 * r + c)[h, :], None, ALU.add)
                            last.then_inc(b_aq_v.sem, 1)
                    for s in range(SLOTS):
                        for t in range(T):
                            dve.wait_ge(b_av_ps.sem, b_av_ps.at(n, s, t + 1, use=r))
                            dve.tensor_tensor(va[s][:, t, :], banks[s][t][:, :],
                                                          Row("abv")[:, 512 * r:512 * r + 512], ALU.add).then_inc(b_av.sem, 1)
                    for s in range(SLOTS):
                        for c in range(4):
                            dve.wait_ge(b_as_ps.sem, b_as_ps.at(n, s, c + 1, use=r))
                            mx = gs[s][:, 0, 8 * c:8 * c + 8]
                            st2(dve.tensor_reduce(mx, seqs(banks[s][c][:, :]), AX.X, ALU.max))
                            dve.tensor_tensor(seqs(P[s][:, c, :]), seqs(banks[s][c][:, :]),
                                                              each(mx, SEQ), ALU.subtract).then_inc(b_as_sub.sem, 1)
                    for s in range(SLOTS):
                        for c in range(4):
                            dve.wait_ge(b_ap.sem, b_ap.at(n, s, c + 1, use=r))
                            sm = gs[s][:, 1, 8 * c:8 * c + 8]
                            st2(dve.tensor_reduce(sm, seqs(P[s][:, c, :]), AX.X, ALU.add))
                            dve.reciprocal(gs[s][:, 2, 8 * c:8 * c + 8], sm).then_inc(b_arc.sem, 1)
                    for s in range(SLOTS):
                        dve.wait_ge(b_out_ps.sem, b_out_ps.at(n, s, use=r))
                        if r == 0:
                            st2(dve.tensor_tensor(R[s][:, :, :], tok(banks[s][0][:, :]), X[s][:, :, :], ALU.add))
                            dve.tensor_tensor(R[s][:, :, :], R[s][:, :, :], over(Row("abo"), T), ALU.add).then_inc(b_out.sem, 1)
                        else:
                            dve.wait_ge(b_out.sem, b_out.at(n, s, use=0))
                            dve.tensor_tensor(R[s][:, :, :], tok(banks[s][0][:, :]), R[s][:, :, :], ALU.add).then_inc(b_out.sem, 1)
                for s in range(SLOTS):
                    dve.wait_ge(b_out.sem, b_out.at(n, s, use=1))
                    norm(n, s, 1, b_ln_mv, b_ln_rstd, dve2, b_x)
                for s in range(SLOTS):
                    dve.wait_ge(b_cqk_ps.sem, b_cqk_ps.at(n, s, 2))
                    dve.tensor_copy(kcat[s][:, :, SEQ:128], seqs(banks[s][1][:, :])).then_inc(b_ck.sem, 1)
                    for k in range(2):
                        dve.wait_ge(b_cv_ps.sem, b_cv_ps.at(n, s, k + 1))
                        last = dve.tensor_copy(vcat[s][64:128, 4 * k:4 * k + 4, :, 0:16],
                                               banks[s][2 + k][64:128, :].rearrange("p (b g v) -> p b g v", b=4, v=16))
                    last.then_inc(b_cv.sem, 1)
                for t in range(T):
                    for s in range(SLOTS):
                        subtract_max(n, s, t, 128)
                    for s in range(SLOTS):
                        dve.wait_ge(b_r_ps.sem, b_r_ps.at(n, s, use=t))
                        rv = banks[s][0][:, 0:272].rearrange("p (g c) -> p g c", c=17)
                        rc = gs[s][:, 1, 0:16]
                        st2(dve.reciprocal(rc, rv[:, :, 16]))
                        for r in range(2):
                            h = slice(64 * r, 64 * r + 64)
                            last = dve.tensor_tensor(
                                O[s][h, 2 * t:2 * t + 2, :].rearrange("p b (g v) -> p (b g) v", v=8),
                                rv[h, :, 8 * r:8 * r + 8], each(rc[h, :], 8), ALU.mult)
                        last.then_inc(b_r.sem, 1)
                for s in range(SLOTS):
                    project_add(n, s, 0, banks[s][3], "pb", 2)
                    norm(n, s, 2, b_ln_mv, b_ln_rstd, dve2, b_x)
                for s in range(SLOTS):
                    for k, (bias, table) in enumerate((("fbq", "cos"), ("fbqs", "sin"), ("fbk", "cos"), ("fbks", "sin"))):
                        dve.wait_ge(b_fqk_ps.sem, b_fqk_ps.at(n, s, k + 1))
                        dve.scalar_tensor_tensor(seqs(P[s][:, k, :]), seqs(banks[s][k][:, :]), Col(bias),
                                                               over(C(table), TB), ALU.add, ALU.mult).then_inc(b_frot.sem, 1)
                for s in range(SLOTS):
                    dve.wait_ge(b_fzero.sem, b_fzero.at(n, s))
                    dve.wait_ge(b_fv_ps.sem, b_fv_ps.at(n, s))
                    for b in range(2):
                        h = slice(64 * b, 64 * b + 64)
                        last = dve.tensor_tensor(
                            vf[s][h, :, :, b, 0:16], banks[s][0][h, :].rearrange("p (t g v) -> p t g v", t=T, v=16),
                            over(Row("fbv")[h, :], T).rearrange("p t (g v) -> p t g v", v=16), ALU.add)
                    last.then_inc(b_fv.sem, 1)
                for jh in range(2):
                    for s in range(SLOTS):
                        subtract_max(n, s, 4 + jh, SEQ)
                    for s in range(SLOTS):
                        dve.wait_ge(b_r_ps.sem, b_r_ps.at(n, s, use=4 + jh))
                        for k in range(2):
                            rv = banks[s][k][:, 0:272].rearrange("p (g c) -> p g c", c=17)
                            rc = gs[s][:, 1, 16 * k:16 * k + 16]
                            st2(dve.reciprocal(rc, rv[:, :, 16]))
                            for r in range(2):
                                h = slice(64 * r, 64 * r + 64)
                                last = dve.tensor_tensor(
                                    O[s][h, 4 * k:4 * k + 4, :].rearrange("p b (i c) -> p (b i) c", i=4)[:, :, 8 * jh:8 * jh + 8],
                                    rv[h, :, 8 * r:8 * r + 8], each(rc[h, :], 8), ALU.mult)
                        last.then_inc(b_r.sem, 1)
                for s in range(SLOTS):
                    project_add(n, s, 1, banks[s][1], "fbo", 3)
                    norm(n, s, 3, b_ln_mv, b_ln_rstd, dve2, b_ln_x1, X1[s])
                for s in range(SLOTS):
                    dve.wait_ge(b_g_ps.sem, b_g_ps.at(n, s))
                    lg = small[s][:, 3, :].rearrange("p (t e) -> p t e", t=T)
                    st2(dve.tensor_tensor(lg, banks[s][0][:, 0:T * NE].rearrange("p (t e) -> p t e", t=T),
                                          over(Row("bg"), T), ALU.add))
                    choose(n, s, b_g_diff, b_g_exp, b_g_done, dve2, lg, share[s], False)
                    dve.wait_ge(b_g_done.sem, b_g_done.at(n, s))
                for s in range(SLOTS):
                    dve.wait_ge(b_b2_ps.sem, b_b2_ps.at(n, s))
                    dve.tensor_tensor(R[s][:, :, :], tok(banks[s][2][:, :]), X1[s][:, :, :], ALU.add).then_inc(b_b2.sem, 1)

                def moe_down(s, e):
                    dve.wait_ge(b_mdown_ps.sem, b_mdown_ps.at(n, s, use=e))
                    if e:
                        dve.wait_ge(b_mcomb.sem, b_mcomb.at(n, s, use=e - 1))
                    else:
                        dve.wait_ge(b_b2.sem, b_b2.at(n, s))
                    combine(n, s, e, banks[s][3], b_mcomb, R[s])

                for e in range(NE):
                    for s in range(SLOTS):
                        moe_down(s, e)
                for s in range(SLOTS):
                    dve.wait_ge(b_mcomb.sem, b_mcomb.at(n, s, use=NE - 1))
                    norm(n, s, 4, b_ln_mv, b_ln_rstd, dve2, b_ln_x1, X1[s])
                for s in range(SLOTS):
                    dve.wait_ge(b_r2.sem, b_r2.at(n, s))
                    norm(n, s, 5, b_ln_mv, b_ln_rstd, dve2, b_x)

        @block.tensor
        def _(pe):
            pe.wait_ge(s_init, 2)
            pe.wait_ge(s_const, 16 * 7)
            mm = pe.matmul

            def turn_state(n, s, use, bank, src):
                pe.wait_ge(a_x.sem, a_x.at(n, s, use=use))
                for t in range(T):
                    last = pe.transpose(bank[:, 128 * t:128 * t + 128], src[:, t, :], ident)
                last.then_inc(a_x_ps.sem, 1)

            with pe.Fori(0, passes) as n:
                for s in range(SLOTS):
                    pe.wait_ge(loaded[s], 16 * 6 * (n + 1))
                    for k, w in enumerate(("wk", "wks", "wq", "wqs")):
                        mm(banks[s][k][:, :], A(w), XT[s][:, :], start=True, stop=True).then_inc(a_qk_ps.sem, 1)
                for s in range(SLOTS):
                    pe.wait_ge(a_qk_mul.sem, a_qk_mul.at(n, s))
                    for b in range(TB):
                        for r in range(2):
                            last = mm(banks[s][0][64 * r:64 * r + 64, 64 * b:64 * b + 64], XT[s][:, 64 * b:64 * b + 64],
                                      A("wv")[:, 64 * r:64 * r + 64], start=True, stop=True)
                    last.then_inc(a_vg_ps.sem, 1)
                    for t in range(T):
                        last = mm(banks[s][1][:, 128 * t:128 * t + 128], XT[s][:, 128 * t:128 * t + 128], A("wg"),
                                  start=True, stop=True)
                    last.then_inc(a_vg_ps.sem, 1)
                for s in range(SLOTS):
                    pe.wait_ge(a_k_pair.sem, a_k_pair.at(n, s))
                    pe.wait_ge(a_k_sum.sem, a_k_sum.at(n, s))
                    pe.wait_ge(a_v_diag.sem, a_v_diag.at(n, s))
                    pe.wait_ge(a_gated.sem, a_gated.at(n, s))
                    for i in range(4):
                        h = slice(32 * i, 32 * i + 32)
                        for b in range(TB):
                            last = mm(banks[s][i][:, 64 * b:64 * b + 64], pair[s][h, b, :, :],
                                      QT[s][h, 64 * b:64 * b + 64], start=True, stop=True)
                        last.then_inc(a_st_ps.sem, 1)
                for s in range(SLOTS):
                    pe.wait_ge(a_st.sem, a_st.at(n, s))
                    for i in range(4):
                        for b in range(TB):
                            o = (b // 2) * 128 + 32 * i
                            last = mm(banks[s][0][64 * (b % 2):64 * (b % 2) + 64, o:o + 32],
                                      P[s][:, i, 64 * b:64 * b + 64], vdiag[s][:, b, i, :], start=True, stop=True)
                    last.then_inc(a_y_ps.sem, 1)
                for s in range(SLOTS):
                    pe.wait_ge(a_h.sem, a_h.at(n, s))
                    for t in range(T):
                        last = pe.transpose(banks[s][1][:, 128 * t:128 * t + 128], yc[s][:, 128 * t:128 * t + 128], ident)
                    last.then_inc(a_h_ps.sem, 1)
                for s in range(SLOTS):
                    pe.wait_ge(a_hT.sem, a_hT.at(n, s))
                    for t in range(T):
                        last = mm(banks[s][2][:, 128 * t:128 * t + 128], hT[s][:, 128 * t:128 * t + 128], A("wo"),
                                  start=True, stop=True)
                    last.then_inc(a_o_ps.sem, 1)
                for s in range(SLOTS):
                    pe.wait_ge(a_x.sem, a_x.at(n, s, use=0))
                    for c in range(2):
                        last = mm(banks[s][2][:, :], A("xk")[:, 128 * c:128 * c + 128], ctxT[s][:, c, :],
                                  start=c == 0, stop=c == 1)
                    last.then_inc(a_kv_ps.sem, 1)
                    for t in range(T):
                        for c in range(2):
                            last = mm(banks[s][3][:, 128 * t:128 * t + 128], ctxT[s][:, c, 128 * t:128 * t + 128],
                                      A("xv")[:, 128 * c:128 * c + 128], start=c == 0, stop=c == 1)
                    last.then_inc(a_kv_ps.sem, 1)
                    turn_state(n, s, 0, banks[s][0], X[s])
                for s in range(SLOTS):
                    pe.wait_ge(a_xT.sem, a_xT.at(n, s, use=0))
                    mm(banks[s][1][:, :], A("xq"), XT[s][:, :], start=True, stop=True).then_inc(a_kv_ps.sem, 1)
                for s in range(SLOTS):
                    pe.wait_ge(a_kT.sem, a_kT.at(n, s))
                    pe.wait_ge(a_v.sem, a_v.at(n, s))
                    pe.wait_ge(a_q_pair.sem, a_q_pair.at(n, s))
                    for i in range(4):
                        h = slice(32 * i, 32 * i + 32)
                        for b in range(TB):
                            last = mm(banks[s][i][:, 64 * b:64 * b + 64], pair[s][h, b, :, :],
                                      KT[s][h, 64 * b:64 * b + 64], start=True, stop=True)
                        last.then_inc(a_s_ps.sem, 1)
                for s in range(SLOTS):
                    for i in range(4):
                        pe.wait_ge(a_p.sem, a_p.at(n, s, i + 1))
                        for t in range(T):
                            last = pe.transpose(banks[s][i][:, 128 * t:128 * t + 128], P[s][:, i, 128 * t:128 * t + 128], ident)
                        last.then_inc(a_p_ps.sem, 1)
                for s in range(SLOTS):
                    pe.wait_ge(a_pT.sem, a_pT.at(n, s))
                    for t in range(T):
                        rv = banks[s][t][:, 0:264].rearrange("p (b i c) -> p b i c", b=2, i=4)
                        for i in range(4):
                            last = mm(rv[:, :, i, :], PT[s][:, i, 128 * t:128 * t + 128], xv[s][:, t, i, :, :],
                                      start=True, stop=True)
                        last.then_inc(a_r_ps.sem, 1)
                for s in range(SLOTS):
                    pe.wait_ge(a_r.sem, a_r.at(n, s))
                    apart(pe)
                    for k in range(2):
                        for b in range(4):
                            last = pe.transpose(banks[s][k][0:64, 128 * b:128 * b + 128], O[s][:, 4 * k + b, :], ident)
                        last.then_inc(a_rt_ps.sem, 1)
                for s in range(SLOTS):
                    pe.wait_ge(a_rT.sem, a_rT.at(n, s))
                    for t in range(T):
                        o = banks[s][2][:, 128 * t:128 * t + 128]
                        mm(o, XT[s][:, 128 * t:128 * t + 128], A("xo"), start=True, stop=False)
                        for r in range(2):
                            last = mm(o, OT2[s][:, r, 128 * t:128 * t + 128], Wp("xo", r), start=False, stop=r == 1)
                    last.then_inc(a_o2_ps.sem, 1)
                for s in range(SLOTS):
                    turn_state(n, s, 1, banks[s][3], X[s])
                for s in range(SLOTS):
                    pe.wait_ge(a_xT.sem, a_xT.at(n, s, use=1))
                    for t in range(T):
                        last = mm(banks[s][0][:, NE * t:NE * t + NE], XT[s][:, 128 * t:128 * t + 128], A("gate"),
                                  start=True, stop=True)
                    last.then_inc(a_g_ps.sem, 1)

            pe.wait_ge(s_prim, 1)
            mm(banks[0][0][0:8, 0:8], C("ones"), prim[:, :], start=True, stop=True)
            mm(banks[0][0][0:8, 8:16], prim[:, :], C("ones"), start=True, stop=True).then_inc(s_cnt, 1)
            pe.wait_ge(s_map, 1)

            def tile(ap, t):
                return ap[:, 128 * t:128 * t + 128]

            def turn(n, use, bank, src, ready, ready_use):
                for s in range(SLOTS):
                    if ready is None:
                        pe.wait_ge(reloaded[s], 16 * n + 16)
                    else:
                        pe.wait_ge(ready.sem, ready.at(n, s, use=ready_use))
                    for t in range(T):
                        last = pe.transpose(tile(banks[s][bank], t), src[s][:, t, :], ident)
                    last.then_inc(b_x_ps.sem, 1)

            def turn_weights(n, s, src):
                for t in range(T):
                    last = pe.transpose(banks[s][1][0:8, 128 * t:128 * t + 128], src[:, t, :], ident)
                last.then_inc(b_wt_ps.sem, 1)

            def turn_probs(n, use):
                for s in range(SLOTS):
                    for i in range(4):
                        pe.wait_ge(b_p.sem, b_p.at(n, s, i + 1, use=use))
                        for t in range(T):
                            last = pe.transpose(tile(banks[s][i], t), tile(P[s][:, i, :], t), ident)
                        last.then_inc(b_p_ps.sem, 1)

            def turn_results(n, s, base, use):
                for k in range(2):
                    for b in range(4):
                        last = pe.transpose(banks[s][base + k][0:64, 128 * b:128 * b + 128], O[s][:, 4 * k + b, :], ident)
                    last.then_inc(b_rt_ps.sem, 1)

            def out_project(n, s, w, bank, use):
                pe.wait_ge(b_rT.sem, b_rT.at(n, s, use=use))
                for t in range(T):
                    for r in range(2):
                        last = mm(tile(bank, t), tile(OT2[s][:, r, :], t), Wp(w, r), start=r == 0, stop=r == 1)
                last.then_inc(b_o_ps.sem, 1)

            with pe.Fori(0, passes) as n:
                turn(n, 0, 0, X, None, 0)
                for s in range(SLOTS):
                    pe.wait_ge(b_wts.sem, b_wts.at(n, s))
                    apart(pe)
                    turn_weights(n, s, wts[s])
                for s in range(SLOTS):
                    pe.wait_ge(b_wtT.sem, b_wtT.at(n, s, use=0))
                    for t in range(T):
                        last = mm(banks[s][2][:, NE * t:NE * t + NE], tile(wtT[s], t), emap[:, 11, :], start=True, stop=True)
                    last.then_inc(b_share_ps.sem, 1)

                def up0(s, e):
                    if e:
                        pe.wait_ge(b_fh.sem, b_fh.at(n, s, use=e - 1))
                    else:
                        pe.wait_ge(b_xT.sem, b_xT.at(n, s, use=0))
                    for k in range(2):
                        o = 256 * e + 128 * k
                        mm(banks[s][k][:, :], B("gu")[:, o:o + 128], XT[s][:, :], start=True, stop=True).then_inc(b_up_ps.sem, 1)

                def down0(s, e):
                    pe.wait_ge(b_fh.sem, b_fh.at(n, s, use=e))
                    if e >= 2:
                        pe.wait_ge(b_comb.sem, b_comb.at(n, s, use=e - 2))
                    else:
                        pe.wait_ge(b_share.sem, b_share.at(n, s))
                    for t in range(T):
                        last = mm(tile(banks[s][2 + e % 2], t), tile(P[s][:, 1, :], t), B("down")[:, 128 * e:128 * e + 128],
                                  start=True, stop=True)
                    last.then_inc(b_down_ps.sem, 1)

                up0(0, 0)
                for e in range(NE):
                    if e:
                        down0(1, e - 1)
                    up0(1, e)
                    down0(0, e)
                    if e < NE - 1:
                        up0(0, e + 1)
                down0(1, NE - 1)

                turn(n, 1, 0, X, b_x, 0)
                for r in range(2):
                    for s in range(SLOTS):
                        if r == 0:
                            pe.wait_ge(b_xT.sem, b_xT.at(n, s, use=1))
                        else:
                            pe.wait_ge(b_out.sem, b_out.at(n, s, use=0))
                        for c in range(4):
                            o = 128 * (4 * r + c)
                            mm(banks[s][c][:, :], B("aq")[:, o:o + 128], XT[s][:, :], start=True, stop=True).then_inc(b_aq_ps.sem, 1)
                    for s in range(SLOTS):
                        for c in range(4):
                            o = 128 * (4 * r + c)
                            if c % 2:
                                pe.wait_ge(b_aq_v.sem, b_aq_v.at(n, s, c // 2 + 1, use=r))
                            else:
                                pe.wait_ge(b_aq_a.sem, b_aq_a.at(n, s, c // 2 + 1, use=r))
                            mm(banks[s][c][:, :], B("ak")[:, o:o + 128], XT[s][:, :], start=True, stop=True).then_inc(b_ak_ps.sem, 1)
                    for s in range(SLOTS):
                        for t in range(T):
                            pe.wait_ge(b_ak.sem, b_ak.at(n, s, t + 1, use=r))
                            mm(banks[s][t][:, :], tile(XT[s], t), B("av")[:, 512 * r:512 * r + 512],
                                              start=True, stop=True).then_inc(b_av_ps.sem, 1)
                    for s in range(SLOTS):
                        for c in range(4):
                            pe.wait_ge(b_av.sem, b_av.at(n, s, c + 1, use=r))
                            for b in range(TB):
                                last = mm(banks[s][c][:, 64 * b:64 * b + 64], qdiag[s][:, c, b, :, :],
                                          kc[s][:, c, 64 * b:64 * b + 64], start=True, stop=True)
                            last.then_inc(b_as_ps.sem, 1)
                    for s in range(SLOTS):
                        for c in range(4):
                            pe.wait_ge(b_an.sem, b_an.at(n, s, c + 1, use=r))
                            for t in range(T):
                                last = pe.transpose(tile(banks[s][c], t), tile(P[s][:, c, :], t), ident)
                            last.then_inc(b_ap_ps.sem, 1)
                    for s in range(SLOTS):
                        pe.wait_ge(b_apT.sem, b_apT.at(n, s, use=r))
                        apart(pe)
                        for b in range(2):
                            h = slice(64 * b, 64 * b + 64)
                            for half in range(2):
                                for c in range(2):
                                    for t in range(T):
                                        for q in range(2):
                                            o = 64 * (2 * (2 * half + c) + q)
                                            last = mm(banks[s][2 * b + half][64 * q:64 * q + 64,
                                                                             256 * c + 64 * t:256 * c + 64 * t + 64],
                                                      va[s][h, t, o:o + 64],
                                                      PT[s][h, 2 * half + c, 128 * t + 64 * q:128 * t + 64 * q + 64],
                                                      start=True, stop=True)
                                last.then_inc(b_ao_ps.sem, 1)
                    for s in range(SLOTS):
                        pe.wait_ge(b_aoT.sem, b_aoT.at(n, s, use=r))
                        for t in range(T):
                            for c in range(4):
                                o = 128 * (4 * r + c)
                                last = mm(tile(banks[s][0], t), tile(P[s][:, c, :], t), B("ao")[:, o:o + 128],
                                          start=c == 0, stop=c == 3)
                        last.then_inc(b_out_ps.sem, 1)

                turn(n, 2, 0, X, b_x, 1)
                for s in range(SLOTS):
                    pe.wait_ge(b_xT.sem, b_xT.at(n, s, use=2))
                    for k, w in enumerate(("cq", "ck")):
                        mm(banks[s][k][:, :], B(w), XT[s][:, :], start=True, stop=True).then_inc(b_cqk_ps.sem, 1)
                    for k in range(2):
                        for b in range(4):
                            last = mm(banks[s][2 + k][64:128, 128 * b:128 * b + 128],
                                      XT[s][:, 64 * (4 * k + b):64 * (4 * k + b) + 64], B("cv"), start=True, stop=True)
                        last.then_inc(b_cv_ps.sem, 1)
                for t in range(T):
                    for s in range(SLOTS):
                        if t == 0:
                            pe.wait_ge(b_cq.sem, b_cq.at(n, s))
                            pe.wait_ge(b_ck.sem, b_ck.at(n, s))
                            pe.wait_ge(b_cv.sem, b_cv.at(n, s))
                            pe.wait_ge(b_cones.sem, b_cones.at(n, s))
                            pe.wait_ge(context[s], 16 * 9 * (n + 1))
                        else:
                            pe.wait_ge(b_r.sem, b_r.at(n, s, use=t - 1))
                        for i in range(4):
                            h = slice(32 * i, 32 * i + 32)
                            for b in range(2):
                                for j in range(2):
                                    last = mm(tile(banks[s][i], 2 * b + j), q4[0][s][h, 2 * t + b, 2 * j:2 * j + 2, :],
                                              kcat[s][h, 2 * t + b, :], start=True, stop=True)
                            last.then_inc(b_s_ps.sem, 1)
                    turn_probs(n, t)
                    for s in range(SLOTS):
                        pe.wait_ge(b_pT.sem, b_pT.at(n, s, use=t))
                        for i in range(4):
                            for b in range(2):
                                for j in range(2):
                                    o = 17 * (8 * b + 2 * i + j)
                                    last = mm(banks[s][0][:, o:o + 17], tile(PT[s][:, i, :], 2 * b + j),
                                              vcat[s][:, 2 * t + b, 2 * i + j, :], start=True, stop=True)
                        last.then_inc(b_r_ps.sem, 1)
                for s in range(SLOTS):
                    pe.wait_ge(b_r.sem, b_r.at(n, s, use=3))
                    apart(pe)
                    turn_results(n, s, 1, 0)
                for s in range(SLOTS):
                    out_project(n, s, "x1", banks[s][3], 0)

                turn(n, 3, 0, X, b_x, 2)
                for s in range(SLOTS):
                    pe.wait_ge(b_xT.sem, b_xT.at(n, s, use=3))
                    for k, w in enumerate(("fq", "fqs", "fk", "fks")):
                        mm(banks[s][k][:, :], B(w), XT[s][:, :], start=True, stop=True).then_inc(b_fqk_ps.sem, 1)
                for s in range(SLOTS):
                    pe.wait_ge(b_frot.sem, b_frot.at(n, s, 1))
                    for t in range(T):
                        last = mm(tile(banks[s][0], t), tile(XT[s], t), B("fv"), start=True, stop=True)
                    last.then_inc(b_fv_ps.sem, 1)
                for jh in range(2):
                    for s in range(SLOTS):
                        if jh == 0:
                            pe.wait_ge(b_fsum.sem, b_fsum.at(n, s))
                            pe.wait_ge(b_fq.sem, b_fq.at(n, s))
                            pe.wait_ge(b_fv.sem, b_fv.at(n, s))
                        else:
                            pe.wait_ge(b_r.sem, b_r.at(n, s, use=4))
                        for i in range(4):
                            h = slice(32 * i, 32 * i + 32)
                            for b in range(TB):
                                last = mm(banks[s][i][:, 64 * b:64 * b + 64], q4[1][s][h, b, 2 * jh:2 * jh + 2, :],
                                          kf[s][h, 64 * b:64 * b + 64], start=True, stop=True)
                            last.then_inc(b_s_ps.sem, 1)
                    turn_probs(n, 4 + jh)
                    for s in range(SLOTS):
                        pe.wait_ge(b_pT.sem, b_pT.at(n, s, use=4 + jh))
                        for t in range(T):
                            rv = banks[s][t // 2][:, 0:272].rearrange("p (t b i c) -> p t b i c", t=2, b=2, i=4)
                            for i in range(4):
                                last = mm(rv[:, t % 2, :, i, :], tile(PT[s][:, i, :], t), vf[s][:, t, 2 * i + jh, :, :],
                                          start=True, stop=True)
                        last.then_inc(b_r_ps.sem, 1)
                for s in range(SLOTS):
                    pe.wait_ge(b_r.sem, b_r.at(n, s, use=5))
                    apart(pe)
                    turn_results(n, s, 2, 1)
                for s in range(SLOTS):
                    out_project(n, s, "fo", banks[s][1], 1)

                turn(n, 4, 3, X1, b_x1, 0)
                for s in range(SLOTS):
                    pe.wait_ge(b_xT.sem, b_xT.at(n, s, use=4))
                    for t in range(T):
                        last = mm(banks[s][0][:, NE * t:NE * t + NE], tile(XT[s], t), B("fg"), start=True, stop=True)
                    last.then_inc(b_g_ps.sem, 1)
                for s in range(SLOTS):
                    pe.wait_ge(b_g_done.sem, b_g_done.at(n, s))
                    apart(pe)
                    turn_weights(n, s, share[s])
                for s in range(SLOTS):
                    pe.wait_ge(b_wtT.sem, b_wtT.at(n, s, use=1))
                    for t in range(T):
                        last = mm(tile(banks[s][2], t), tile(wtT[s], t), W8p("b2"), start=True, stop=True)
                    last.then_inc(b_b2_ps.sem, 1)

                def up1(s, e):
                    if e == 0:
                        pe.wait_ge(b_b2.sem, b_b2.at(n, s))
                    if s == 0:
                        pe.wait_ge(w_loaded[e % 2], 32 * (n * (NE // 2) + e // 2 + 1))
                    for c in range(NC):
                        if c == 3:
                            pe.wait_ge(b_gelu.sem, b_gelu.at(n, s, 1, use=e))
                        mm(banks[s][c % 3][:, :], w1r[e % 2][:, 128 * c:128 * c + 128], XT[s][:, :],
                                           start=True, stop=True).then_inc(b_mup_ps.sem, 1)

                def down1(s, e):
                    pe.wait_ge(b_gelu.sem, b_gelu.at(n, s, use=e))
                    if e:
                        pe.wait_ge(b_mcomb.sem, b_mcomb.at(n, s, use=e - 1))
                    for t in range(T):
                        for c in range(NC):
                            last = mm(tile(banks[s][3], t), tile(PT[s][:, c, :], t), w2r[e % 2][:, c, :],
                                      start=c == 0, stop=c == NC - 1)
                    last.then_inc(b_mdown_ps.sem, 1)

                up1(0, 0)
                for e in range(NE):
                    if e:
                        down1(1, e - 1)
                    up1(1, e)
                    down1(0, e)
                    if e < NE - 1:
                        up1(0, e + 1)
                down1(1, NE - 1)

        for name, steps in (("dve1", dve1), ("act1", act1), ("pool1", pool1), ("dve2", dve2), ("pool2", pool2)):
            assert steps.k == steps.per_pass, (name, steps.k)


STEPS = dict(dve1=56, act1=0, pool1=8, dve2=148, pool2=20)


def tables():
    f = np.float32
    p = np.arange(128)
    pos = np.arange(SEQ, dtype=f)
    e = p % 16
    base = ((e // 2 * 2).astype(f) + f(0.4 * 16)) / f(1.4 * 16)
    scale = base[:, None] ** (pos[None, :] / f(512.0))
    ang = pos[None, :] * (f(1.0) / f(10000.0) ** ((e // 2).astype(f) / f(8)))[:, None]
    sign = np.where(e % 2 == 0, -1, 1).astype(f)[:, None]
    lo, hi = np.log(1.0 / 32.0), np.log(1.0 / 512.0)
    gam = f(1.0) - np.exp(np.linspace(lo, hi, 8)).astype(f)
    m, l = p % 64, np.arange(64)
    dec = np.zeros((128, 4, 64), f)
    for i in range(4):
        g = gam[2 * i + p // 64]
        expo = (l[None, :] - m[:, None]).astype(f)
        dec[:, i, :] = np.where(expo >= 0, np.exp(expo * np.log(g)[:, None]), 0)
    ang8 = pos[None, :] * (f(1.0) / f(10000.0) ** ((2 * (p % 4)).astype(f) / f(8)))[:, None]
    sign8 = np.where(p % 8 < 4, -1, 1).astype(f)[:, None]
    cols = [np.eye(128), np.cos(ang) * scale, sign * np.sin(ang) * scale, np.cos(ang) / scale,
            sign * np.sin(ang) / scale, dec.reshape(128, 256), np.cos(ang8), sign8 * np.sin(ang8),
            (p[:, None] // 16) % 2 == np.arange(2), (p[:, None] // 8) % 4 == np.arange(4),
            np.broadcast_to(np.arange(8), (128, 8)), np.ones((128, 8))]
    return np.concatenate([np.asarray(c, f) for c in cols], axis=1)


def lay_out(a):
    batch, seq, dim = a["x"].shape
    wide = lambda *parts: np.ascontiguousarray(np.concatenate([np.asarray(q).reshape(q.shape[0], -1) for q in parts], axis=1))
    swap16 = np.arange(128) ^ 1
    swap8 = np.arange(128) // 8 * 8 + (np.arange(128) + 4) % 8
    heads = lambda w: np.transpose(w, (1, 0, 2)).reshape(dim, dim)
    by_par = lambda w, v: w.reshape(128, -1, 2, v).transpose(0, 2, 1, 3)
    rows_par = lambda w, v: w.reshape(-1, 2, v, 128).transpose(0, 2, 1, 3)
    split_rows = lambda w, v: np.ascontiguousarray(rows_par(w, v)).reshape(64, 256)
    wq, wk, wv = heads(a["L0_attn_W_Q"]), heads(a["L0_attn_W_K"]), heads(a["L0_attn_W_V"])
    ws = a["L0_xattn_W_src"].T
    chunks = lambda w: w.reshape(-1, 128, w.shape[1]).transpose(1, 0, 2)
    wo = a["L0_xattn_W_out"].T
    qkv = a["L1_xattn_w_qkv"].T
    wa = wide(wq, wq[:, swap16], wk, wk[:, swap16], by_par(wv, 16), a["L0_attn_W_G"], a["L0_attn_W_O"],
              chunks(ws[:, :128]), chunks(ws[:, 128:]), a["L0_xattn_W_tgt"].T, wo[:128], a["L0_ffn_gate_weight"].T)
    w64 = wide(split_rows(wo[128:], 16), split_rows(a["L1_xattn_w_proj"].T, 8), split_rows(a["L1_ffn_Wo"], 8))
    rows = np.concatenate([a["L0_attn_gn_weight"], a["L0_attn_gn_bias"], a["L0_xattn_b_src"][128:], a["L0_xattn_b_out"],
                           a["L1_attn_bo"], a["L1_xattn_b_proj"], a["L1_ffn_bv"], a["L1_ffn_bo"], a["L1_ffn_g1"],
                           a["L1_ffn_be1"], a["L1_ffn_g2"], a["L1_ffn_be2"], a["L1_ffn_bg"], a["L1_attn_bv"]])
    col = lambda v: v.reshape(-1, 128).T
    cols = wide(col(a["L0_xattn_b_tgt"]), col(a["L0_xattn_b_src"][:128]), col(a["L1_attn_bq"]), col(a["L1_attn_bk"]),
                col(a["L1_ffn_bq"]), col(a["L1_ffn_bq"][swap8]), col(a["L1_ffn_bk"]), col(a["L1_ffn_bk"][swap8]),
                col(a["L1_ffn_b1"].reshape(-1)))
    fq, fk = a["L1_ffn_Wq"], a["L1_ffn_Wk"]
    wb = wide(a["L0_ffn_gate_up_proj"].transpose(2, 0, 1), a["L0_ffn_down_proj"].transpose(2, 0, 1),
              a["L1_attn_Wq"], a["L1_attn_Wk"], a["L1_attn_Wv"], chunks(a["L1_attn_Wo"]),
              qkv, fq, fq[:, swap8], fk, fk[:, swap8], a["L1_ffn_Wv"], a["L1_ffn_Wg"])
    w8 = wide(a["L0_ffn_similarity_matrix"], np.eye(8, dtype=np.float32), a["L1_ffn_b2"])
    x = a["x"].reshape(batch * seq, dim)
    c = a["ctx_2048"].reshape(batch * seq, CTX)
    return dict(x=x, xT=np.ascontiguousarray(x.T), ctx=c, ctxT=np.ascontiguousarray(c.T),
                mask=a["mask_BxS2_fk1"].reshape(-1), const=tables(), wa=wa, w64=w64, rows=rows, cols=cols, wb=wb,
                w8=w8, w1=a["L1_ffn_W1"], w2=a["L1_ffn_W2"])


def kernel(**inputs):
    import numpy as _np
    import concourse.bacc as _bacc
    from concourse.bass_utils import run_bass_kernel_spmd as _run

    a = {name: _np.asarray(v) for name, v in inputs.items()}
    shape = a["x"].shape
    arrays = {f"in_{k}": _np.ascontiguousarray(v) for k, v in lay_out(a).items()}
    nc = _bacc.Bacc("TRN2", target_bir_lowering=False, num_devices=1)
    d = {k[3:]: nc.dram_tensor(k, v.shape, F32, kind="ExternalInput").ap() for k, v in arrays.items()}
    n = shape[0] * shape[1]
    out = nc.dram_tensor("out", (n, shape[2]), F32, kind="ExternalOutput").ap()
    d["x_mid"] = nc.dram_tensor("x_mid", (n, shape[2]), F32, kind="Internal").ap()
    build(nc, d, out, n // NT)
    r = _run(nc, [arrays], core_ids=[0])
    return r.results[0]["out"].reshape(shape)
```

```python
from contextlib import ExitStack

import numpy as np

import concourse.bass as bass
from concourse import mybir

F32 = mybir.dt.float32
U32 = mybir.dt.uint32
ACT = mybir.ActivationFunctionType
ALU = mybir.AluOpType
AX = mybir.AxisListType

SEQ = 64
DIM = 128
CTX = 256
SLOTS = 2
TB = 8
T = 4
NT = TB * SEQ
NE = 8
FF = 512
NC = FF // 128
EPS = 1e-5
NEG = -1e30



def spans(*sizes):
    at, out = 0, {}
    for name, n in sizes:
        out[name] = (at, n)
        at += n
    return out, at


CONST, NCONST = spans(("ident", 128), ("cq", 64), ("sq", 64), ("ck", 64), ("sk", 64), ("decay", 256),
                      ("cos", 64), ("sin", 64), ("par", 2), ("quad", 4), ("iota", 8),
                      ("ones", 8))
WA, NWA = spans(("wq", 128), ("wqs", 128), ("wk", 128), ("wks", 128), ("wv", 128), ("wg", 128), ("wo", 128),
                ("xk", 256), ("xv", 256), ("xq", 128), ("xo", 128), ("gate", 8))
W64, NW64 = spans(("xo", 256), ("x1", 256), ("fo", 256))
ROWS, NROWS = spans(("gnw", 128), ("gnb", 128), ("xbv", 128), ("xbo", 128),
                    ("abo", 128), ("pb", 128), ("fbv", 128), ("fbo", 128), ("g1", 128), ("be1", 128),
                    ("g2", 128), ("be2", 128), ("bg", 8), ("abv", 1024))
COLS, NCOLS = spans(("xbt", 1), ("xbk", 1), ("abq", 8), ("abk", 8), ("fbq", 1), ("fbqs", 1), ("fbk", 1),
                    ("fbks", 1), ("b1", 32))
WB, NWB = spans(("gu", NE * 256), ("down", NE * 128), ("aq", 1024), ("ak", 1024), ("av", 1024), ("ao", 1024),
                ("cq", 128), ("ck", 128), ("cv", 128), ("fq", 128), ("fqs", 128), ("fk", 128), ("fks", 128),
                ("fv", 128), ("fg", 8))
W8, NW8 = spans(("sim", 8), ("eye", 8), ("b2", 128))


class Signal:

    def __init__(self, sem, each=1, uses=1):
        self.sem, self.each, self.uses = sem, each, uses

    def at(self, n, s, k=None, use=0):
        return n * (SLOTS * self.uses * self.each) + (s * self.uses + use) * self.each + (self.each if k is None else k)


class Steps:

    def __init__(self, sem):
        self.sem, self.base, self.k = sem, 0, 0

    def section(self, base):
        k, self.base, self.k = self.k, base, 0
        return k

    def __call__(self, eng, ins):
        self.k += 1
        ins.then_inc(self.sem, 1)
        eng.wait_ge(self.sem, self.base + self.k)


def part_of(stage, i):
    return f"{stage}.{i}" if i else stage


def stages(*names):
    split = [(name + "*1").split("*")[:2] for name in names]
    return [part_of(name, i) for name, parts in split for i in range(int(parts))]


A_FIRST = stages("qk*4", "vg", "st*4", "y", "yv", "yn", "yh", "h", "o", "on")
A_SECOND = stages("kv", "q", "s*4", "p*4", "r*4", "rt", "o2", "on", "x", "g", "gb")
B_FIRST = stages("in", "sh", *(f"{w}{e}" for e in range(NE) for w in ("up", "down")), "n0", "t1",
                 *(f"{w}{r}*4" for r in range(2) for w in ("aq", "ak", "av", "as", "am", "ap", "ao", "out")),
                 "n1", "t2", "cq", *(f"{w}{t}{k}" for t in range(T) for w, k in (("cs", "*4"), ("cp", "*4"), ("cr", ""))),
                 "crt", "co", "n2")
B_SECOND = stages("t3", "fq*4", "fv", *(f"{w}{j}{k}" for j in range(2) for w, k in (("fs", "*4"), ("fp", "*4"), ("fr", ""))),
                  "frt", "fo", "n3", "t4", "g", "gb", "wt", "b2",
                  *(f"{w}{e}*4" for e in range(NE) for w in ("mup", "md")), "n4", "n5s", "n5")
A_TURNS = (2, 2, 1, 2, 1, 1, 2, 4, 4, 1, 2, 1, 2, 1, 2, 2, 1, 1, 1, 1, 2)
B_TURNS = (0, 1, 1, 2, 1, 2, 3, 1, 1, 1, 1, 2, 1, 2, 1, 2, 4, 1, 1, 1, 1, 3, 2, 1, 1, 1, 1, 2, 2, 1, 1, 1, 1,
           1, 1, 3, 1, 1, 1, 3, 1, 5, 1, 3, 1, 2, 1, 2, 1, 2, 1, 1, 1, 1, 2, 1, 1, 2, 1, 1, 2, 2, 2, 7, 1, 1,
           1, 3, 1, 4, 5, 3, 3, 4, 3, 2, 2, 2, 2, 2, 1, 2, 5, 1, 4, 1, 5, 1, 2, 4, 2, 3, 1, 1, 2, 1, 2, 8, 1,
           1, 3, 1, 1, 7, 2, 1, 2, 4, 3, 1, 2, 4, 1, 1, 1, 2)


def alternate(second, first, turns):
    halves, order = [iter(second), iter(first)], []
    for k, count in enumerate(turns):
        order += [(k % 2, next(halves[k % 2])) for _ in range(count)]
    assert len(order) == len(second) + len(first)
    return order


def weave(order, *halves):
    halves = [iter(h) for h in halves]
    coming = [next(h, None) for h in halves]
    for who, name in order:
        if coming[who] == name:
            coming[who] = next(halves[who], None)
    assert coming == [None] * len(halves)


def passes_of(eng, passes, x, y, turns, first, second, steps, per_turn):
    only = lambda stages: [(0, name) for name in stages]
    together, last = alternate(y, x, turns), passes - 1
    if steps:
        steps.section(0)
    weave(only(x), first(0, 0))
    k = steps.section(0) if steps else 0
    with eng.Fori(0, last) as n:
        if steps:
            steps.section(n * per_turn + k)
        weave(together, second(n, 0, False), first(n, 1))
        weave(together, second(n, 1, False), first(n + 1, 0))
    if steps:
        turn = steps.section(last * per_turn + k)
        assert turn == per_turn, (steps.sem.name, turn)
    weave(together, second(last, 0, True), first(last, 1))
    weave(only(y), second(last, 1, True))


def apart(eng):
    eng.nop(nofuse=True)


def build(nc, d, out, groups):
    passes = groups // SLOTS
    ctx = ExitStack()
    with ctx:
        def sb(name, shape, dt=F32):
            return ctx.enter_context(nc.sbuf_tensor(name, shape, dt))

        def sem(name):
            return ctx.enter_context(nc.semaphore(name))

        def signal(name, each=1, uses=1):
            return Signal(sem(name), each, uses)

        const = sb("const", [128, NCONST])
        wa = sb("wa", [128, NWA])
        w64 = sb("w64", [64, NW64])
        rows = sb("rows", [128, NROWS])
        cols = sb("cols", [128, NCOLS])
        wb = sb("wb", [128, NWB])
        w8 = sb("w8", [8, NW8])

        def part(tensor, table, name, p=128):
            at, n = table[name]
            return tensor[0:p, at:at + n]

        def C(name): return part(const, CONST, name)
        def A(name): return part(wa, WA, name)
        def Wp(name, par): return part(w64, W64, name, 64)[:, par * 128:par * 128 + 128]
        def Row(name): return part(rows, ROWS, name)
        def Col(name, k=0): return part(cols, COLS, name)[:, k:k + 1]
        def B(name): return part(wb, WB, name)
        def W8p(name): return part(w8, W8, name, 8)
        ident = C("ident")
        x_mid = d["x_mid"]
        wt_all = sb("wt_all", [128, groups * T, NE])
        prim = sb("prim", [128, NE])

        def per_slot(name, shape, dt=F32):
            return [sb(f"{name}{s}", shape, dt) for s in range(SLOTS)]

        X = per_slot("X", [128, T, DIM])
        XT = per_slot("XT", [128, NT])
        R = per_slot("R", [128, T, DIM])
        X1 = per_slot("X1", [128, T, DIM])
        P = per_slot("P", [128, 4, 512])
        PT = per_slot("PT", [128, 4, 512])
        Q2 = per_slot("Q2", [128, 4, 1024])
        K8 = per_slot("K8", [128, 2048])
        V8 = per_slot("V8", [128, 2048])
        O = per_slot("O", [128, TB, 64])
        stats = per_slot("stats", [128, T, 6])
        mv = per_slot("mv", [128, T, 2])
        rstd = per_slot("rstd", [128, T])
        small = per_slot("small", [128, 5, 32])
        gs = per_slot("gs", [128, 8, 32])
        gidx = per_slot("gidx", [128, T, 8], U32)
        maskc = per_slot("maskc", [128, T])
        power = sb("power", [128, 32])
        w1r = [sb(f"w1r{k}", [128, FF]) for k in range(2)]
        w2r = [sb(f"w2r{k}", [128, NC, DIM]) for k in range(2)]
        emap = sb("emap", [8, 12, 8])
        eidx = sb("eidx", [8, 8], U32)

        banks = [[ctx.enter_context(nc.psum_tensor(f"bank{s}_{k}", [128, 512], F32)) for k in range(4)]
                 for s in range(SLOTS)]

        def tok(ap):
            return ap.rearrange("p (t d) -> p t d", t=T)

        def seqs(ap):
            return ap.rearrange("p (b l) -> p b l", l=SEQ)

        def over(ap, n):
            return ap.unsqueeze(1).to_broadcast([ap.shape[0], n, ap.shape[1]])

        def each(ap, n):
            return ap.unsqueeze(2).to_broadcast([ap.shape[0], ap.shape[1], n])

        ctxT = [V8[s][:, 0:1024].rearrange("p (c n) -> p c n", c=2) for s in range(SLOTS)]
        maskr = [V8[s][:, 1024:1536] for s in range(SLOTS)]
        maskb = [V8[s][:, 1536:2048] for s in range(SLOTS)]
        KT = [K8[s][:, 0:512] for s in range(SLOTS)]
        QT = [K8[s][:, 512:1024] for s in range(SLOTS)]
        tmpa = [K8[s][:, 1024:1536] for s in range(SLOTS)]
        tmpb = [K8[s][:, 1536:2048] for s in range(SLOTS)]
        pair = [PT[s][:, 0:2, :].rearrange("p a (b r l) -> p (a b) r l", r=2, l=SEQ) for s in range(SLOTS)]
        vdiag = [Q2[s][:, 0, :].rearrange("p (b i c) -> p b i c", b=TB, c=32) for s in range(SLOTS)]
        xv = [Q2[s][:, 1:3, :].rearrange("p a c -> p (a c)")[:, 0:T * 4 * 66]
              .rearrange("p (t i b c) -> p t i b c", t=T, i=4, b=2) for s in range(SLOTS)]
        sg = [Q2[s][:, 3, 0:512] for s in range(SLOTS)]
        yc = [Q2[s][:, 3, 512:1024] for s in range(SLOTS)]
        ysq = [PT[s][:, 2, :] for s in range(SLOTS)]
        hT = [PT[s][:, 3, :] for s in range(SLOTS)]
        OT2 = [P[s][0:64, 0:2, :] for s in range(SLOTS)]

        s_const, s_init = sem("s_const"), sem("s_init")
        s_const2 = sem("s_const2")
        loaded = [sem(f"loaded{s}") for s in range(SLOTS)]
        stored = [sem(f"stored{s}") for s in range(SLOTS)]
        a_qk_ps = signal("a_qk_ps", 4)
        a_qk_mul = signal("a_qk_mul", 4)
        a_k_sum = signal("a_k_sum", 2)
        a_k_pair = signal("a_k_pair")
        a_vg_ps = signal("a_vg_ps", 2)
        a_v_diag = signal("a_v_diag")
        a_tanh = signal("a_tanh")
        a_gated = signal("a_gated")
        a_st_ps = signal("a_st_ps", 4)
        a_st = signal("a_st", 4)
        a_y_ps = signal("a_y_ps")
        a_y_cent = signal("a_y_cent")
        a_y_sq = signal("a_y_sq")
        a_y_var = signal("a_y_var")
        a_y_rstd = signal("a_y_rstd")
        a_y_norm = signal("a_y_norm")
        a_y_aff = signal("a_y_aff")
        a_h = signal("a_h")
        a_h_ps = signal("a_h_ps")
        a_hT = signal("a_hT")
        a_o_ps = signal("a_o_ps")
        a_ln_mv = signal("a_ln_mv")
        a2_ln_mv = signal("a2_ln_mv")
        a_ln_rstd = signal("a_ln_rstd")
        a2_ln_rstd = signal("a2_ln_rstd")
        a_x = signal("a_x")
        a2_x = signal("a2_x")
        a_x_ps = signal("a_x_ps", 1, 2)
        a_xT = signal("a_xT", 1, 2)
        a_kv_ps = signal("a_kv_ps", 3)
        a_bias = signal("a_bias")
        a_q = signal("a_q")
        a_kT = signal("a_kT")
        a_v = signal("a_v")
        a_q_pair = signal("a_q_pair")
        a_s_ps = signal("a_s_ps", 4)
        a_s_sub = signal("a_s_sub", 4)
        a_p = signal("a_p", 4)
        a_p_ps = signal("a_p_ps", 4)
        a_pT = signal("a_pT", 4)
        a_r_ps = signal("a_r_ps", 4)
        a_r = signal("a_r")
        a_rt_ps = signal("a_rt_ps", 2)
        a_rT = signal("a_rT", 2)
        a_o2_ps = signal("a_o2_ps")
        a_g_ps = signal("a_g_ps")
        a_g_diff = signal("a_g_diff")
        a_g_exp = signal("a_g_exp")
        a_g_done = signal("a_g_done")
        dve1, pool1 = Steps(sem("dve1")), Steps(sem("pool1"))

        kcat = [K8[s][:, 0:1024].rearrange("p (b m) -> p b m", m=128) for s in range(SLOTS)]
        vcat = [V8[s][:, 0:TB * 8 * 17].rearrange("p (b g c) -> p b g c", b=TB, g=8) for s in range(SLOTS)]
        vf = [V8[s][:, 0:T * 8 * 34].rearrange("p (t g b c) -> p t g b c", t=T, g=8, b=2) for s in range(SLOTS)]
        qdiag = [Q2[s][:, :, :].rearrange("p c (b r l) -> p c b r l", r=2, l=SEQ) for s in range(SLOTS)]
        kc = [K8[s][:, :].rearrange("p (c n) -> p c n", c=4) for s in range(SLOTS)]
        va = [V8[s][:, :].rearrange("p (t n) -> p t n", t=T) for s in range(SLOTS)]
        q4 = [[Q2[s][:, 2 * k:2 * k + 2, :].rearrange("p a (b j l) -> p (a b) j l", j=4, l=SEQ)
               for s in range(SLOTS)] for k in range(2)]
        kf = [K8[s][:, 0:512] for s in range(SLOTS)]
        qf = [K8[s][:, 512:1024] for s in range(SLOTS)]
        wts = [gs[s][:, 2, :].rearrange("p (t e) -> p t e", t=T) for s in range(SLOTS)]
        share = [gs[s][:, 3, :].rearrange("p (t e) -> p t e", t=T) for s in range(SLOTS)]
        wtT = [O[s][0:8, :, :].rearrange("p b c -> p (b c)") for s in range(SLOTS)]
        s_prim, s_cnt, s_map, s_q2 = sem("s_prim"), sem("s_cnt"), sem("s_map"), sem("s_q2")
        s_mid = Steps(sem("s_mid"))
        reloaded = [sem(f"reloaded{s}") for s in range(SLOTS)]
        context = [sem(f"context{s}") for s in range(SLOTS)]
        w_loaded = [sem(f"w_loaded{k}") for k in range(2)]
        written = [sem(f"written{s}") for s in range(SLOTS)]
        b_x_ps = signal("b_x_ps", 1, 3)
        b2_x_ps = signal("b2_x_ps", 1, 2)
        b_xT = signal("b_xT", 1, 3)
        b2_xT = signal("b2_xT", 1, 2)
        b_x = signal("b_x", 1, 3)
        b2_x = signal("b2_x")
        b_x1 = signal("b_x1")
        b_ln_x1 = signal("b_ln_x1", 1, 2)
        b_ln_mv = signal("b_ln_mv", 1, 3)
        b2_ln_mv = signal("b2_ln_mv", 1, 3)
        b_ln_rstd = signal("b_ln_rstd", 1, 3)
        b2_ln_rstd = signal("b2_ln_rstd", 1, 3)
        b_wts = signal("b_wts")
        b_wt_ps = signal("b_wt_ps")
        b2_wt_ps = signal("b2_wt_ps")
        b_wtT = signal("b_wtT")
        b2_wtT = signal("b2_wtT")
        b_share_ps = signal("b_share_ps")
        b_share = signal("b_share")
        b_up_ps = signal("b_up_ps", 2, 8)
        b_tanh = signal("b_tanh", 1, 8)
        b_fh = signal("b_fh", 1, 8)
        b_down_ps = signal("b_down_ps", 1, 8)
        b_comb = signal("b_comb", 1, 8)
        b_proj_ps = signal("b_proj_ps", 4, 6)
        b_aq_a = signal("b_aq_a", 2, 2)
        b_aq_v = signal("b_aq_v", 2, 2)
        b_ak = signal("b_ak", 4, 2)
        b_av = signal("b_av", 4, 2)
        b_arc = signal("b_arc", 4, 2)
        b_an = signal("b_an", 4, 2)
        b_ao_ps = signal("b_ao_ps", 4, 2)
        b_aoT = signal("b_aoT", 4, 2)
        b_out_ps = signal("b_out_ps", 1, 2)
        b_out = signal("b_out", 1, 2)
        b_cqk_ps = signal("b_cqk_ps", 2)
        b_cv_ps = signal("b_cv_ps", 2)
        b_cq = signal("b_cq")
        b_ck = signal("b_ck")
        b_cv = signal("b_cv")
        b_cones = signal("b_cones")
        b_s_ps = signal("b_s_ps", 4, 6)
        b2_s_ps = signal("b2_s_ps", 4, 2)
        b_s_sub = signal("b_s_sub", 4, 6)
        b2_s_sub = signal("b2_s_sub", 4, 2)
        b_p = signal("b_p", 4, 6)
        b2_p = signal("b2_p", 4, 2)
        b_p_ps = signal("b_p_ps", 4, 6)
        b2_p_ps = signal("b2_p_ps", 4, 2)
        b_pT = signal("b_pT", 4, 6)
        b2_pT = signal("b2_pT", 4, 2)
        b_r_ps = signal("b_r_ps", 1, 4)
        b2_r_ps = signal("b2_r_ps", 1, 2)
        b_r = signal("b_r", 1, 4)
        b2_r = signal("b2_r", 1, 2)
        b_rt_ps = signal("b_rt_ps", 2)
        b2_rt_ps = signal("b2_rt_ps", 2)
        b_rT = signal("b_rT", 2)
        b2_rT = signal("b2_rT", 2)
        b_o_ps = signal("b_o_ps")
        b2_o_ps = signal("b2_o_ps")
        b_fqk_ps = signal("b_fqk_ps", 4)
        b_frot = signal("b_frot", 4)
        b_fsum = signal("b_fsum", 2)
        b_fq = signal("b_fq")
        b_fzero = signal("b_fzero")
        b_fv_ps = signal("b_fv_ps")
        b_fv = signal("b_fv")
        b_g_ps = signal("b_g_ps")
        b_g_diff = signal("b_g_diff")
        b_g_exp = signal("b_g_exp")
        b_g_done = signal("b_g_done")
        b_b2_ps = signal("b_b2_ps")
        b_b2 = signal("b_b2")
        b_mup_ps = signal("b_mup_ps", 4, 8)
        b_gelu = signal("b_gelu", 4, 8)
        b_mdown_ps = signal("b_mdown_ps", 1, 8)
        b_mcomb = signal("b_mcomb", 1, 8)
        b_r2 = signal("b_r2")
        dve2, pool2 = Steps(sem("dve2")), Steps(sem("pool2"))

        block = ctx.enter_context(nc.Block())

        @block.sync
        def _(sp):
            for dst, src in ((const, d["const"]), (wa, d["wa"])):
                sp.dma_start(dst[:, :], src).then_inc(s_const, 16)
            sp.dma_start(rows[:, :], d["rows"].partition_broadcast(128)).then_inc(s_const, 16)

            def token_rows(dram, n, s):
                return dram[bass.ds((n * SLOTS + s) * NT, NT), :].rearrange("(t p) d -> p t d", p=128)

            def loads(n, s):
                t0 = (n * SLOTS + s) * NT
                sp.dma_start(XT[s][:, :], d["xT"][:, bass.ds(t0, NT)]).then_inc(loaded[s], 16)
                for c in range(2):
                    sp.dma_start(ctxT[s][:, c, :], d["ctxT"][c * 128:c * 128 + 128, bass.ds(t0, NT)])\
                      .then_inc(loaded[s], 16)
                sp.dma_start(X[s][:, :, :], token_rows(d["x"], n, s)).then_inc(loaded[s], 16)
                sp.dma_start(maskr[s], d["mask"][bass.ds(t0, NT)].partition_broadcast(128))\
                  .then_inc(loaded[s], 16)
                sp.dma_start(maskc[s][:, :], d["mask"][bass.ds(t0, NT)].rearrange("(t p) -> p t", p=128),
                             allow_slow_non_contiguous=True).then_inc(loaded[s], 16)

            def first(n, s):
                yield from ()

            def second(n, s, last):
                yield "gb"
                sp.wait_ge(a2_x.sem, a2_x.at(n, s))
                apart(sp)
                sp.dma_start(token_rows(x_mid, n, s), X[s][:, :, :]).then_inc(stored[s], 16)
                if not last:
                    sp.wait_ge(a_g_done.sem, a_g_done.at(n, s))
                    apart(sp)
                    sp.wait_ge(stored[s], 16 * n + 16)
                    apart(sp)
                    loads(n + 1, s)

            loads(0, 0)
            loads(0, 1)
            for dst, src in ((w64, d["w64"]), (cols, d["cols"]), (w8, d["w8"]), (wb, d["wb"])):
                sp.dma_start(dst[:, :], src).then_inc(s_const2, 16)
            passes_of(sp, passes, A_FIRST, A_SECOND, A_TURNS, first, second, None, 0)
            for s in range(SLOTS):
                sp.wait_ge(stored[s], 16 * passes)
                sp.wait_ge(a_g_done.sem, a_g_done.at(passes - 1, s))

            def load_state(n, s):
                sp.dma_start(X[s][:, :, :], token_rows(x_mid, n, s)).then_inc(reloaded[s], 16)

            def load_expert(e):
                sp.dma_start(w1r[e % 2][:, :], d["w1"][e]).then_inc(w_loaded[e % 2], 16)
                sp.dma_start(w2r[e % 2][:, :, :], d["w2"][e].rearrange("(c p) d -> p c d", p=128))\
                  .then_inc(w_loaded[e % 2], 16)

            def first2(n, s):
                yield "out1"
                t0 = (n * SLOTS + s) * NT
                sp.wait_ge(b_ao_ps.sem, b_ao_ps.at(n, s, use=1))
                apart(sp)
                sp.dma_start(kcat[s][:, :, 0:SEQ], d["ctxT"][0:128, bass.ds(t0, NT)]
                             .rearrange("p (b m) -> p b m", m=SEQ)).then_inc(context[s], 16)
                for b in range(TB):
                    sp.dma_start(vcat[s][0:SEQ, b, :, 0:16], d["ctx"][bass.ds(t0 + SEQ * b, SEQ), 128:256]
                                 .rearrange("m (g v) -> m g v", v=16)).then_inc(context[s], 16)

            def second2(n, s, last):
                for e in range(NE):
                    yield part_of(f"md{e}", T - 1)
                    sp.wait_ge(b_mdown_ps.sem, b_mdown_ps.at(n, s, use=e))
                    apart(sp)
                    if e < NE - 2 or not (last and s == 1):
                        load_expert((e + 2) % NE)
                yield "n5"
                sp.wait_ge(b2_x.sem, b2_x.at(n, s))
                apart(sp)
                sp.dma_start(token_rows(out, n, s), X[s][:, :, :]).then_inc(written[s], 16)
                if not last:
                    sp.wait_ge(written[s], 16 * n + 16)
                    apart(sp)
                    load_state(n + 1, s)

            for s in range(SLOTS):
                load_state(0, s)
            for e in range(2):
                load_expert(e)
            passes_of(sp, passes, B_FIRST, B_SECOND, B_TURNS, first2, second2, None, 0)
            for s in range(SLOTS):
                sp.wait_ge(written[s], 16 * passes)

        @block.gpsimd
        def _(pool):
            pool.memset(power[:, :], -0.5)
            pool.memset(prim[:, :], 0.0)
            for s in range(SLOTS):
                last = pool.memset(Q2[s][:, :, :], 0.0)
            last.then_inc(s_init, 1)
            pool.wait_ge(s_init, 1)
            for s in range(SLOTS):
                for b in range(2):
                    last = pool.memset(xv[s][64 * b:64 * b + 64, :, :, b, 32:33], 1.0)
            last.then_inc(s_init, 1)
            pool.wait_ge(s_const, 16 * 3)

            def root(n, s, ln_mv, ln_rstd, step, use=0):
                pool.wait_ge(ln_mv.sem, ln_mv.at(n, s, use=use))
                apart(pool)
                step(pool, pool.tensor_scalar(rstd[s][:, :], mv[s][:, :, 1], EPS, None, ALU.add))
                pool.tensor_tensor(rstd[s][:, :], rstd[s][:, :], power[:, 0:T], ALU.pow).then_inc(ln_rstd.sem, 1)

            def first(n, s):
                yield "qk.1"
                pool.wait_ge(a_qk_mul.sem, a_qk_mul.at(n, s, 2))
                pool.tensor_tensor(KT[s], P[s][:, 0, :], P[s][:, 1, :], ALU.add).then_inc(a_k_sum.sem, 1)
                yield "qk.3"
                pool.wait_ge(a_qk_mul.sem, a_qk_mul.at(n, s, 4))
                pool.tensor_tensor(QT[s], P[s][:, 2, :], P[s][:, 3, :], ALU.add).then_inc(a_k_sum.sem, 1)
                pool.tensor_scalar(maskb[s], maskr[s], 0.0, NEG, ALU.is_equal, ALU.mult).then_inc(a_bias.sem, 1)
                yield "yv"
                pool.wait_ge(a_y_var.sem, a_y_var.at(n, s))
                apart(pool)
                pool1(pool, pool.tensor_scalar(gs[s][:, 2, :], gs[s][:, 1, :], 1.0 / 16, EPS, ALU.mult, ALU.add))
                pool.tensor_tensor(gs[s][:, 3, :], gs[s][:, 2, :], power[:, :], ALU.pow).then_inc(a_y_rstd.sem, 1)
                yield "yn"
                pool.wait_ge(a_y_norm.sem, a_y_norm.at(n, s))
                pool1(pool, pool.tensor_tensor(tok(yc[s]), tok(yc[s]), over(Row("gnw"), T), ALU.mult))
                pool.tensor_tensor(tok(yc[s]), tok(yc[s]), over(Row("gnb"), T), ALU.add).then_inc(a_y_aff.sem, 1)
                yield "o"
                root(n, s, a_ln_mv, a_ln_rstd, pool1)

            def second(n, s, last):
                yield "o2"
                root(n, s, a2_ln_mv, a2_ln_rstd, pool1)

            passes_of(pool, passes, A_FIRST, A_SECOND, A_TURNS, first, second, pool1, STEPS["pool1"])

            for s in range(SLOTS):
                pool.wait_ge(a_g_done.sem, a_g_done.at(passes - 1, s))
            for s in range(SLOTS):
                pool.memset(Q2[s][:, :, :], 0.0).then_inc(s_q2, 1)

            def scale_shift(s, g, b):
                pool2(pool, pool.tensor_tensor(X1[s][:, :, :], X1[s][:, :, :], over(Row(g), T), ALU.mult))
                return pool.tensor_tensor(X1[s][:, :, :], X1[s][:, :, :], over(Row(b), T), ALU.add)

            def first2(n, s):
                yield "in"
                apart(pool)
                pool.tensor_copy(wts[s], wt_all[:, bass.ds((n * SLOTS + s) * T, T), :]).then_inc(b_wts.sem, 1)
                yield f"down{NE - 1}"
                root(n, s, b_ln_mv, b_ln_rstd, pool2, 0)
                for r in range(2):
                    for c in range(4):
                        yield part_of(f"am{r}", c)
                        pool.wait_ge(b_arc.sem, b_arc.at(n, s, c + 1, use=r))
                        pool.tensor_tensor(seqs(P[s][:, c, :]), seqs(P[s][:, c, :]),
                                           each(gs[s][:, 2, 8 * c:8 * c + 8], SEQ), ALU.mult).then_inc(b_an.sem, 1)
                yield "out1"
                pool.wait_ge(b_ao_ps.sem, b_ao_ps.at(n, s, use=1))
                apart(pool)
                pool.memset(vcat[s][:, :, :, 16:17], 1.0).then_inc(b_cones.sem, 1)
                root(n, s, b_ln_mv, b_ln_rstd, pool2, 1)
                yield "co"
                pool.wait_ge(b_r_ps.sem, b_r_ps.at(n, s, use=3))
                apart(pool)
                pool2(pool, pool.memset(V8[s][:, 0:T * 8 * 34], 0.0))
                apart(pool)
                for b in range(2):
                    last = pool.memset(vf[s][64 * b:64 * b + 64, :, :, b, 16:17], 1.0)
                last.then_inc(b_fzero.sem, 1)
                pool.wait_ge(b_fzero.sem, b_fzero.at(n, s))
                root(n, s, b_ln_mv, b_ln_rstd, pool2, 2)

            def second2(n, s, last):
                yield "fq.1"
                pool.wait_ge(b_frot.sem, b_frot.at(n, s, 2))
                pool.tensor_tensor(qf[s], P[s][:, 0, :], P[s][:, 1, :], ALU.add).then_inc(b_fsum.sem, 1)
                yield "fq.3"
                pool.wait_ge(b_frot.sem, b_frot.at(n, s, 4))
                pool.tensor_tensor(kf[s], P[s][:, 2, :], P[s][:, 3, :], ALU.add).then_inc(b_fsum.sem, 1)
                yield "fs1"
                pool.wait_ge(b2_s_ps.sem, b2_s_ps.at(n, s, use=1))
                apart(pool)
                pool.memset(Q2[s][:, :, :], 0.0).then_inc(s_q2, 1)
                yield "fo"
                root(n, s, b2_ln_mv, b2_ln_rstd, pool2, 0)
                yield "n3"
                pool.wait_ge(b_ln_x1.sem, b_ln_x1.at(n, s, use=0))
                scale_shift(s, "g1", "be1").then_inc(b_x1.sem, 1)
                yield f"md{NE - 1}"
                root(n, s, b2_ln_mv, b2_ln_rstd, pool2, 1)
                yield "n4"
                pool.wait_ge(b_ln_x1.sem, b_ln_x1.at(n, s, use=1))
                pool2(pool, scale_shift(s, "g2", "be2"))
                pool.tensor_tensor(R[s][:, :, :], X1[s][:, :, :], X[s][:, :, :], ALU.add).then_inc(b_r2.sem, 1)
                yield "n5s"
                root(n, s, b2_ln_mv, b2_ln_rstd, pool2, 2)

            passes_of(pool, passes, B_FIRST, B_SECOND, B_TURNS, first2, second2, pool2, STEPS["pool2"])

        @block.scalar
        def _(act):
            act.wait_ge(s_init, 2)
            act.wait_ge(s_const, 16 * 3)

            def first(n, s):
                yield "qk.1"
                act.wait_ge(a_k_sum.sem, a_k_sum.at(n, s, 1))
                for r in range(2):
                    last = act.activation(pair[s][:, :, r, :], seqs(KT[s]), ACT.Copy, scale=C("par")[:, r:r + 1])
                last.then_inc(a_k_pair.sem, 1)
                yield "vg"
                act.wait_ge(a_vg_ps.sem, a_vg_ps.at(n, s, 1))
                for r in range(2):
                    h = slice(64 * r, 64 * r + 64)
                    last = act.activation(vdiag[s][h, :, :, 16 * r:16 * r + 16],
                                          banks[s][0][h, :].rearrange("p (b i v) -> p b i v", b=TB, v=16), ACT.Copy)
                last.then_inc(a_v_diag.sem, 1)
                act.wait_ge(a_vg_ps.sem, a_vg_ps.at(n, s, 2))
                act.activation(sg[s], banks[s][1][:, :], ACT.Tanh, scale=0.5).then_inc(a_tanh.sem, 1)
                yield "y"
                act.wait_ge(a_y_cent.sem, a_y_cent.at(n, s))
                act.activation(ysq[s], yc[s], ACT.Square).then_inc(a_y_sq.sem, 1)
                yield "h"
                act.wait_ge(a_h_ps.sem, a_h_ps.at(n, s))
                act.activation(hT[s], banks[s][1][:, :], ACT.Copy).then_inc(a_hT.sem, 1)

            def second(n, s, last):
                yield "kv"
                act.wait_ge(a_x_ps.sem, a_x_ps.at(n, s, use=0))
                act.activation(XT[s][:, :], banks[s][0][:, :], ACT.Copy).then_inc(a_xT.sem, 1)
                yield "q"
                act.wait_ge(a_q.sem, a_q.at(n, s))
                for r in range(2):
                    ins = act.activation(pair[s][:, :, r, :], seqs(QT[s]), ACT.Copy, scale=C("par")[:, r:r + 1])
                ins.then_inc(a_q_pair.sem, 1)
                for i in range(4):
                    yield part_of("s", i)
                    act.wait_ge(a_s_sub.sem, a_s_sub.at(n, s, i + 1))
                    act.activation(P[s][:, i, :], P[s][:, i, :], ACT.Exp).then_inc(a_p.sem, 1)
                for i in range(4):
                    yield part_of("p", i)
                    act.wait_ge(a_p_ps.sem, a_p_ps.at(n, s, i + 1))
                    act.activation(PT[s][:, i, :], banks[s][i][:, :], ACT.Copy).then_inc(a_pT.sem, 1)
                yield "rt"
                for k in range(2):
                    act.wait_ge(a_rt_ps.sem, a_rt_ps.at(n, s, k + 1))
                    act.activation(OT2[s][:, :, 256 * k:256 * k + 256].rearrange("p r (b l) -> p b r l", l=SEQ),
                                   banks[s][k][0:64, :].rearrange("p (b r l) -> p b r l", r=2, l=SEQ),
                                   ACT.Copy).then_inc(a_rT.sem, 1)
                yield "x"
                act.wait_ge(a_x_ps.sem, a_x_ps.at(n, s, use=1))
                act.activation(XT[s][:, :], banks[s][3][:, :], ACT.Copy).then_inc(a_xT.sem, 1)
                yield "g"
                act.wait_ge(a_g_diff.sem, a_g_diff.at(n, s))
                act.activation(small[s][:, 1, 0:4], small[s][:, 0, 0:4], ACT.Exp).then_inc(a_g_exp.sem, 1)

            passes_of(act, passes, A_FIRST, A_SECOND, A_TURNS, first, second, None, 0)

            def state_turned(n, s, bank, x_ps, xT, use):
                act.wait_ge(x_ps.sem, x_ps.at(n, s, use=use))
                act.activation(XT[s][:, :], banks[s][bank][:, :], ACT.Copy).then_inc(xT.sem, 1)

            def weights_turned(n, s, wt_ps, wt_T):
                act.wait_ge(wt_ps.sem, wt_ps.at(n, s))
                act.activation(wtT[s], banks[s][1][0:8, :], ACT.Copy).then_inc(wt_T.sem, 1)

            def exps(n, s, stage, s_sub, p, use, scale):
                for i in range(4):
                    yield part_of(stage, i)
                    act.wait_ge(s_sub.sem, s_sub.at(n, s, i + 1, use=use))
                    act.activation(P[s][:, i, :], P[s][:, i, :], ACT.Exp, scale=scale).then_inc(p.sem, 1)

            def probs_turned(n, s, stage, p_ps, pT, use):
                for i in range(4):
                    yield part_of(stage, i)
                    act.wait_ge(p_ps.sem, p_ps.at(n, s, i + 1, use=use))
                    act.activation(PT[s][:, i, :], banks[s][i][:, :], ACT.Copy).then_inc(pT.sem, 1)

            def results_turned(n, s, base, rt_ps, rT):
                for k in range(2):
                    act.wait_ge(rt_ps.sem, rt_ps.at(n, s, k + 1))
                    act.activation(OT2[s][:, :, 256 * k:256 * k + 256].rearrange("p r (b l) -> p b r l", l=SEQ),
                                   banks[s][base + k][0:64, :].rearrange("p (b r l) -> p b r l", r=2, l=SEQ),
                                   ACT.Copy).then_inc(rT.sem, 1)

            def first2(n, s):
                yield "in"
                state_turned(n, s, 0, b_x_ps, b_xT, 0)
                weights_turned(n, s, b_wt_ps, b_wtT)
                for e in range(NE):
                    yield f"up{e}"
                    act.wait_ge(b_up_ps.sem, b_up_ps.at(n, s, 1, use=e))
                    act.activation(P[s][:, 0, :], banks[s][0][:, :], ACT.Tanh, scale=0.5).then_inc(b_tanh.sem, 1)
                yield "t1"
                state_turned(n, s, 0, b_x_ps, b_xT, 1)
                for r in range(2):
                    for c in (0, 2):
                        yield part_of(f"aq{r}", c)
                        act.wait_ge(s_q2, SLOTS * n + s + 1)
                        act.wait_ge(b_proj_ps.sem, b_proj_ps.at(n, s, c + 1, use=3 * r))
                        for q in range(2):
                            h = slice(64 * q, 64 * q + 64)
                            last = act.activation(qdiag[s][h, c, :, q, :], seqs(banks[s][c][h, :]),
                                                  ACT.Identity, bias=Col("abq", 4 * r + c)[h, :])
                        last.then_inc(b_aq_a.sem, 1)
                    for c in range(4):
                        yield part_of(f"ak{r}", c)
                        act.wait_ge(b_proj_ps.sem, b_proj_ps.at(n, s, c + 1, use=3 * r + 1))
                        act.activation(kc[s][:, c, :], banks[s][c][:, :], ACT.Identity,
                                       bias=Col("abk", 4 * r + c)).then_inc(b_ak.sem, 1)
                    yield from exps(n, s, f"as{r}", b_s_sub, b_p, r, 1.0)
                    yield from probs_turned(n, s, f"ap{r}", b_p_ps, b_pT, r)
                    for c in range(4):
                        yield part_of(f"ao{r}", c)
                        act.wait_ge(b_ao_ps.sem, b_ao_ps.at(n, s, c + 1, use=r))
                        act.activation(
                            P[s][:, 2 * (c % 2):2 * (c % 2) + 2, :].rearrange("p c (t b l) -> p c t b l", t=T, b=2)[:, :, :, c // 2, :],
                            banks[s][c][:, :].rearrange("p (c t l) -> p c t l", c=2, t=T), ACT.Copy).then_inc(b_aoT.sem, 1)
                yield "t2"
                state_turned(n, s, 0, b_x_ps, b_xT, 2)
                yield "cq"
                act.wait_ge(b_cqk_ps.sem, b_cqk_ps.at(n, s, 1))
                for j in range(4):
                    last = act.activation(q4[0][s][:, :, j, :], seqs(banks[s][0][:, :]), ACT.Copy,
                                          scale=C("quad")[:, j:j + 1])
                last.then_inc(b_cq.sem, 1)
                for t in range(T):
                    yield from exps(n, s, f"cs{t}", b_s_sub, b_p, 2 + t, 8 ** -0.5)
                    yield from probs_turned(n, s, f"cp{t}", b_p_ps, b_pT, 2 + t)
                yield "crt"
                results_turned(n, s, 1, b_rt_ps, b_rT)

            def second2(n, s, last):
                yield "t3"
                state_turned(n, s, 0, b2_x_ps, b2_xT, 0)
                yield "fq.1"
                act.wait_ge(b_fsum.sem, b_fsum.at(n, s, 1))
                for j in range(4):
                    ins = act.activation(q4[1][s][:, :, j, :], seqs(qf[s]), ACT.Copy, scale=C("quad")[:, j:j + 1])
                ins.then_inc(b_fq.sem, 1)
                for jh in range(2):
                    yield from exps(n, s, f"fs{jh}", b2_s_sub, b2_p, jh, 8 ** -0.5)
                    yield from probs_turned(n, s, f"fp{jh}", b2_p_ps, b2_pT, jh)
                yield "frt"
                results_turned(n, s, 2, b2_rt_ps, b2_rT)
                yield "t4"
                state_turned(n, s, 3, b2_x_ps, b2_xT, 1)
                yield "g"
                act.wait_ge(b_g_diff.sem, b_g_diff.at(n, s))
                act.activation(small[s][:, 1, 0:4], small[s][:, 0, 0:4], ACT.Exp).then_inc(b_g_exp.sem, 1)
                yield "wt"
                weights_turned(n, s, b2_wt_ps, b2_wtT)
                for e in range(NE):
                    for c in range(NC):
                        yield part_of(f"mup{e}", c)
                        act.wait_ge(b_mup_ps.sem, b_mup_ps.at(n, s, c + 1, use=e))
                        act.activation(PT[s][:, c, :], banks[s][c % 3][:, :], ACT.Gelu,
                                       bias=Col("b1", NC * e + c)).then_inc(b_gelu.sem, 1)

            act.wait_ge(s_const2, 16 * 4)
            passes_of(act, passes, B_FIRST, B_SECOND, B_TURNS, first2, second2, None, 0)

        @block.vector
        def _(dve):
            dve.wait_ge(s_init, 2)
            dve.wait_ge(s_const, 16 * 3)
            dve.wait_ge(s_const2, 16 * 4)
            st1 = lambda ins: dve1(dve, ins)
            st2 = lambda ins: dve2(dve, ins)

            def norm_stats(s, step, ln_mv):
                for t in range(T):
                    last = dve.bn_stats(stats[s][:, t, :], R[s][:, t, :])
                step(last)
                apart(dve)
                for t in range(T):
                    last = dve.bn_aggr(mv[s][:, t, :], stats[s][:, t, :])
                last.then_inc(ln_mv.sem, 1)

            def norm_apply(n, s, ln_rstd, done, use=0, dst=None):
                dst = dst or X[s]
                dve.wait_ge(ln_rstd.sem, ln_rstd.at(n, s, use=use))
                for t in range(T):
                    last = dve.tensor_scalar(dst[:, t, :], R[s][:, t, :], mv[s][:, t, 0:1], rstd[s][:, t:t + 1],
                                             ALU.subtract, ALU.mult)
                last.then_inc(done.sem, 1)

            def top(s):
                return (gs[s][:, 4, :].rearrange("p (t e) -> p t e", t=T),
                        gs[s][:, 5, 0:8].rearrange("p (t k) -> p t k", t=T),
                        gs[s][:, 6, :].rearrange("p (t e) -> p t e", t=T),
                        gs[s][:, 7, :].rearrange("p (t e) -> p t e", t=T))

            def choose(s, g_diff, st, logits):
                mx, idf, _, _ = top(s)
                apart(dve)
                for t in range(T):
                    last = dve.max(mx[:, t, :], logits[:, t, :])
                st(last)
                apart(dve)
                for t in range(T):
                    last = dve.max_index(gidx[s][:, t, :], mx[:, t, :], logits[:, t, :])
                st(last)
                dve.tensor_copy(idf, gidx[s][:, :, 0:2])
                dve.tensor_tensor(small[s][:, 0, 0:4], mx[:, :, 1], mx[:, :, 0], ALU.subtract).then_inc(g_diff.sem, 1)

            def weigh(n, s, g_exp, g_done, st, weights, primary):
                _, idf, one1, one2 = top(s)
                dve.wait_ge(g_exp.sem, g_exp.at(n, s))
                st(dve.tensor_scalar(small[s][:, 2, 0:4], small[s][:, 1, 0:4], 1.0, None, ALU.add))
                st(dve.reciprocal(small[s][:, 3, 0:4], small[s][:, 2, 0:4]))
                dve.tensor_tensor(small[s][:, 4, 0:4], small[s][:, 1, 0:4], small[s][:, 3, 0:4], ALU.mult)
                iota = over(C("iota"), T)
                dve.tensor_tensor(one1, iota, each(idf[:, :, 0], NE), ALU.is_equal)
                st(dve.tensor_tensor(one2, iota, each(idf[:, :, 1], NE), ALU.is_equal))
                if primary:
                    st(dve.tensor_reduce(small[s][:, 2, 0:8], one1.rearrange("p t e -> p e t"), AX.X, ALU.max))
                    dve.tensor_tensor(prim[:, :], prim[:, :], small[s][:, 2, 0:8], ALU.max)
                dve.tensor_tensor(one1, one1, each(small[s][:, 3, 0:4], NE), ALU.mult)
                st(dve.tensor_tensor(one2, one2, each(small[s][:, 4, 0:4], NE), ALU.mult))
                dve.tensor_tensor(weights, one1, one2, ALU.add).then_inc(g_done.sem, 1)

            def first(n, s):
                for k, table in enumerate(("ck", "sk", "cq", "sq")):
                    yield part_of("qk", k)
                    dve.wait_ge(a_qk_ps.sem, a_qk_ps.at(n, s, k + 1))
                    dve.tensor_tensor(seqs(P[s][:, k, :]), seqs(banks[s][k][:, :]), over(C(table), TB),
                                      ALU.mult).then_inc(a_qk_mul.sem, 1)
                yield "vg"
                dve.wait_ge(a_tanh.sem, a_tanh.at(n, s))
                dve.scalar_tensor_tensor(sg[s], sg[s], 1.0, banks[s][1][:, :], ALU.add, ALU.mult).then_inc(a_gated.sem, 1)
                for i in range(4):
                    yield part_of("st", i)
                    dve.wait_ge(a_st_ps.sem, a_st_ps.at(n, s, i + 1))
                    dve.tensor_tensor(seqs(P[s][:, i, :]), seqs(banks[s][i][:, :]),
                                      over(C("decay")[:, 64 * i:64 * i + 64], TB), ALU.mult).then_inc(a_st.sem, 1)
                y = banks[s][0][:, :].rearrange("p (g v) -> p g v", v=16)
                ycv = yc[s].rearrange("p (g v) -> p g v", v=16)
                yield "y"
                dve.wait_ge(a_y_ps.sem, a_y_ps.at(n, s))
                st1(dve.tensor_reduce(gs[s][:, 0, :], y, AX.X, ALU.add))
                st1(dve.tensor_scalar(gs[s][:, 1, :], gs[s][:, 0, :], 1.0 / 16, None, ALU.mult))
                dve.tensor_tensor(ycv, y, each(gs[s][:, 1, :], 16), ALU.subtract).then_inc(a_y_cent.sem, 1)
                yield "yv"
                dve.wait_ge(a_y_sq.sem, a_y_sq.at(n, s))
                dve.tensor_reduce(gs[s][:, 1, :], ysq[s].rearrange("p (g v) -> p g v", v=16), AX.X,
                                  ALU.add).then_inc(a_y_var.sem, 1)
                yield "yn"
                dve.wait_ge(a_y_rstd.sem, a_y_rstd.at(n, s))
                dve.tensor_tensor(ycv, ycv, each(gs[s][:, 3, :], 16), ALU.mult).then_inc(a_y_norm.sem, 1)
                yield "yh"
                dve.wait_ge(a_y_aff.sem, a_y_aff.at(n, s))
                dve.scalar_tensor_tensor(yc[s], sg[s], 0.5, yc[s], ALU.mult, ALU.mult).then_inc(a_h.sem, 1)
                yield "o"
                dve.wait_ge(a_o_ps.sem, a_o_ps.at(n, s))
                st1(dve.tensor_tensor(R[s][:, :, :], tok(banks[s][2][:, :]), X[s][:, :, :], ALU.add))
                norm_stats(s, st1, a_ln_mv)
                yield "on"
                norm_apply(n, s, a_ln_rstd, a_x)

            def second(n, s, last):
                yield "kv"
                dve.wait_ge(a_kv_ps.sem, a_kv_ps.at(n, s, 1))
                dve.scalar_tensor_tensor(KT[s], banks[s][2][:, :], Col("xbk"), maskr[s], ALU.add, ALU.mult).then_inc(a_kT.sem, 1)
                dve.wait_ge(a_kv_ps.sem, a_kv_ps.at(n, s, 2))
                st1(dve.tensor_tensor(tok(tmpa[s]), tok(banks[s][3][:, :]), over(Row("xbv"), T), ALU.add))
                for b in range(2):
                    h = slice(64 * b, 64 * b + 64)
                    for t in range(T):
                        ins = dve.tensor_scalar(
                            xv[s][h, t, :, b, 0:32], tmpa[s][h, 128 * t:128 * t + 128].rearrange("p (i c) -> p i c", c=32),
                            maskc[s][h, t:t + 1], None, ALU.mult)
                ins.then_inc(a_v.sem, 1)
                yield "q"
                dve.wait_ge(a_kv_ps.sem, a_kv_ps.at(n, s, 3))
                dve.scalar_tensor_tensor(QT[s], banks[s][1][:, :], Col("xbt"), maskr[s], ALU.add, ALU.mult).then_inc(a_q.sem, 1)
                for i in range(4):
                    yield part_of("s", i)
                    dve.wait_ge(a_bias.sem, a_bias.at(n, s))
                    dve.wait_ge(a_s_ps.sem, a_s_ps.at(n, s, i + 1))
                    st1(dve.scalar_tensor_tensor(P[s][:, i, :], banks[s][i][:, :], 0.25, maskb[s], ALU.mult, ALU.add))
                    st1(dve.tensor_reduce(gs[s][:, 0, 8 * i:8 * i + 8], seqs(P[s][:, i, :]), AX.X, ALU.max))
                    dve.tensor_tensor(seqs(P[s][:, i, :]), seqs(P[s][:, i, :]),
                                      each(gs[s][:, 0, 8 * i:8 * i + 8], SEQ), ALU.subtract).then_inc(a_s_sub.sem, 1)
                for t in range(T):
                    yield part_of("r", t)
                    dve.wait_ge(a_r_ps.sem, a_r_ps.at(n, s, t + 1))
                    rv = banks[s][t][:, 0:264].rearrange("p (b i c) -> p b i c", b=2, i=4)
                    rc = gs[s][:, 1, 8 * t:8 * t + 8]
                    st1(dve.reciprocal(rc.rearrange("p (b i) -> p b i", b=2), rv[:, :, :, 32]))
                    for r in range(2):
                        h = slice(64 * r, 64 * r + 64)
                        ins = dve.tensor_tensor(
                            O[s][h, 2 * t:2 * t + 2, :].rearrange("p b (i v) -> p (b i) v", v=16),
                            banks[s][t][h, 0:264].rearrange("p (g c) -> p g c", c=33)[:, :, 16 * r:16 * r + 16],
                            each(rc[h, :], 16), ALU.mult)
                ins.then_inc(a_r.sem, 1)
                yield "o2"
                dve.wait_ge(a_o2_ps.sem, a_o2_ps.at(n, s))
                st1(dve.tensor_tensor(R[s][:, :, :], tok(banks[s][2][:, :]), X[s][:, :, :], ALU.add))
                st1(dve.tensor_tensor(R[s][:, :, :], R[s][:, :, :], over(Row("xbo"), T), ALU.add))
                norm_stats(s, st1, a2_ln_mv)
                yield "on"
                norm_apply(n, s, a2_ln_rstd, a2_x)
                yield "g"
                dve.wait_ge(a_g_ps.sem, a_g_ps.at(n, s))
                lg = small[s][:, 3, :].rearrange("p (t e) -> p t e", t=T)
                st1(dve.tensor_copy(lg, banks[s][0][:, 0:T * NE].rearrange("p (t e) -> p t e", t=T)))
                choose(s, a_g_diff, st1, lg)
                yield "gb"
                weigh(n, s, a_g_exp, a_g_done, st1, wt_all[:, bass.ds((n * SLOTS + s) * T, T), :], True)

            passes_of(dve, passes, A_FIRST, A_SECOND, A_TURNS, first, second, dve1, STEPS["dve1"])

            for s in range(SLOTS):
                dve.wait_ge(a_g_done.sem, a_g_done.at(passes - 1, s))
            dve.tensor_copy(prim[:, :], prim[:, :]).then_inc(s_prim, 1)
            dve.wait_ge(s_cnt, 1)
            mid = lambda ins: s_mid(dve, ins)
            E = lambda k: emap[:, k, :]
            dve.tensor_scalar(E(0), banks[0][0][0:8, 0:8], 0.0, None, ALU.is_gt)
            mid(dve.tensor_scalar(E(1), banks[0][0][0:8, 8:16], 0.0, None, ALU.is_gt))
            mid(dve.tensor_tensor(E(2), W8p("sim"), E(0), ALU.mult))
            mid(dve.tensor_scalar(E(3), E(0), -NEG, NEG, ALU.mult, ALU.add))
            mid(dve.tensor_tensor(E(2), E(2), E(3), ALU.add))
            mid(dve.max(E(4), E(2)))
            mid(dve.max_index(eidx[:, :], E(4), E(2)))
            mid(dve.tensor_copy(E(5), eidx[:, :]))
            mid(dve.tensor_tensor(E(6), C("iota")[0:8, :], E(5)[:, 0:1].to_broadcast([8, 8]), ALU.is_equal))
            mid(dve.tensor_tensor(E(6), E(6), W8p("eye"), ALU.subtract))
            mid(dve.tensor_scalar(E(7), E(4), float(np.float32(0.7)), None, ALU.is_ge))
            mid(dve.tensor_scalar(E(8), E(1), -1.0, 1.0, ALU.mult, ALU.add))
            mid(dve.tensor_tensor(E(9), E(7)[:, 0:1].to_broadcast([8, 8]), E(8), ALU.mult))
            mid(dve.tensor_tensor(E(10), E(6), E(9), ALU.mult))
            dve.tensor_tensor(E(11), E(10), W8p("eye"), ALU.add).then_inc(s_map, 1)

            def combine(s, e, bank, done, src):
                for t in range(T):
                    last = dve.scalar_tensor_tensor(R[s][:, t, :], bank[:, 128 * t:128 * t + 128],
                                                    share[s][:, t, e:e + 1], src[:, t, :], ALU.mult, ALU.add)
                last.then_inc(done.sem, 1)

            def subtract_max(n, s, stage, s_ps, s_sub, use, width):
                g = 512 // width
                for i in range(4):
                    yield part_of(stage, i)
                    dve.wait_ge(s_ps.sem, s_ps.at(n, s, i + 1, use=use))
                    v = banks[s][i][:, :].rearrange("p (g m) -> p g m", m=width)
                    mx = gs[s][:, 0, g * i:g * i + g]
                    st2(dve.tensor_reduce(mx, v, AX.X, ALU.max))
                    dve.tensor_tensor(P[s][:, i, :].rearrange("p (g m) -> p g m", m=width), v,
                                      each(mx, width), ALU.subtract).then_inc(s_sub.sem, 1)

            def add_projection(s, bank, row):
                st2(dve.tensor_tensor(R[s][:, :, :], tok(bank[:, :]), X[s][:, :, :], ALU.add))
                st2(dve.tensor_tensor(R[s][:, :, :], R[s][:, :, :], over(Row(row), T), ALU.add))

            def first2(n, s):
                yield "sh"
                dve.wait_ge(b_share_ps.sem, b_share_ps.at(n, s))
                dve.tensor_copy(share[s], banks[s][2][:, 0:T * NE].rearrange("p (t e) -> p t e", t=T)).then_inc(b_share.sem, 1)
                for e in range(NE):
                    yield f"up{e}"
                    dve.wait_ge(b_tanh.sem, b_tanh.at(n, s, use=e))
                    st2(dve.scalar_tensor_tensor(P[s][:, 0, :], P[s][:, 0, :], 1.0, banks[s][0][:, :], ALU.add, ALU.mult))
                    dve.wait_ge(b_up_ps.sem, b_up_ps.at(n, s, 2, use=e))
                    dve.scalar_tensor_tensor(P[s][:, 1, :], P[s][:, 0, :], 0.5, banks[s][1][:, :],
                                             ALU.mult, ALU.mult).then_inc(b_fh.sem, 1)
                    yield f"down{e}"
                    dve.wait_ge(b_down_ps.sem, b_down_ps.at(n, s, use=e))
                    if e:
                        dve.wait_ge(b_comb.sem, b_comb.at(n, s, use=e - 1))
                    else:
                        dve.wait_ge(b_share.sem, b_share.at(n, s))
                    combine(s, e, banks[s][2 + e % 2], b_comb, R[s] if e else X[s])
                dve.wait_ge(b_comb.sem, b_comb.at(n, s, use=NE - 1))
                norm_stats(s, st2, b_ln_mv)
                yield "n0"
                norm_apply(n, s, b_ln_rstd, b_x, 0)
                for r in range(2):
                    for c in (1, 3):
                        yield part_of(f"aq{r}", c)
                        dve.wait_ge(s_q2, SLOTS * n + s + 1)
                        dve.wait_ge(b_proj_ps.sem, b_proj_ps.at(n, s, c + 1, use=3 * r))
                        for q in range(2):
                            h = slice(64 * q, 64 * q + 64)
                            last = dve.tensor_scalar(qdiag[s][h, c, :, q, :], seqs(banks[s][c][h, :]),
                                                     Col("abq", 4 * r + c)[h, :], None, ALU.add)
                        last.then_inc(b_aq_v.sem, 1)
                    for t in range(T):
                        yield part_of(f"av{r}", t)
                        dve.wait_ge(b_proj_ps.sem, b_proj_ps.at(n, s, t + 1, use=3 * r + 2))
                        dve.tensor_tensor(va[s][:, t, :], banks[s][t][:, :],
                                          Row("abv")[:, 512 * r:512 * r + 512], ALU.add).then_inc(b_av.sem, 1)
                    yield from subtract_max(n, s, f"as{r}", b_s_ps, b_s_sub, r, SEQ)
                    for c in range(4):
                        yield part_of(f"am{r}", c)
                        dve.wait_ge(b_p.sem, b_p.at(n, s, c + 1, use=r))
                        sm = gs[s][:, 1, 8 * c:8 * c + 8]
                        st2(dve.tensor_reduce(sm, seqs(P[s][:, c, :]), AX.X, ALU.add))
                        dve.reciprocal(gs[s][:, 2, 8 * c:8 * c + 8], sm).then_inc(b_arc.sem, 1)
                    yield f"out{r}"
                    dve.wait_ge(b_out_ps.sem, b_out_ps.at(n, s, use=r))
                    if r == 0:
                        st2(dve.tensor_tensor(R[s][:, :, :], tok(banks[s][0][:, :]), X[s][:, :, :], ALU.add))
                        dve.tensor_tensor(R[s][:, :, :], R[s][:, :, :], over(Row("abo"), T), ALU.add).then_inc(b_out.sem, 1)
                    else:
                        dve.wait_ge(b_out.sem, b_out.at(n, s, use=0))
                        dve.tensor_tensor(R[s][:, :, :], tok(banks[s][0][:, :]), R[s][:, :, :], ALU.add).then_inc(b_out.sem, 1)
                        dve.wait_ge(b_out.sem, b_out.at(n, s, use=1))
                        norm_stats(s, st2, b_ln_mv)
                yield "n1"
                norm_apply(n, s, b_ln_rstd, b_x, 1)
                yield "cq"
                dve.wait_ge(b_cqk_ps.sem, b_cqk_ps.at(n, s, 2))
                dve.tensor_copy(kcat[s][:, :, SEQ:128], seqs(banks[s][1][:, :])).then_inc(b_ck.sem, 1)
                for k in range(2):
                    dve.wait_ge(b_cv_ps.sem, b_cv_ps.at(n, s, k + 1))
                    last = dve.tensor_copy(vcat[s][64:128, 4 * k:4 * k + 4, :, 0:16],
                                           banks[s][2 + k][64:128, :].rearrange("p (b g v) -> p b g v", b=4, v=16))
                last.then_inc(b_cv.sem, 1)
                for t in range(T):
                    yield from subtract_max(n, s, f"cs{t}", b_s_ps, b_s_sub, 2 + t, 128)
                    yield f"cr{t}"
                    dve.wait_ge(b_r_ps.sem, b_r_ps.at(n, s, use=t))
                    rv = banks[s][0][:, 0:272].rearrange("p (g c) -> p g c", c=17)
                    rc = gs[s][:, 1, 0:16]
                    st2(dve.reciprocal(rc, rv[:, :, 16]))
                    for r in range(2):
                        h = slice(64 * r, 64 * r + 64)
                        last = dve.tensor_tensor(
                            O[s][h, 2 * t:2 * t + 2, :].rearrange("p b (g v) -> p (b g) v", v=8),
                            rv[h, :, 8 * r:8 * r + 8], each(rc[h, :], 8), ALU.mult)
                    last.then_inc(b_r.sem, 1)
                yield "co"
                dve.wait_ge(b_o_ps.sem, b_o_ps.at(n, s))
                add_projection(s, banks[s][3], "pb")
                norm_stats(s, st2, b_ln_mv)
                yield "n2"
                norm_apply(n, s, b_ln_rstd, b_x, 2)

            def second2(n, s, last):
                for k, (bias, table) in enumerate((("fbq", "cos"), ("fbqs", "sin"), ("fbk", "cos"), ("fbks", "sin"))):
                    yield part_of("fq", k)
                    dve.wait_ge(b_fqk_ps.sem, b_fqk_ps.at(n, s, k + 1))
                    dve.scalar_tensor_tensor(seqs(P[s][:, k, :]), seqs(banks[s][k][:, :]), Col(bias),
                                             over(C(table), TB), ALU.add, ALU.mult).then_inc(b_frot.sem, 1)
                yield "fv"
                dve.wait_ge(b_fzero.sem, b_fzero.at(n, s))
                dve.wait_ge(b_fv_ps.sem, b_fv_ps.at(n, s))
                for b in range(2):
                    h = slice(64 * b, 64 * b + 64)
                    ins = dve.tensor_tensor(
                        vf[s][h, :, :, b, 0:16], banks[s][0][h, :].rearrange("p (t g v) -> p t g v", t=T, v=16),
                        over(Row("fbv")[h, :], T).rearrange("p t (g v) -> p t g v", v=16), ALU.add)
                ins.then_inc(b_fv.sem, 1)
                for jh in range(2):
                    yield from subtract_max(n, s, f"fs{jh}", b2_s_ps, b2_s_sub, jh, SEQ)
                    yield f"fr{jh}"
                    dve.wait_ge(b2_r_ps.sem, b2_r_ps.at(n, s, use=jh))
                    for k in range(2):
                        rv = banks[s][k][:, 0:272].rearrange("p (g c) -> p g c", c=17)
                        rc = gs[s][:, 1, 16 * k:16 * k + 16]
                        st2(dve.reciprocal(rc, rv[:, :, 16]))
                        for r in range(2):
                            h = slice(64 * r, 64 * r + 64)
                            ins = dve.tensor_tensor(
                                O[s][h, 4 * k:4 * k + 4, :].rearrange("p b (i c) -> p (b i) c", i=4)[:, :, 8 * jh:8 * jh + 8],
                                rv[h, :, 8 * r:8 * r + 8], each(rc[h, :], 8), ALU.mult)
                    ins.then_inc(b2_r.sem, 1)
                yield "fo"
                dve.wait_ge(b2_o_ps.sem, b2_o_ps.at(n, s))
                add_projection(s, banks[s][1], "fbo")
                norm_stats(s, st2, b2_ln_mv)
                yield "n3"
                norm_apply(n, s, b2_ln_rstd, b_ln_x1, 0, X1[s])
                yield "g"
                dve.wait_ge(b_g_ps.sem, b_g_ps.at(n, s))
                lg = small[s][:, 3, :].rearrange("p (t e) -> p t e", t=T)
                st2(dve.tensor_tensor(lg, banks[s][0][:, 0:T * NE].rearrange("p (t e) -> p t e", t=T),
                                      over(Row("bg"), T), ALU.add))
                choose(s, b_g_diff, st2, lg)
                yield "gb"
                weigh(n, s, b_g_exp, b_g_done, st2, share[s], False)
                yield "b2"
                dve.wait_ge(b_b2_ps.sem, b_b2_ps.at(n, s))
                dve.tensor_tensor(R[s][:, :, :], tok(banks[s][2][:, :]), X1[s][:, :, :], ALU.add).then_inc(b_b2.sem, 1)
                for e in range(NE):
                    yield f"md{e}"
                    dve.wait_ge(b_mdown_ps.sem, b_mdown_ps.at(n, s, use=e))
                    if e:
                        dve.wait_ge(b_mcomb.sem, b_mcomb.at(n, s, use=e - 1))
                    else:
                        dve.wait_ge(b_b2.sem, b_b2.at(n, s))
                    combine(s, e, banks[s][3], b_mcomb, R[s])
                dve.wait_ge(b_mcomb.sem, b_mcomb.at(n, s, use=NE - 1))
                norm_stats(s, st2, b2_ln_mv)
                yield "n4"
                norm_apply(n, s, b2_ln_rstd, b_ln_x1, 1, X1[s])
                yield "n5s"
                dve.wait_ge(b_r2.sem, b_r2.at(n, s))
                norm_stats(s, st2, b2_ln_mv)
                yield "n5"
                norm_apply(n, s, b2_ln_rstd, b2_x, 2)

            passes_of(dve, passes, B_FIRST, B_SECOND, B_TURNS, first2, second2, dve2, STEPS["dve2"])

        @block.tensor
        def _(pe):
            pe.wait_ge(s_init, 2)
            pe.wait_ge(s_const, 16 * 3)
            mm = pe.matmul

            def tile(ap, t):
                return ap[:, 128 * t:128 * t + 128]

            def turn_state(s, bank, src, x_ps):
                for t in range(T):
                    last = pe.transpose(tile(banks[s][bank], t), src[s][:, t, :], ident)
                last.then_inc(x_ps.sem, 1)

            def turn_probs(n, s, stage, p, p_ps, use=0):
                for i in range(4):
                    yield part_of(stage, i)
                    pe.wait_ge(p.sem, p.at(n, s, i + 1, use=use))
                    for t in range(T):
                        last = pe.transpose(tile(banks[s][i], t), tile(P[s][:, i, :], t), ident)
                    last.then_inc(p_ps.sem, 1)

            def turn_results(s, base, rt_ps):
                for k in range(2):
                    for b in range(4):
                        last = pe.transpose(banks[s][base + k][0:64, 128 * b:128 * b + 128], O[s][:, 4 * k + b, :], ident)
                    last.then_inc(rt_ps.sem, 1)

            def first(n, s):
                yield "qk"
                pe.wait_ge(loaded[s], 16 * 6 * (n + 1))
                for k, w in enumerate(("wk", "wks", "wq", "wqs")):
                    if k:
                        yield part_of("qk", k)
                    mm(banks[s][k][:, :], A(w), XT[s][:, :], start=True, stop=True).then_inc(a_qk_ps.sem, 1)
                yield "vg"
                pe.wait_ge(a_qk_mul.sem, a_qk_mul.at(n, s))
                for b in range(TB):
                    for r in range(2):
                        last = mm(banks[s][0][64 * r:64 * r + 64, 64 * b:64 * b + 64], XT[s][:, 64 * b:64 * b + 64],
                                  A("wv")[:, 64 * r:64 * r + 64], start=True, stop=True)
                last.then_inc(a_vg_ps.sem, 1)
                for t in range(T):
                    last = mm(tile(banks[s][1], t), tile(XT[s], t), A("wg"), start=True, stop=True)
                last.then_inc(a_vg_ps.sem, 1)
                yield "st"
                pe.wait_ge(a_k_pair.sem, a_k_pair.at(n, s))
                pe.wait_ge(a_k_sum.sem, a_k_sum.at(n, s))
                pe.wait_ge(a_v_diag.sem, a_v_diag.at(n, s))
                pe.wait_ge(a_gated.sem, a_gated.at(n, s))
                for i in range(4):
                    if i:
                        yield part_of("st", i)
                    h = slice(32 * i, 32 * i + 32)
                    for b in range(TB):
                        last = mm(banks[s][i][:, 64 * b:64 * b + 64], pair[s][h, b, :, :],
                                  QT[s][h, 64 * b:64 * b + 64], start=True, stop=True)
                    last.then_inc(a_st_ps.sem, 1)
                yield "y"
                pe.wait_ge(a_st.sem, a_st.at(n, s))
                for i in range(4):
                    for b in range(TB):
                        o = (b // 2) * 128 + 32 * i
                        last = mm(banks[s][0][64 * (b % 2):64 * (b % 2) + 64, o:o + 32],
                                  P[s][:, i, 64 * b:64 * b + 64], vdiag[s][:, b, i, :], start=True, stop=True)
                last.then_inc(a_y_ps.sem, 1)
                yield "h"
                pe.wait_ge(a_h.sem, a_h.at(n, s))
                for t in range(T):
                    last = pe.transpose(tile(banks[s][1], t), tile(yc[s], t), ident)
                last.then_inc(a_h_ps.sem, 1)
                yield "o"
                pe.wait_ge(a_hT.sem, a_hT.at(n, s))
                for t in range(T):
                    last = mm(tile(banks[s][2], t), tile(hT[s], t), A("wo"), start=True, stop=True)
                last.then_inc(a_o_ps.sem, 1)

            def second(n, s, last):
                yield "kv"
                pe.wait_ge(a_x.sem, a_x.at(n, s))
                for c in range(2):
                    ins = mm(banks[s][2][:, :], tile(A("xk"), c), ctxT[s][:, c, :], start=c == 0, stop=c == 1)
                ins.then_inc(a_kv_ps.sem, 1)
                for t in range(T):
                    for c in range(2):
                        ins = mm(tile(banks[s][3], t), tile(ctxT[s][:, c, :], t), tile(A("xv"), c),
                                 start=c == 0, stop=c == 1)
                ins.then_inc(a_kv_ps.sem, 1)
                turn_state(s, 0, X, a_x_ps)
                yield "q"
                pe.wait_ge(a_xT.sem, a_xT.at(n, s, use=0))
                mm(banks[s][1][:, :], A("xq"), XT[s][:, :], start=True, stop=True).then_inc(a_kv_ps.sem, 1)
                yield "s"
                pe.wait_ge(a_kT.sem, a_kT.at(n, s))
                pe.wait_ge(a_v.sem, a_v.at(n, s))
                pe.wait_ge(a_q_pair.sem, a_q_pair.at(n, s))
                for i in range(4):
                    if i:
                        yield part_of("s", i)
                    h = slice(32 * i, 32 * i + 32)
                    for b in range(TB):
                        ins = mm(banks[s][i][:, 64 * b:64 * b + 64], pair[s][h, b, :, :],
                                 KT[s][h, 64 * b:64 * b + 64], start=True, stop=True)
                    ins.then_inc(a_s_ps.sem, 1)
                yield from turn_probs(n, s, "p", a_p, a_p_ps)
                yield "r"
                pe.wait_ge(a_pT.sem, a_pT.at(n, s))
                for t in range(T):
                    if t:
                        yield part_of("r", t)
                    rv = banks[s][t][:, 0:264].rearrange("p (b i c) -> p b i c", b=2, i=4)
                    for i in range(4):
                        ins = mm(rv[:, :, i, :], tile(PT[s][:, i, :], t), xv[s][:, t, i, :, :], start=True, stop=True)
                    ins.then_inc(a_r_ps.sem, 1)
                yield "rt"
                pe.wait_ge(a_r.sem, a_r.at(n, s))
                apart(pe)
                turn_results(s, 0, a_rt_ps)
                yield "o2"
                pe.wait_ge(a_rT.sem, a_rT.at(n, s))
                for t in range(T):
                    o = tile(banks[s][2], t)
                    mm(o, tile(XT[s], t), A("xo"), start=True, stop=False)
                    for r in range(2):
                        ins = mm(o, tile(OT2[s][:, r, :], t), Wp("xo", r), start=False, stop=r == 1)
                ins.then_inc(a_o2_ps.sem, 1)
                yield "x"
                pe.wait_ge(a2_x.sem, a2_x.at(n, s))
                turn_state(s, 3, X, a_x_ps)
                yield "g"
                pe.wait_ge(a_xT.sem, a_xT.at(n, s, use=1))
                for t in range(T):
                    ins = mm(banks[s][0][:, NE * t:NE * t + NE], tile(XT[s], t), A("gate"), start=True, stop=True)
                ins.then_inc(a_g_ps.sem, 1)

            pe.wait_ge(s_const2, 16 * 4)
            passes_of(pe, passes, A_FIRST, A_SECOND, A_TURNS, first, second, None, 0)

            pe.wait_ge(s_prim, 1)
            mm(banks[0][0][0:8, 0:8], C("ones"), prim[:, :], start=True, stop=True)
            mm(banks[0][0][0:8, 8:16], prim[:, :], C("ones"), start=True, stop=True).then_inc(s_cnt, 1)
            pe.wait_ge(s_map, 1)

            def turn_weights(s, src, wt_ps):
                for t in range(T):
                    last = pe.transpose(banks[s][1][0:8, 128 * t:128 * t + 128], src[:, t, :], ident)
                last.then_inc(wt_ps.sem, 1)

            def out_project(s, w, bank, o_ps):
                for t in range(T):
                    for r in range(2):
                        last = mm(tile(bank, t), tile(OT2[s][:, r, :], t), Wp(w, r), start=r == 0, stop=r == 1)
                last.then_inc(o_ps.sem, 1)

            def first2(n, s):
                yield "in"
                pe.wait_ge(reloaded[s], 16 * n + 16)
                turn_state(s, 0, X, b_x_ps)
                pe.wait_ge(b_wts.sem, b_wts.at(n, s))
                apart(pe)
                turn_weights(s, wts[s], b_wt_ps)
                yield "sh"
                pe.wait_ge(b_wtT.sem, b_wtT.at(n, s))
                for t in range(T):
                    last = mm(banks[s][2][:, NE * t:NE * t + NE], tile(wtT[s], t), emap[:, 11, :], start=True, stop=True)
                last.then_inc(b_share_ps.sem, 1)
                for e in range(NE):
                    yield f"up{e}"
                    if e:
                        pe.wait_ge(b_fh.sem, b_fh.at(n, s, use=e - 1))
                    else:
                        pe.wait_ge(b_xT.sem, b_xT.at(n, s, use=0))
                    for k in range(2):
                        mm(banks[s][k][:, :], tile(B("gu"), 2 * e + k), XT[s][:, :], start=True, stop=True).then_inc(b_up_ps.sem, 1)
                    yield f"down{e}"
                    pe.wait_ge(b_fh.sem, b_fh.at(n, s, use=e))
                    if e >= 2:
                        pe.wait_ge(b_comb.sem, b_comb.at(n, s, use=e - 2))
                    else:
                        pe.wait_ge(b_share.sem, b_share.at(n, s))
                    for t in range(T):
                        last = mm(tile(banks[s][2 + e % 2], t), tile(P[s][:, 1, :], t), tile(B("down"), e),
                                  start=True, stop=True)
                    last.then_inc(b_down_ps.sem, 1)

                yield "t1"
                pe.wait_ge(b_x.sem, b_x.at(n, s, use=0))
                turn_state(s, 0, X, b_x_ps)
                for r in range(2):
                    yield f"aq{r}"
                    if r == 0:
                        pe.wait_ge(b_xT.sem, b_xT.at(n, s, use=1))
                    else:
                        pe.wait_ge(b_out.sem, b_out.at(n, s, use=0))
                    for c in range(4):
                        if c:
                            yield part_of(f"aq{r}", c)
                        mm(banks[s][c][:, :], tile(B("aq"), 4 * r + c), XT[s][:, :], start=True, stop=True).then_inc(b_proj_ps.sem, 1)
                    for c in range(4):
                        yield part_of(f"ak{r}", c)
                        if c % 2:
                            pe.wait_ge(b_aq_v.sem, b_aq_v.at(n, s, c // 2 + 1, use=r))
                        else:
                            pe.wait_ge(b_aq_a.sem, b_aq_a.at(n, s, c // 2 + 1, use=r))
                        mm(banks[s][c][:, :], tile(B("ak"), 4 * r + c), XT[s][:, :], start=True, stop=True).then_inc(b_proj_ps.sem, 1)
                    for t in range(T):
                        yield part_of(f"av{r}", t)
                        pe.wait_ge(b_ak.sem, b_ak.at(n, s, t + 1, use=r))
                        mm(banks[s][t][:, :], tile(XT[s], t), B("av")[:, 512 * r:512 * r + 512],
                           start=True, stop=True).then_inc(b_proj_ps.sem, 1)
                    for c in range(4):
                        yield part_of(f"as{r}", c)
                        pe.wait_ge(b_av.sem, b_av.at(n, s, c + 1, use=r))
                        for b in range(TB):
                            last = mm(banks[s][c][:, 64 * b:64 * b + 64], qdiag[s][:, c, b, :, :],
                                      kc[s][:, c, 64 * b:64 * b + 64], start=True, stop=True)
                        last.then_inc(b_s_ps.sem, 1)
                    yield from turn_probs(n, s, f"ap{r}", b_an, b_p_ps, r)
                    yield f"ao{r}"
                    pe.wait_ge(b_pT.sem, b_pT.at(n, s, use=r))
                    apart(pe)
                    for b in range(2):
                        h = slice(64 * b, 64 * b + 64)
                        for half in range(2):
                            if b or half:
                                yield part_of(f"ao{r}", 2 * b + half)
                            for c in range(2):
                                for t in range(T):
                                    for q in range(2):
                                        o = 64 * (2 * (2 * half + c) + q)
                                        last = mm(banks[s][2 * b + half][64 * q:64 * q + 64,
                                                                         256 * c + 64 * t:256 * c + 64 * t + 64],
                                                  va[s][h, t, o:o + 64],
                                                  PT[s][h, 2 * half + c, 128 * t + 64 * q:128 * t + 64 * q + 64],
                                                  start=True, stop=True)
                            last.then_inc(b_ao_ps.sem, 1)
                    yield f"out{r}"
                    pe.wait_ge(b_aoT.sem, b_aoT.at(n, s, use=r))
                    for t in range(T):
                        if t:
                            yield part_of(f"out{r}", t)
                        for c in range(4):
                            last = mm(tile(banks[s][0], t), tile(P[s][:, c, :], t), tile(B("ao"), 4 * r + c),
                                      start=c == 0, stop=c == 3)
                    last.then_inc(b_out_ps.sem, 1)

                yield "t2"
                pe.wait_ge(b_x.sem, b_x.at(n, s, use=1))
                turn_state(s, 0, X, b_x_ps)
                yield "cq"
                pe.wait_ge(b_xT.sem, b_xT.at(n, s, use=2))
                for k, w in enumerate(("cq", "ck")):
                    mm(banks[s][k][:, :], B(w), XT[s][:, :], start=True, stop=True).then_inc(b_cqk_ps.sem, 1)
                for k in range(2):
                    for b in range(4):
                        last = mm(banks[s][2 + k][64:128, 128 * b:128 * b + 128],
                                  XT[s][:, 64 * (4 * k + b):64 * (4 * k + b) + 64], B("cv"), start=True, stop=True)
                    last.then_inc(b_cv_ps.sem, 1)
                for t in range(T):
                    yield f"cs{t}"
                    if t == 0:
                        pe.wait_ge(b_cq.sem, b_cq.at(n, s))
                        pe.wait_ge(b_ck.sem, b_ck.at(n, s))
                        pe.wait_ge(b_cv.sem, b_cv.at(n, s))
                        pe.wait_ge(b_cones.sem, b_cones.at(n, s))
                        pe.wait_ge(context[s], 16 * 9 * (n + 1))
                    else:
                        pe.wait_ge(b_r.sem, b_r.at(n, s, use=t - 1))
                    for i in range(4):
                        if i:
                            yield part_of(f"cs{t}", i)
                        h = slice(32 * i, 32 * i + 32)
                        for b in range(2):
                            for j in range(2):
                                last = mm(tile(banks[s][i], 2 * b + j), q4[0][s][h, 2 * t + b, 2 * j:2 * j + 2, :],
                                          kcat[s][h, 2 * t + b, :], start=True, stop=True)
                        last.then_inc(b_s_ps.sem, 1)
                    yield from turn_probs(n, s, f"cp{t}", b_p, b_p_ps, 2 + t)
                    yield f"cr{t}"
                    pe.wait_ge(b_pT.sem, b_pT.at(n, s, use=2 + t))
                    for i in range(4):
                        for b in range(2):
                            for j in range(2):
                                o = 17 * (8 * b + 2 * i + j)
                                last = mm(banks[s][0][:, o:o + 17], tile(PT[s][:, i, :], 2 * b + j),
                                          vcat[s][:, 2 * t + b, 2 * i + j, :], start=True, stop=True)
                    last.then_inc(b_r_ps.sem, 1)
                yield "crt"
                pe.wait_ge(b_r.sem, b_r.at(n, s, use=3))
                apart(pe)
                turn_results(s, 1, b_rt_ps)
                yield "co"
                pe.wait_ge(b_rT.sem, b_rT.at(n, s))
                out_project(s, "x1", banks[s][3], b_o_ps)

            def second2(n, s, last):
                yield "t3"
                pe.wait_ge(b_x.sem, b_x.at(n, s, use=2))
                turn_state(s, 0, X, b2_x_ps)
                yield "fq"
                pe.wait_ge(b2_xT.sem, b2_xT.at(n, s, use=0))
                for k, w in enumerate(("fq", "fqs", "fk", "fks")):
                    if k:
                        yield part_of("fq", k)
                    mm(banks[s][k][:, :], B(w), XT[s][:, :], start=True, stop=True).then_inc(b_fqk_ps.sem, 1)
                yield "fv"
                pe.wait_ge(b_frot.sem, b_frot.at(n, s, 1))
                for t in range(T):
                    ins = mm(tile(banks[s][0], t), tile(XT[s], t), B("fv"), start=True, stop=True)
                ins.then_inc(b_fv_ps.sem, 1)
                for jh in range(2):
                    yield f"fs{jh}"
                    if jh == 0:
                        pe.wait_ge(b_fsum.sem, b_fsum.at(n, s))
                        pe.wait_ge(b_fq.sem, b_fq.at(n, s))
                        pe.wait_ge(b_fv.sem, b_fv.at(n, s))
                    else:
                        pe.wait_ge(b2_r.sem, b2_r.at(n, s, use=0))
                    for i in range(4):
                        if i:
                            yield part_of(f"fs{jh}", i)
                        h = slice(32 * i, 32 * i + 32)
                        for b in range(TB):
                            ins = mm(banks[s][i][:, 64 * b:64 * b + 64], q4[1][s][h, b, 2 * jh:2 * jh + 2, :],
                                     kf[s][h, 64 * b:64 * b + 64], start=True, stop=True)
                        ins.then_inc(b2_s_ps.sem, 1)
                    yield from turn_probs(n, s, f"fp{jh}", b2_p, b2_p_ps, jh)
                    yield f"fr{jh}"
                    pe.wait_ge(b2_pT.sem, b2_pT.at(n, s, use=jh))
                    for t in range(T):
                        rv = banks[s][t // 2][:, 0:272].rearrange("p (t b i c) -> p t b i c", t=2, b=2, i=4)
                        for i in range(4):
                            ins = mm(rv[:, t % 2, :, i, :], tile(PT[s][:, i, :], t), vf[s][:, t, 2 * i + jh, :, :],
                                     start=True, stop=True)
                    ins.then_inc(b2_r_ps.sem, 1)
                yield "frt"
                pe.wait_ge(b2_r.sem, b2_r.at(n, s, use=1))
                apart(pe)
                turn_results(s, 2, b2_rt_ps)
                yield "fo"
                pe.wait_ge(b2_rT.sem, b2_rT.at(n, s))
                out_project(s, "fo", banks[s][1], b2_o_ps)

                yield "t4"
                pe.wait_ge(b_x1.sem, b_x1.at(n, s))
                turn_state(s, 3, X1, b2_x_ps)
                yield "g"
                pe.wait_ge(b2_xT.sem, b2_xT.at(n, s, use=1))
                for t in range(T):
                    ins = mm(banks[s][0][:, NE * t:NE * t + NE], tile(XT[s], t), B("fg"), start=True, stop=True)
                ins.then_inc(b_g_ps.sem, 1)
                yield "wt"
                pe.wait_ge(b_g_done.sem, b_g_done.at(n, s))
                apart(pe)
                turn_weights(s, share[s], b2_wt_ps)
                yield "b2"
                pe.wait_ge(b2_wtT.sem, b2_wtT.at(n, s))
                for t in range(T):
                    ins = mm(tile(banks[s][2], t), tile(wtT[s], t), W8p("b2"), start=True, stop=True)
                ins.then_inc(b_b2_ps.sem, 1)
                for e in range(NE):
                    yield f"mup{e}"
                    if e == 0:
                        pe.wait_ge(b_b2.sem, b_b2.at(n, s))
                    pe.wait_ge(w_loaded[e % 2], 32 * ((n * SLOTS + s) * (NE // 2) + e // 2 + 1))
                    for c in range(NC):
                        if c:
                            yield part_of(f"mup{e}", c)
                        if c == 3:
                            pe.wait_ge(b_gelu.sem, b_gelu.at(n, s, 1, use=e))
                        mm(banks[s][c % 3][:, :], tile(w1r[e % 2], c), XT[s][:, :], start=True, stop=True).then_inc(b_mup_ps.sem, 1)
                    yield f"md{e}"
                    pe.wait_ge(b_gelu.sem, b_gelu.at(n, s, use=e))
                    if e:
                        pe.wait_ge(b_mcomb.sem, b_mcomb.at(n, s, use=e - 1))
                    for t in range(T):
                        if t:
                            yield part_of(f"md{e}", t)
                        for c in range(NC):
                            ins = mm(tile(banks[s][3], t), tile(PT[s][:, c, :], t), w2r[e % 2][:, c, :],
                                     start=c == 0, stop=c == NC - 1)
                    ins.then_inc(b_mdown_ps.sem, 1)

            passes_of(pe, passes, B_FIRST, B_SECOND, B_TURNS, first2, second2, None, 0)


STEPS = dict(dve1=56, pool1=8, dve2=148, pool2=20)



def tables():
    f = np.float32
    p = np.arange(128)
    pos = np.arange(SEQ, dtype=f)
    e = p % 16
    base = ((e // 2 * 2).astype(f) + f(0.4 * 16)) / f(1.4 * 16)
    scale = base[:, None] ** (pos[None, :] / f(512.0))
    ang = pos[None, :] * (f(1.0) / f(10000.0) ** ((e // 2).astype(f) / f(8)))[:, None]
    sign = np.where(e % 2 == 0, -1, 1).astype(f)[:, None]
    lo, hi = np.log(1.0 / 32.0), np.log(1.0 / 512.0)
    gam = f(1.0) - np.exp(np.linspace(lo, hi, 8)).astype(f)
    m, l = p % 64, np.arange(64)
    dec = np.zeros((128, 4, 64), f)
    for i in range(4):
        g = gam[2 * i + p // 64]
        expo = (l[None, :] - m[:, None]).astype(f)
        dec[:, i, :] = np.where(expo >= 0, np.exp(expo * np.log(g)[:, None]), 0)
    ang8 = pos[None, :] * (f(1.0) / f(10000.0) ** ((2 * (p % 4)).astype(f) / f(8)))[:, None]
    sign8 = np.where(p % 8 < 4, -1, 1).astype(f)[:, None]
    cols = [np.eye(128), np.cos(ang) * scale, sign * np.sin(ang) * scale, np.cos(ang) / scale,
            sign * np.sin(ang) / scale, dec.reshape(128, 256), np.cos(ang8), sign8 * np.sin(ang8),
            (p[:, None] // 16) % 2 == np.arange(2), (p[:, None] // 8) % 4 == np.arange(4),
            np.broadcast_to(np.arange(8), (128, 8)), np.ones((128, 8))]
    return np.concatenate([np.asarray(c, f) for c in cols], axis=1)


def lay_out(a):
    batch, seq, dim = a["x"].shape
    wide = lambda *parts: np.ascontiguousarray(np.concatenate([np.asarray(q).reshape(q.shape[0], -1) for q in parts], axis=1))
    swap16 = np.arange(128) ^ 1
    swap8 = np.arange(128) // 8 * 8 + (np.arange(128) + 4) % 8
    heads = lambda w: np.transpose(w, (1, 0, 2)).reshape(dim, dim)
    by_par = lambda w, v: w.reshape(128, -1, 2, v).transpose(0, 2, 1, 3)
    rows_par = lambda w, v: w.reshape(-1, 2, v, 128).transpose(0, 2, 1, 3)
    split_rows = lambda w, v: np.ascontiguousarray(rows_par(w, v)).reshape(64, 256)
    wq, wk, wv = heads(a["L0_attn_W_Q"]), heads(a["L0_attn_W_K"]), heads(a["L0_attn_W_V"])
    ws = a["L0_xattn_W_src"].T
    chunks = lambda w: w.reshape(-1, 128, w.shape[1]).transpose(1, 0, 2)
    wo = a["L0_xattn_W_out"].T
    qkv = a["L1_xattn_w_qkv"].T
    wa = wide(wq, wq[:, swap16], wk, wk[:, swap16], by_par(wv, 16), a["L0_attn_W_G"], a["L0_attn_W_O"],
              chunks(ws[:, :128]), chunks(ws[:, 128:]), a["L0_xattn_W_tgt"].T, wo[:128], a["L0_ffn_gate_weight"].T)
    w64 = wide(split_rows(wo[128:], 16), split_rows(a["L1_xattn_w_proj"].T, 8), split_rows(a["L1_ffn_Wo"], 8))
    rows = np.concatenate([a["L0_attn_gn_weight"], a["L0_attn_gn_bias"], a["L0_xattn_b_src"][128:], a["L0_xattn_b_out"],
                           a["L1_attn_bo"], a["L1_xattn_b_proj"], a["L1_ffn_bv"], a["L1_ffn_bo"], a["L1_ffn_g1"],
                           a["L1_ffn_be1"], a["L1_ffn_g2"], a["L1_ffn_be2"], a["L1_ffn_bg"], a["L1_attn_bv"]])
    col = lambda v: v.reshape(-1, 128).T
    cols = wide(col(a["L0_xattn_b_tgt"]), col(a["L0_xattn_b_src"][:128]), col(a["L1_attn_bq"]), col(a["L1_attn_bk"]),
                col(a["L1_ffn_bq"]), col(a["L1_ffn_bq"][swap8]), col(a["L1_ffn_bk"]), col(a["L1_ffn_bk"][swap8]),
                col(a["L1_ffn_b1"].reshape(-1)))
    fq, fk = a["L1_ffn_Wq"], a["L1_ffn_Wk"]
    wb = wide(a["L0_ffn_gate_up_proj"].transpose(2, 0, 1), a["L0_ffn_down_proj"].transpose(2, 0, 1),
              a["L1_attn_Wq"], a["L1_attn_Wk"], a["L1_attn_Wv"], chunks(a["L1_attn_Wo"]),
              qkv, fq, fq[:, swap8], fk, fk[:, swap8], a["L1_ffn_Wv"], a["L1_ffn_Wg"])
    w8 = wide(a["L0_ffn_similarity_matrix"], np.eye(8, dtype=np.float32), a["L1_ffn_b2"])
    x = a["x"].reshape(batch * seq, dim)
    c = a["ctx_2048"].reshape(batch * seq, CTX)
    return dict(x=x, xT=np.ascontiguousarray(x.T), ctx=c, ctxT=np.ascontiguousarray(c.T),
                mask=a["mask_BxS2_fk1"].reshape(-1), const=tables(), wa=wa, w64=w64, rows=rows, cols=cols, wb=wb,
                w8=w8, w1=a["L1_ffn_W1"], w2=a["L1_ffn_W2"])


def kernel(**inputs):
    import numpy as _np
    import concourse.bacc as _bacc
    from concourse.bass_utils import run_bass_kernel_spmd as _run

    a = {name: _np.asarray(v) for name, v in inputs.items()}
    shape = a["x"].shape
    arrays = {f"in_{k}": _np.ascontiguousarray(v) for k, v in lay_out(a).items()}
    nc = _bacc.Bacc("TRN2", target_bir_lowering=False, num_devices=1)
    d = {k[3:]: nc.dram_tensor(k, v.shape, F32, kind="ExternalInput").ap() for k, v in arrays.items()}
    n = shape[0] * shape[1]
    out = nc.dram_tensor("out", (n, shape[2]), F32, kind="ExternalOutput").ap()
    d["x_mid"] = nc.dram_tensor("x_mid", (n, shape[2]), F32, kind="Internal").ap()
    build(nc, d, out, n // NT)
    r = _run(nc, [arrays], core_ids=[0])
    return r.results[0]["out"].reshape(shape)
```
